# Optimizing a Trainium2 kernel written in Bass

```python
import numpy as np
import jax
import jax.numpy as jnp

def _softmax(x, axis=-1):
    return jax.nn.softmax(x, axis=axis)

def _gelu(x):
    return jax.nn.gelu(x, approximate=True)

def _silu(x):
    return jax.nn.silu(x)

def _sigmoid(x):
    return jax.nn.sigmoid(x)

def _layernorm(x, axis=-1, eps=1e-05):
    m = jnp.mean(x, axis=axis, keepdims=True)
    v = jnp.var(x, axis=axis, keepdims=True)
    return (x - m) / jnp.sqrt(v + eps)

def _scatter_add(tgt, idx, src, axis=0):
    return tgt.at[idx].add(src)

def _segment_sum(src, seg, n):
    return jax.ops.segment_sum(src, seg, n)
kernel_name = 'mk_seq_postln_d2_jaxref_r8_0aea3e'

def setup_inputs(seed: int=0):
    np.random.seed(seed)
    _w = jnp.asarray

    def _L0_attn_setup():
        import jax, jax.numpy as jnp
        import numpy as np
        N_HEADS = 16
        SCALE = 8.0
        key = jax.random.key(seed)
        k1, k2, k3, k4 = jax.random.split(key, 4)
        b, n, d_model, inner = (8, 256, 128, 128)
        x = jax.random.normal(k1, (b, n, d_model), dtype=jnp.float32)
        Wqkv = jax.random.normal(k2, (3 * inner, d_model), dtype=jnp.float32) * (1.0 / np.sqrt(d_model))
        Wproj = jax.random.normal(k3, (d_model, inner), dtype=jnp.float32) * (1.0 / np.sqrt(inner))
        bproj = jax.random.normal(k4, (d_model,), dtype=jnp.float32) * 0.01
        return {'x': x, 'Wqkv': Wqkv, 'Wproj': Wproj, 'bproj': bproj}
    _L0_attn_in = _L0_attn_setup()

    def _L0_ffn_setup():
        import jax, jax.numpy as jnp
        import numpy as np
        B, S, D, O, E, K = (4, 256, 128, 128, 8, 2)
        key = jax.random.key(seed)
        ks = jax.random.split(key, 5)
        scale_in = 1.0 / np.sqrt(D)
        x = jax.random.normal(ks[0], (B, S, D), dtype=jnp.float32)
        gate_w = jax.random.uniform(ks[1], (E, D), jnp.float32, -scale_in, scale_in)
        gate_b = jax.random.uniform(ks[2], (E,), jnp.float32, -scale_in, scale_in)
        expert_w = jax.random.uniform(ks[3], (E, D, O), jnp.float32, -scale_in, scale_in)
        expert_b = jax.random.uniform(ks[4], (E, O), jnp.float32, -scale_in, scale_in)
        return {'x': x, 'gate_w': gate_w, 'gate_b': gate_b, 'expert_w': expert_w, 'expert_b': expert_b}
    _L0_ffn_in = _L0_ffn_setup()

    def _L1_attn_setup():
        import jax, jax.numpy as jnp
        import numpy as np
        D = 128
        H = 16
        DH = D // H
        B, N = (4, 128)
        key = jax.random.key(seed)
        k0, k1, k2 = jax.random.split(key, 3)
        x = jax.random.normal(k0, (B, N, D), jnp.float32)
        Wkqv = jax.random.normal(k1, (H, D, 2 * D + DH), jnp.float32) * 0.02
        bkqv = jnp.zeros((H, 2 * D + DH), jnp.float32)
        Wp = jax.random.normal(k2, (D, D), jnp.float32) * 0.02
        bp = jnp.zeros((D,), jnp.float32)
        return {'x': x, 'Wkqv': Wkqv, 'bkqv': bkqv, 'Wp': Wp, 'bp': bp}
    _L1_attn_in = _L1_attn_setup()

    def _L1_ffn_setup():
        import jax, jax.numpy as jnp
        import numpy as np
        E = 8
        K = 2
        D = 128
        H = 342
        B, S = (2, 256)

        def _moe_forward(x, centroid, Wg, bg, W1, b1, W2, b2):
            T = x.shape[0] * x.shape[1]
            xs = x.reshape(T, D)
            d2 = jnp.sum(xs * xs, axis=-1, keepdims=True) + jnp.sum(centroid * centroid, axis=-1)[None, :] - 2.0 * (xs @ centroid.T)
            dist = jnp.sqrt(jnp.maximum(d2, 1e-12))
            w, sel = jax.lax.top_k(dist, K)
            w = jax.nn.softmax(w.astype(jnp.float32), axis=1).astype(x.dtype)
            we = jnp.zeros((T, E), dtype=x.dtype).at[jnp.arange(T)[:, None], sel].add(w)
            out = jnp.zeros_like(xs)
            for e in range(E):
                h = jax.nn.silu(xs @ Wg[e] + bg[e]) * (xs @ W1[e] + b1[e])
                out = out + we[:, e:e + 1] * (h @ W2[e] + b2[e])
            return out.reshape(x.shape)
        key = jax.random.key(seed)
        ks = jax.random.split(key, 9)
        scale = 0.02
        return {'x': jax.random.normal(ks[0], (B, S, D), dtype=jnp.float32), 'centroid': jax.random.normal(ks[1], (E, D), dtype=jnp.float32), 'Wg': jax.random.normal(ks[2], (E, D, H), dtype=jnp.float32) * scale, 'bg': jnp.zeros((E, H), dtype=jnp.float32), 'W1': jax.random.normal(ks[3], (E, D, H), dtype=jnp.float32) * scale, 'b1': jnp.zeros((E, H), dtype=jnp.float32), 'W2': jax.random.normal(ks[4], (E, H, D), dtype=jnp.float32) * scale, 'b2': jnp.zeros((E, D), dtype=jnp.float32)}
    _L1_ffn_in = _L1_ffn_setup()
    _d = {'L0_attn_x': _L0_attn_in['x'], 'L0_attn_Wqkv': _L0_attn_in['Wqkv'], 'L0_attn_Wproj': _L0_attn_in['Wproj'], 'L0_attn_bproj': _L0_attn_in['bproj'], 'L0_ffn_gate_w': _L0_ffn_in['gate_w'], 'L0_ffn_gate_b': _L0_ffn_in['gate_b'], 'L0_ffn_expert_w': _L0_ffn_in['expert_w'], 'L0_ffn_expert_b': _L0_ffn_in['expert_b'], 'L1_attn_Wkqv': _L1_attn_in['Wkqv'], 'L1_attn_bkqv': _L1_attn_in['bkqv'], 'L1_attn_Wp': _L1_attn_in['Wp'], 'L1_attn_bp': _L1_attn_in['bp'], 'L1_ffn_centroid': _L1_ffn_in['centroid'], 'L1_ffn_Wg': _L1_ffn_in['Wg'], 'L1_ffn_bg': _L1_ffn_in['bg'], 'L1_ffn_W1': _L1_ffn_in['W1'], 'L1_ffn_b1': _L1_ffn_in['b1'], 'L1_ffn_W2': _L1_ffn_in['W2'], 'L1_ffn_b2': _L1_ffn_in['b2']}
    _x0 = _d['L0_attn_x']
    _d['L0_attn_x'] = jax.random.normal(jax.random.fold_in(jax.random.key(seed), 1), (16, 512, 128), dtype=_x0.dtype)
    del _x0
    return _d

def reference(L0_attn_x, L0_attn_Wqkv, L0_attn_Wproj, L0_attn_bproj, L0_ffn_gate_w, L0_ffn_gate_b, L0_ffn_expert_w, L0_ffn_expert_b, L1_attn_Wkqv, L1_attn_bkqv, L1_attn_Wp, L1_attn_bp, L1_ffn_centroid, L1_ffn_Wg, L1_ffn_bg, L1_ffn_W1, L1_ffn_b1, L1_ffn_W2, L1_ffn_b2):

    def _L0_attn_ref(x, Wqkv, Wproj, bproj):
        import jax, jax.numpy as jnp
        import numpy as np
        N_HEADS = 16
        SCALE = 8.0
        b, n, _ = x.shape
        qkv = jnp.einsum('bnm,fm->bnf', x, Wqkv)
        qkv = qkv.reshape(b, n, N_HEADS, -1)
        dh = qkv.shape[3] // 3
        q, k, v = (qkv[..., :dh], qkv[..., dh:2 * dh], qkv[..., 2 * dh:])
        scores = jnp.einsum('bnhd,bngd->bnhg', q, k) / SCALE
        attn = jax.nn.softmax(scores, axis=-1)
        out = jnp.einsum('bnhg,bngd->bnhd', attn, v)
        out = out.reshape(b, n, -1)
        return jnp.einsum('bni,mi->bnm', out, Wproj) + bproj

    def _L0_ffn_ref(x, gate_w, gate_b, expert_w, expert_b):
        import jax, jax.numpy as jnp
        import numpy as np
        B, S, D, O, E, K = (4, 256, 128, 128, 8, 2)
        logits = jnp.einsum('bsd,ed->bse', x, gate_w) + gate_b
        if K < E:
            topv, topi = jax.lax.top_k(logits, K)
            keep = jax.nn.one_hot(topi, E, dtype=jnp.float32).sum(axis=-2)
            logits = jnp.where(keep > 0, logits, -jnp.inf)
        gate_score = jax.nn.softmax(logits, axis=-1)
        expert_out = jnp.einsum('bsd,edo->bseo', x, expert_w) + expert_b
        out = jnp.einsum('bseo,bse->bso', expert_out, gate_score)
        return out

    def _L1_attn_ref(x, Wkqv, bkqv, Wp, bp):
        import jax, jax.numpy as jnp
        import numpy as np
        D = 128
        H = 16
        DH = D // H
        B, N = (4, 128)
        Bm, Nm, Dm = x.shape
        y = jnp.einsum('bnd,hde->bhne', x, Wkqv) + bkqv[None, :, None, :]
        k = y[..., :Dm]
        q = y[..., Dm:2 * Dm]
        v = y[..., 2 * Dm:]
        A = jnp.einsum('bhnd,bhmd->bhnm', q, k) / jnp.sqrt(jnp.float32(Dm))
        mask = jnp.tril(jnp.ones((Nm, Nm), dtype=bool))
        A = jnp.where(mask[None, None], A, -jnp.inf)
        A = jax.nn.softmax(A, axis=-1)
        sa = jnp.einsum('bhnm,bhmd->bnhd', A, v).reshape(Bm, Nm, Dm)
        return sa @ Wp + bp

    def _L1_ffn_ref(x, centroid, Wg, bg, W1, b1, W2, b2):
        import jax, jax.numpy as jnp
        import numpy as np
        E = 8
        K = 2
        D = 128
        H = 342
        B, S = (2, 256)

        def _moe_forward(x, centroid, Wg, bg, W1, b1, W2, b2):
            T = x.shape[0] * x.shape[1]
            xs = x.reshape(T, D)
            d2 = jnp.sum(xs * xs, axis=-1, keepdims=True) + jnp.sum(centroid * centroid, axis=-1)[None, :] - 2.0 * (xs @ centroid.T)
            dist = jnp.sqrt(jnp.maximum(d2, 1e-12))
            w, sel = jax.lax.top_k(dist, K)
            w = jax.nn.softmax(w.astype(jnp.float32), axis=1).astype(x.dtype)
            we = jnp.zeros((T, E), dtype=x.dtype).at[jnp.arange(T)[:, None], sel].add(w)
            out = jnp.zeros_like(xs)
            for e in range(E):
                h = jax.nn.silu(xs @ Wg[e] + bg[e]) * (xs @ W1[e] + b1[e])
                out = out + we[:, e:e + 1] * (h @ W2[e] + b2[e])
            return out.reshape(x.shape)
        return _moe_forward(x, centroid, Wg, bg, W1, b1, W2, b2)
    x = L0_attn_x
    x = _layernorm(x + _L0_attn_ref(x, L0_attn_Wqkv, L0_attn_Wproj, L0_attn_bproj), axis=-1)
    x = _layernorm(x + _L0_ffn_ref(x, L0_ffn_gate_w, L0_ffn_gate_b, L0_ffn_expert_w, L0_ffn_expert_b), axis=-1)
    x = _layernorm(x + _L1_attn_ref(x, L1_attn_Wkqv, L1_attn_bkqv, L1_attn_Wp, L1_attn_bp), axis=-1)
    x = _layernorm(x + _L1_ffn_ref(x, L1_ffn_centroid, L1_ffn_Wg, L1_ffn_bg, L1_ffn_W1, L1_ffn_b1, L1_ffn_W2, L1_ffn_b2), axis=-1)
    return x

_drawn_inputs = setup_inputs


def setup_inputs(seed=0):
    import zlib

    import numpy as np

    out = dict(_drawn_inputs(seed))
    spreads = {'L1_attn_bkqv': (0.0, 0.372),
     'L1_attn_bp': (0.0, 0.1),
     'L1_ffn_bg': (0.0, 0.8),
     'L1_ffn_b1': (0.0, 0.8),
     'L1_ffn_b2': (0.0, 0.447)}
    factors = {'L1_attn_Wkqv': 8.0,
     'L1_attn_Wp': 2.737,
     'L1_ffn_Wg': 7.464,
     'L1_ffn_W1': 7.396,
     'L1_ffn_W2': 6.721}
    for name, (base, spread) in spreads.items():
        noise = np.random.default_rng([zlib.crc32(name.encode()), seed]).standard_normal(out[name].shape)
        drawn = base * np.exp(spread * noise) if base else spread * noise
        out[name] = jnp.asarray(drawn.astype(out[name].dtype))
    for name, factor in factors.items():
        out[name] = (out[name] * factor).astype(out[name].dtype)
    return out
```

```python
from contextlib import ExitStack

import concourse.bass as bass
from concourse import mybir

ALU = mybir.AluOpType
ACT = mybir.ActivationFunctionType
F32 = mybir.dt.float32
BF16 = mybir.dt.bfloat16
U32 = mybir.dt.uint32
AX_X = mybir.AxisListType.X

P = 128
H = 16
DH = P // H
E = 8
EPS = 1e-5
MASKED = -1e30


def when(eng, semaphore, count):
    if not isinstance(count, int) or count > 0:
        eng.wait_ge(semaphore, count)


def wait_alone(eng, semaphore, count, passed):
    eng.wait_ge(semaphore, count)
    eng.sem_inc(passed, 1)


class Shapes:

    def __init__(self, tokens, seq, hidden):
        self.tokens, self.seq, self.hidden = tokens, seq, hidden
        self.tiles = tokens // P
        self.blocks = seq // P
        self.batches = tokens // seq
        self.chunks = -(-hidden // P)
        self.chunk = hidden // self.chunks
        assert self.chunk * self.chunks == hidden and self.blocks == 4


def layer0(nc, sh, x, xT_in, wqkv, wproj, bproj, gate_w, gate_b, expert_w, expert_b, wv1, bv1,
           keep):
    x_all, xT_all, v_all, ident, ones = keep
    NT = sh.tiles
    with ExitStack() as ctx:
        def sb(name, shape, dt=F32):
            return ctx.enter_context(nc.sbuf_tensor(name, shape, dt))

        def pb(name, shape):
            return ctx.enter_context(nc.psum_tensor(name, shape, F32))

        def sem(name):
            return ctx.enter_context(nc.semaphore(name))

        wqkv_sb = sb("wqkv_sb", [P, 3 * P])
        wproj_sb = sb("wproj_sb", [P, P])
        bproj_sb = sb("bproj_sb", [1, P])
        gatew_sb = sb("gatew_sb", [P, E])
        gateb_sb = sb("gateb_sb", [1, E])
        expw_sb = sb("expw_sb", [P, E * P])
        expb_sb = sb("expb_sb", [E, P])
        wv1_sb = sb("wv1_sb", [P, P])
        bv1_sb = sb("bv1_sb", [1, P])
        iota = sb("iota", [P, E])
        minus_half = sb("minus_half", [P, 1])

        xT = [sb(f"xT{j}", [P, P]) for j in range(2)]
        x2 = [sb(f"x2_{j}", [P, P]) for j in range(2)]
        x2T = [sb(f"x2T{j}", [P, P]) for j in range(2)]
        qkv = [sb(f"qkv{j}", [P, 3 * P]) for j in range(2)]
        qk_prod = sb("qk_prod", [P, H * H * DH])
        pv_prod = sb("pv_prod", [P, H * H * DH])
        scores = sb("scores", [P, H * H])
        score_max = sb("score_max", [P, H])
        shifted = [sb(f"shifted{j}", [P, H * H]) for j in range(2)]
        probs = [sb(f"probs{j}", [P, H * H]) for j in range(2)]
        prob_sum = [sb(f"prob_sum{j}", [P, H]) for j in range(2)]
        prob_rec = [sb(f"prob_rec{j}", [P, H]) for j in range(2)]
        pv_sum = sb("pv_sum", [P, P])
        attn = sb("attn", [P, P])
        attnT = sb("attnT", [P, P])
        r1 = sb("r1", [P, P])
        stats1 = sb("stats1", [P, 6])
        mv1 = sb("mv1", [P, 2])
        var1 = sb("var1", [P, 1])
        rstd1 = sb("rstd1", [P, 1])
        x1 = [sb(f"x1_{j}", [P, P]) for j in range(2)]
        x1T = sb("x1T", [P, P])
        top = sb("top", [P, 8])
        top_idx = sb("top_idx", [P, 8], U32)
        top_idxf = sb("top_idxf", [P, 2])
        gdiff = sb("gdiff", [P, 1])
        gexp = sb("gexp", [P, 1])
        gden = sb("gden", [P, 1])
        gw = sb("gw", [P, 2])
        gate1 = sb("gate1", [P, E])
        gate2 = sb("gate2", [P, E])
        gates = sb("gates", [P, E])
        gatesT = sb("gatesT", [E, P])
        acc = sb("acc", [P, P])
        stats2 = sb("stats2", [P, 6])
        mv2 = sb("mv2", [P, 2])
        var2 = sb("var2", [P, 1])
        rstd2 = sb("rstd2", [P, 1])

        ps_qkv = [pb(f"ps_qkv{j}", [P, 4 * P]) for j in range(2)]
        ps_post = pb("ps_post", [P, 4 * P])
        ps_keep = pb("ps_keep", [P, 4 * P])
        ps_proj_bank = pb("ps_proj_bank", [P, 4 * P])
        ps_gate = pb("ps_gate", [P, 4 * P])
        ps_y = pb("ps_y", [P, E * P])
        ps_oT, ps_x1T, ps_gT = ps_post[:, 0:P], ps_post[:, P:2 * P], ps_post[0:E, 2 * P:3 * P]
        ps_x2T, ps_v = ps_keep[:, 0:P], ps_keep[:, P:2 * P]
        ps_proj = ps_proj_bank[:, 0:P]
        ps_eb, ps_logits = ps_gate[:, 0:P], ps_gate[:, P:P + E]

        consts_made, passed, sp_passed = sem("consts_made"), sem("passed"), sem("sp_passed")
        ident_zeroed = sem("ident_zeroed")
        weights_in = sem("weights_in")
        x_in = [sem(f"x_in{j}") for j in range(2)]
        xT_loaded = [sem(f"xT_loaded{j}") for j in range(2)]
        x2_kept = [sem(f"x2_kept{j}") for j in range(2)]
        x2T_kept = [sem(f"x2T_kept{j}") for j in range(2)]
        qkv_ps, qkv_sb = sem("qkv_ps"), sem("qkv_sb")
        qk_multiplied, scores_summed = sem("qk_multiplied"), sem("scores_summed")
        max_found, scores_shifted = sem("max_found"), sem("scores_shifted")
        probs_ready, probs_summed, recips_ready = sem("probs_ready"), sem("probs_summed"), sem("recips_ready")
        pv_multiplied, pv_summed, attn_ready = sem("pv_multiplied"), sem("pv_summed"), sem("attn_ready")
        oT_ps, oT_sb, proj_ps = sem("oT_ps"), sem("oT_sb"), sem("proj_ps")
        norm1_step, rstd1_ready, x1_ready = sem("norm1_step"), sem("rstd1_ready"), sem("x1_ready")
        x1T_ps, x1T_sb, logits_ps, experts_ps = sem("x1T_ps"), sem("x1T_sb"), sem("logits_ps"), sem("experts_ps")
        gate_step, gate_diff_ready, gate_exp_ready, gates_ready = (
            sem("gate_step"), sem("gate_diff_ready"), sem("gate_exp_ready"), sem("gates_ready"))
        gT_ps, gT_sb, expert_bias_ps = sem("gT_ps"), sem("gT_sb"), sem("expert_bias_ps")
        acc_step, norm2_step, rstd2_ready, x2_ready = (
            sem("acc_step"), sem("norm2_step"), sem("rstd2_ready"), sem("x2_ready"))
        x2T_ps, x2T_sb, v_ps, v_sb = sem("x2T_ps"), sem("x2T_sb"), sem("v_ps"), sem("v_sb")

        NWEIGHTS = 9
        ACC_STEPS = E
        NORM_STEPS = 4
        GATE_STEPS = 8

        def steps(eng, step):
            def one(t):
                step(t // 2, t % 2, (t + 1 < NT, t < NT, 1 <= t <= NT, 2 <= t))
            for t in range(5):
                one(t)
            with eng.Fori(2, NT // 2 - 1) as u:
                step(u, 1, (True, True, True, True))
                step(u + 1, 0, (True, True, True, True))
            for t in range(NT - 1, NT + 2):
                one(t)

        def before(u, j, k):
            return u + (j - k) // 2, (j - k) % 2

        x_tiles = x.rearrange("(t p) d -> p t d", p=P)
        x_sb = x_all[:, :].rearrange("p (t d) -> p t d", d=P)
        v_heads = v_all[:, :].rearrange("p (b h k c) -> p b h k c", h=H, k=sh.blocks, c=DH + 1)

        with nc.Block() as block:

            @block.sync
            def _(sp):
                for dst, src in ((wqkv_sb, wqkv), (wproj_sb, wproj), (bproj_sb, bproj), (gatew_sb, gate_w),
                                 (gateb_sb, gate_b), (expw_sb, expert_w), (expb_sb, expert_b),
                                 (wv1_sb, wv1), (bv1_sb, bv1)):
                    sp.dma_start(dst[:, :], src).then_inc(weights_in, 16)

                def load(u, j):
                    t = 2 * u + j
                    when(sp, x_in[j], 16 * u)
                    sp.sem_inc(sp_passed, 1)
                    sp.dma_start(x_sb[:, bass.ds(t, 1), :], x_tiles[:, bass.ds(t, 1), :]).then_inc(x_in[j], 16)
                    when(sp, qkv_ps, t - 1)
                    sp.sem_inc(sp_passed, 1)
                    sp.dma_start(xT[j][:, :], xT_in[:, bass.ds(t * P, P)]).then_inc(xT_loaded[j], 16)

                def keep_x2(u, j):
                    t = 2 * u + j
                    wait_alone(sp, x2_ready, t + 1, sp_passed)
                    sp.dma_start(x_sb[:, bass.ds(t, 1), :], x2[j][:, :].unsqueeze(1)).then_inc(x2_kept[j], 16)
                    wait_alone(sp, x2T_sb, t + 1, sp_passed)
                    sp.dma_start(xT_all[:, bass.ds(t * P, P)], x2T[j][:, :]).then_inc(x2T_kept[j], 16)

                def step(u, j, part):
                    if part[0]:
                        load(*before(u, j, -1))
                    if part[3]:
                        keep_x2(*before(u, j, 2))
                load(0, 0)
                steps(sp, step)
                for j in range(2):
                    sp.wait_ge(x2_kept[j], 16 * NT // 2)
                    sp.wait_ge(x2T_kept[j], 16 * NT // 2)

            @block.gpsimd
            def _(pool):
                pool.memset(v_all[:, :], 1.0).then_inc(consts_made, 1)
                pool.memset(ones[:, :], 1.0).then_inc(consts_made, 1)
                pool.memset(minus_half[:, :], -0.5).then_inc(consts_made, 1)
                pool.iota(iota[:, :], pattern=[[1, E]], base=0, channel_multiplier=0,
                          allow_small_or_imprecise_dtypes=True).then_inc(consts_made, 1)
                pool.memset(ident[:, :], 0.0).then_inc(ident_zeroed, 1)
                pool.wait_ge(ident_zeroed, 1)
                pool.affine_select(out=ident[:, :], in_=ident[:, :], compare_op=ALU.not_equal, fill=1.0,
                                   base=0, pattern=[[-1, P]], channel_multiplier=1).then_inc(consts_made, 1)
                pool.wait_ge(consts_made, 5)

                def inverse_deviation(u, j, step_sem, var, rstd, done):
                    t = 2 * u + j
                    pool.wait_ge(step_sem, NORM_STEPS * (t + 1))
                    pool.tensor_tensor(rstd[:, :], var[:, :], minus_half[:, :], ALU.pow).then_inc(done, 1)

                def pv_products(u, j):
                    t = 2 * u + j
                    pool.wait_ge(probs_ready, t + 1)
                    when(pool, pv_summed, t)
                    pool.tensor_tensor(
                        pv_prod[:, :].rearrange("p (h d g) -> p h d g", h=H, d=DH),
                        probs[j][:, :].rearrange("p (h g) -> p h g", h=H).unsqueeze(2).to_broadcast([P, H, DH, H]),
                        qkv[j][:, 2 * P:3 * P].rearrange("p (d g) -> p d g", d=DH).unsqueeze(1)
                        .to_broadcast([P, H, DH, H]), ALU.mult).then_inc(pv_multiplied, 1)

                def step(u, j, part):
                    if part[2]:
                        inverse_deviation(*before(u, j, 1), norm1_step, var1, rstd1, rstd1_ready)
                    if part[1]:
                        pv_products(u, j)
                    if part[2]:
                        inverse_deviation(*before(u, j, 1), norm2_step, var2, rstd2, rstd2_ready)
                steps(pool, step)

            @block.tensor
            def _(pe):
                pe.wait_ge(consts_made, 5)
                pe.wait_ge(weights_in, 16 * NWEIGHTS)

                def qkv_product(u, j):
                    t = 2 * u + j
                    pe.wait_ge(xT_loaded[j], 16 * (u + 1))
                    when(pe, qkv_sb, t - 1)
                    pe.matmul(ps_qkv[j][:, 0:3 * P], xT[j][:, :], wqkv_sb[:, :], start=True,
                              stop=True).then_inc(qkv_ps, 1)

                def attention_out(u, j):
                    t = 2 * u + j
                    pe.wait_ge(attn_ready, t + 1)
                    when(pe, gT_sb, t)
                    pe.transpose(ps_oT, attn[:, :], ident[:, :]).then_inc(oT_ps, 1)
                    pe.wait_ge(oT_sb, t + 1)
                    when(pe, norm1_step, NORM_STEPS * t)
                    pe.matmul(ps_proj, attnT[:, :], wproj_sb[:, :], start=True, stop=False)
                    pe.matmul(ps_proj, ones[0:1, 0:P], bproj_sb[:, :], start=False, stop=True).then_inc(proj_ps, 1)

                def experts(u, j):
                    t = 2 * u + j
                    pe.wait_ge(x1_ready, t + 1)
                    pe.transpose(ps_x1T, x1[j][:, :], ident[:, :]).then_inc(x1T_ps, 1)
                    pe.wait_ge(x1T_sb, t + 1)
                    when(pe, norm2_step, NORM_STEPS * t)
                    pe.matmul(ps_logits, x1T[:, :], gatew_sb[:, :], start=True, stop=False)
                    pe.matmul(ps_logits, ones[0:1, 0:P], gateb_sb[:, :], start=False, stop=True)\
                        .then_inc(logits_ps, 1)
                    when(pe, acc_step, ACC_STEPS * t)
                    pe.matmul(ps_y[:, 0:4 * P], x1T[:, :], expw_sb[:, 0:4 * P], start=True, stop=True)
                    pe.matmul(ps_y[:, 4 * P:8 * P], x1T[:, :], expw_sb[:, 4 * P:8 * P], start=True,
                              stop=True).then_inc(experts_ps, 1)
                    pe.wait_ge(gates_ready, t + 1)
                    pe.transpose(ps_gT, gates[:, :], ident[:, :]).then_inc(gT_ps, 1)
                    pe.wait_ge(gT_sb, t + 1)
                    pe.matmul(ps_eb, gatesT[:, :], expb_sb[:, :], start=True, stop=True)\
                        .then_inc(expert_bias_ps, 1)

                def x2_transpose(u, j):
                    t = 2 * u + j
                    pe.wait_ge(x2_ready, t + 1)
                    when(pe, v_sb, t)
                    pe.transpose(ps_x2T, x2[j][:, :], ident[:, :]).then_inc(x2T_ps, 1)

                def values(u, j):
                    t = 2 * u + j
                    pe.wait_ge(x2T_sb, t + 1)
                    pe.matmul(ps_v, x2T[j][:, :], wv1_sb[:, :], start=True, stop=False)
                    pe.matmul(ps_v, ones[0:1, 0:P], bv1_sb[:, :], start=False, stop=True).then_inc(v_ps, 1)

                def step(u, j, part):
                    if part[3]:
                        x2_transpose(*before(u, j, 2))
                    if part[0]:
                        qkv_product(*before(u, j, -1))
                    if part[3]:
                        values(*before(u, j, 2))
                    if part[2]:
                        attention_out(*before(u, j, 1))
                        experts(*before(u, j, 1))
                qkv_product(0, 0)
                steps(pe, step)

            @block.scalar
            def _(act):
                act.wait_ge(consts_made, 5)

                def copy_qkv(u, j):
                    t = 2 * u + j
                    act.wait_ge(qkv_ps, t + 1)
                    when(act, qk_multiplied, t - 1)
                    when(act, pv_multiplied, t - 1)
                    act.copy(qkv[j][:, :], ps_qkv[j][:, 0:3 * P]).then_inc(qkv_sb, 1)

                def copy_oT(u, j):
                    t = 2 * u + j
                    act.wait_ge(oT_ps, t + 1)
                    when(act, proj_ps, t)
                    act.copy(attnT[:, :], ps_oT).then_inc(oT_sb, 1)

                def exponentials(u, j):
                    t = 2 * u + j
                    act.wait_ge(scores_shifted, t + 1)
                    when(act, pv_multiplied, t - 1)
                    when(act, probs_summed, t - 1)
                    act.activation(probs[j][:, :], shifted[j][:, :], ACT.Exp, scale=0.125)\
                        .then_inc(probs_ready, 1)

                def copy_x1T(u, j):
                    t = 2 * u + j
                    act.wait_ge(x1T_ps, t + 1)
                    when(act, experts_ps, t)
                    act.copy(x1T[:, :], ps_x1T).then_inc(x1T_sb, 1)

                def gate_exp(u, j):
                    t = 2 * u + j
                    act.wait_ge(gate_diff_ready, t + 1)
                    act.activation(gexp[:, :], gdiff[:, :], ACT.Exp).then_inc(gate_exp_ready, 1)

                def copy_gT(u, j):
                    t = 2 * u + j
                    act.wait_ge(gT_ps, t + 1)
                    when(act, expert_bias_ps, t)
                    act.copy(gatesT[:, :], ps_gT).then_inc(gT_sb, 1)

                def copy_x2T(u, j):
                    t = 2 * u + j
                    act.wait_ge(x2T_ps, t + 1)
                    when(act, v_ps, t - 1)
                    when(act, x2T_kept[j], 16 * u)
                    act.copy(x2T[j][:, :], ps_x2T).then_inc(x2T_sb, 1)

                def copy_v(u, j):
                    t = 2 * u + j
                    act.wait_ge(v_ps, t + 1)
                    act.copy(v_heads[:, bass.ds(u // 2, 1), :, bass.ds((u % 2) * 2 + j, 1), 0:DH]
                             .rearrange("p b h k c -> p (b h k) c"),
                             ps_v.rearrange("p (h c) -> p h c", h=H)).then_inc(v_sb, 1)

                def step(u, j, part):
                    if part[3]:
                        copy_x2T(*before(u, j, 2))
                    if part[0]:
                        copy_qkv(*before(u, j, -1))
                    if part[3]:
                        copy_v(*before(u, j, 2))
                    if part[2]:
                        copy_oT(*before(u, j, 1))
                    if part[1]:
                        exponentials(u, j)
                    if part[2]:
                        copy_x1T(*before(u, j, 1))
                        gate_exp(*before(u, j, 1))
                        copy_gT(*before(u, j, 1))
                copy_qkv(0, 0)
                steps(act, step)

            @block.vector
            def _(dve):
                dve.wait_ge(consts_made, 5)

                def qk_products(u, j):
                    t = 2 * u + j
                    dve.wait_ge(qkv_sb, t + 1)
                    when(dve, scores_summed, t)
                    dve.tensor_tensor(
                        qk_prod[:, :].rearrange("p (h g d) -> p h g d", h=H, g=H),
                        qkv[j][:, 0:P].rearrange("p (h d) -> p h d", h=H).unsqueeze(2).to_broadcast([P, H, H, DH]),
                        qkv[j][:, P:2 * P].rearrange("p (g d) -> p g d", g=H).unsqueeze(1)
                        .to_broadcast([P, H, H, DH]), ALU.mult).then_inc(qk_multiplied, 1)

                def qk_sums(u, j):
                    t = 2 * u + j
                    dve.wait_ge(qk_multiplied, t + 1)
                    when(dve, scores_shifted, t)
                    dve.tensor_reduce(scores[:, :], qk_prod[:, :].rearrange("p (s d) -> p s d", d=DH),
                                      AX_X, ALU.add).then_inc(scores_summed, 1)

                def shift_scores(u, j):
                    t = 2 * u + j
                    by_head = scores[:, :].rearrange("p (h g) -> p h g", h=H)
                    dve.wait_ge(scores_summed, t + 1)
                    dve.tensor_reduce(score_max[:, :], by_head, AX_X, ALU.max).then_inc(max_found, 1)
                    dve.wait_ge(max_found, t + 1)
                    when(dve, probs_ready, t - 1)
                    dve.tensor_tensor(shifted[j][:, :].rearrange("p (h g) -> p h g", h=H), by_head,
                                      score_max[:, :].unsqueeze(2).to_broadcast([P, H, H]),
                                      ALU.subtract).then_inc(scores_shifted, 1)

                def prob_sums(u, j):
                    t = 2 * u + j
                    dve.wait_ge(probs_ready, t + 1)
                    when(dve, recips_ready, t - 1)
                    dve.tensor_reduce(prob_sum[j][:, :], probs[j][:, :].rearrange("p (h g) -> p h g", h=H),
                                      AX_X, ALU.add).then_inc(probs_summed, 1)
                    dve.wait_ge(probs_summed, t + 1)
                    when(dve, attn_ready, t - 1)
                    dve.reciprocal(prob_rec[j][:, :], prob_sum[j][:, :]).then_inc(recips_ready, 1)

                def pv_sums(u, j):
                    t = 2 * u + j
                    dve.wait_ge(pv_multiplied, t + 1)
                    when(dve, attn_ready, t)
                    dve.tensor_reduce(pv_sum[:, :], pv_prod[:, :].rearrange("p (s g) -> p s g", g=H),
                                      AX_X, ALU.add).then_inc(pv_summed, 1)
                    dve.wait_ge(pv_summed, t + 1)
                    dve.wait_ge(recips_ready, t + 1)
                    when(dve, oT_ps, t)
                    dve.tensor_tensor(attn[:, :].rearrange("p (h d) -> p h d", h=H),
                                      pv_sum[:, :].rearrange("p (h d) -> p h d", h=H),
                                      prob_rec[j][:, :].unsqueeze(2).to_broadcast([P, H, DH]),
                                      ALU.mult).then_inc(attn_ready, 1)

                def norm_stats(t, row, stats, mv, var, count):
                    base = NORM_STEPS * t
                    dve.wait_ge(count, base + 1)
                    dve.bn_stats(stats[:, :], row).then_inc(count, 1)
                    wait_alone(dve, count, base + 2, passed)
                    dve.bn_aggr(mv[:, :], stats[:, :]).then_inc(count, 1)
                    dve.wait_ge(count, base + 3)
                    dve.tensor_scalar(var[:, :], mv[:, 1:2], EPS, None, ALU.add).then_inc(count, 1)

                def residual1(u, j):
                    t = 2 * u + j
                    dve.wait_ge(x_in[j], 16 * (u + 1))
                    dve.wait_ge(proj_ps, t + 1)
                    when(dve, x1_ready, t)
                    dve.tensor_tensor(r1[:, :], x_sb[:, bass.ds(t, 1), :].rearrange("p a d -> p (a d)"), ps_proj,
                                      ALU.add).then_inc(norm1_step, 1)
                    norm_stats(t, r1[:, :], stats1, mv1, var1, norm1_step)

                def norm1(u, j):
                    t = 2 * u + j
                    dve.wait_ge(rstd1_ready, t + 1)
                    when(dve, x1T_ps, t - 1)
                    when(dve, acc_step, ACC_STEPS * (t - 1))
                    dve.tensor_scalar(x1[j][:, :], r1[:, :], mv1[:, 0:1], rstd1[:, :], ALU.subtract,
                                      ALU.mult).then_inc(x1_ready, 1)

                def gate(u, j):
                    t = 2 * u + j
                    base = GATE_STEPS * t
                    dve.wait_ge(logits_ps, t + 1)
                    when(dve, gates_ready, t)
                    dve.sem_inc(passed, 1)
                    dve.max(top[:, :], ps_logits).then_inc(gate_step, 1)
                    dve.wait_ge(gate_step, base + 1)
                    dve.tensor_tensor(gdiff[:, :], top[:, 1:2], top[:, 0:1], ALU.subtract)\
                        .then_inc(gate_diff_ready, 1)
                    dve.max_index(top_idx[:, :], top[:, :], ps_logits).then_inc(gate_step, 1)
                    dve.wait_ge(gate_step, base + 2)
                    dve.tensor_copy(top_idxf[:, :], top_idx[:, 0:2]).then_inc(gate_step, 1)
                    dve.wait_ge(gate_exp_ready, t + 1)
                    dve.tensor_scalar(gden[:, :], gexp[:, :], 1.0, None, ALU.add).then_inc(gate_step, 1)
                    dve.wait_ge(gate_step, base + 4)
                    dve.reciprocal(gw[:, 0:1], gden[:, :]).then_inc(gate_step, 1)
                    dve.wait_ge(gate_step, base + 5)
                    dve.tensor_tensor(gw[:, 1:2], gexp[:, :], gw[:, 0:1], ALU.mult).then_inc(gate_step, 1)
                    dve.tensor_scalar(gate1[:, :], iota[:, :], top_idxf[:, 0:1], gw[:, 0:1], ALU.is_equal,
                                      ALU.mult).then_inc(gate_step, 1)
                    dve.wait_ge(gate_step, base + 7)
                    dve.tensor_scalar(gate2[:, :], iota[:, :], top_idxf[:, 1:2], gw[:, 1:2], ALU.is_equal,
                                      ALU.mult).then_inc(gate_step, 1)
                    dve.wait_ge(gate_step, base + 8)
                    when(dve, gT_ps, t)
                    when(dve, acc_step, ACC_STEPS * t)
                    dve.tensor_tensor(gates[:, :], gate1[:, :], gate2[:, :], ALU.add).then_inc(gates_ready, 1)

                def combine(u, j):
                    t = 2 * u + j
                    base = ACC_STEPS * t
                    dve.wait_ge(experts_ps, t + 1)
                    dve.wait_ge(gates_ready, t + 1)
                    when(dve, x2_ready, t)
                    dve.scalar_tensor_tensor(out=acc[:, :], in0=ps_y[:, 0:P], scalar=gates[:, 0:1],
                                             in1=x1[j][:, :], op0=ALU.mult, op1=ALU.add).then_inc(acc_step, 1)
                    for e in range(1, E):
                        dve.wait_ge(acc_step, base + e)
                        dve.scalar_tensor_tensor(out=acc[:, :], in0=ps_y[:, e * P:(e + 1) * P],
                                                 scalar=gates[:, e:e + 1], in1=acc[:, :], op0=ALU.mult,
                                                 op1=ALU.add).then_inc(acc_step, 1)
                    dve.wait_ge(acc_step, base + E)
                    dve.wait_ge(expert_bias_ps, t + 1)
                    dve.tensor_tensor(acc[:, :], acc[:, :], ps_eb, ALU.add).then_inc(norm2_step, 1)
                    norm_stats(t, acc[:, :], stats2, mv2, var2, norm2_step)

                def norm2(u, j):
                    t = 2 * u + j
                    dve.wait_ge(rstd2_ready, t + 1)
                    when(dve, x2T_ps, t - 1)
                    when(dve, x2_kept[j], 16 * u)
                    dve.tensor_scalar(x2[j][:, :], acc[:, :], mv2[:, 0:1], rstd2[:, :], ALU.subtract,
                                      ALU.mult).then_inc(x2_ready, 1)

                def step(u, j, part):
                    if part[1]:
                        qk_products(u, j)
                    if part[3]:
                        norm2(*before(u, j, 2))
                    if part[2]:
                        pv_sums(*before(u, j, 1))
                    if part[1]:
                        qk_sums(u, j)
                    if part[2]:
                        residual1(*before(u, j, 1))
                    if part[1]:
                        shift_scores(u, j)
                    if part[2]:
                        norm1(*before(u, j, 1))
                    if part[1]:
                        prob_sums(u, j)
                    if part[2]:
                        gate(*before(u, j, 1))
                        combine(*before(u, j, 1))
                steps(dve, step)


def attention1(nc, sh, wqT, wkT, bq, keep, sa_all):
    xT_all, v_all, ident = keep
    S, B = sh.seq, sh.blocks
    NK = sh.batches * H
    PV = DH + 1
    SCALE = float(P) ** -0.5
    with ExitStack() as ctx:
        def sb(name, shape, dt=F32):
            return ctx.enter_context(nc.sbuf_tensor(name, shape, dt))

        def sem(name):
            return ctx.enter_context(nc.semaphore(name))

        wq = sb("wq_sb", [P, H * P])
        wk = sb("wk_sb", [P, H * P])
        bq_sb = sb("bq_sb", [P, H])
        m_all = sb("m_all", [P, H * P])
        mb_all = sb("mb_all", [P, H])
        m_head = [sb(f"m_head{j}", [P, P]) for j in range(2)]
        ident16 = sb("ident16", [P, P], BF16)
        mask16 = sb("mask16", [P, P], BF16)
        qm = [sb(f"qm{j}", [P, S]) for j in range(2)]
        neg_max = sb("neg_max", [P, B])
        probs = [sb(f"p{i}", [P, (i + 1) * P]) for i in range(B)]
        probsT = [sb(f"pT{i}", [P, (i + 1) * P]) for i in range(B)]
        recip = sb("recip", [P, B])

        ps_s = [ctx.enter_context(nc.psum_tensor(f"ps_s{i}", [P, S], F32)) for i in range(B)]
        ps_t = [ctx.enter_context(nc.psum_tensor(f"ps_t{i}", [P, S], F32)) for i in range(2)]
        ps_qm = ctx.enter_context(nc.psum_tensor("ps_qm", [P, S], F32))
        ps_o = ctx.enter_context(nc.psum_tensor("ps_o", [P, S], F32))
        out_ps = ps_o[:, 0:B * PV].rearrange("p (i c) -> p i c", c=PV)

        weights_in = sem("b_weights_in")
        consts_zeroed, consts_made = sem("b_consts_zeroed"), sem("b_consts_made")
        m_ps, m_sb = sem("m_ps"), sem("m_sb")
        mb_ps, mb_sb = sem("mb_ps"), sem("mb_sb")
        m_head_ready = sem("m_head_ready")
        qm_ps, qm_sb = sem("qm_ps"), sem("qm_sb")
        scores_ps = [sem(f"scores_ps{i}") for i in range(B)]
        max_ready = [sem(f"max_ready{i}") for i in range(B)]
        probs_ready = [sem(f"probs_ready{i}") for i in range(B)]
        pT_ps = [sem(f"pT_ps{i}") for i in range(B)]
        pT_sb = [sem(f"pT_sb{i}") for i in range(B)]
        out_block = [sem(f"out_block{i}") for i in range(B)]
        recips_ready, out_ready = sem("b_recips_ready"), sem("out_ready")

        def steps(step):
            def one(k):
                step(k // 2, k % 2, k + 1 < NK, k >= 1, k < NK)
            def run(eng):
                one(0)
                one(1)
                with eng.Fori(1, NK // 2 - 1) as u:
                    for j in range(2):
                        step(u, j, True, True, True)
                for k in range(NK - 2, NK + 1):
                    one(k)
            return run

        def before(u, j, k):
            return u + (j - k) // 2, (j - k) % 2

        sa_steps = sa_all[:, :].rearrange("p (k i c) -> p k i c", i=B, c=DH)

        def sequence(u):
            return u // (H // 2)

        with nc.Block() as block:

            @block.sync
            def _(sp):
                sp.dma_start(wq[:, :], wqT).then_inc(weights_in, 16)
                sp.dma_start(wk[:, :], wkT).then_inc(weights_in, 16)
                sp.dma_start(bq_sb[:, :], bq).then_inc(weights_in, 16)

            @block.gpsimd
            def _(pool):
                pool.memset(mask16[:, :], 0.0).then_inc(consts_zeroed, 1)
                pool.tensor_copy(ident16[:, :], ident[:, :]).then_inc(consts_made, 1)
                pool.wait_ge(consts_zeroed, 1)
                pool.affine_select(out=mask16[:, :], in_=mask16[:, :], compare_op=ALU.is_ge, fill=MASKED,
                                   base=0, pattern=[[-1, P]], channel_multiplier=1).then_inc(consts_made, 1)
                pool.wait_ge(m_sb, H // 4)

                def load_head(u, j):
                    k = 2 * u + j
                    when(pool, qm_ps, k - 1)
                    pool.tensor_copy(m_head[j][:, :], m_all[:, bass.ds((k % H) * P, P)])\
                        .then_inc(m_head_ready, 1)

                def step(u, j, nxt, last, this):
                    if nxt:
                        load_head(*before(u, j, -1))
                load_head(0, 0)
                steps(step)(pool)

            @block.tensor
            def _(pe):
                pe.wait_ge(weights_in, 48)
                for g in range(H // 4):
                    for h in range(4 * g, 4 * g + 4):
                        mm = pe.matmul(ps_s[g][:, (h % 4) * P:(h % 4 + 1) * P], wq[:, h * P:(h + 1) * P],
                                       wk[:, h * P:(h + 1) * P], start=True, stop=True)
                    mm.then_inc(m_ps, 1)
                for h in range(H):
                    mm = pe.matmul(ps_qm[:, h:h + 1], wk[:, h * P:(h + 1) * P], bq_sb[:, h:h + 1],
                                   start=True, stop=True)
                mm.then_inc(mb_ps, 1)
                pe.wait_ge(consts_made, 2)
                pe.wait_ge(m_sb, H // 4)
                pe.wait_ge(mb_sb, 1)

                def queries(u, j):
                    k = 2 * u + j
                    pe.wait_ge(m_head_ready, k + 1)
                    when(pe, qm_sb, k)
                    pe.matmul(ps_qm[:, :], m_head[j][:, :], xT_all[:, bass.ds(sequence(u) * S, S)],
                              start=True, stop=True).then_inc(qm_ps, 1)

                def scores(u, j, i):
                    k = 2 * u + j
                    pe.wait_ge(qm_sb, k + 1)
                    when(pe, probs_ready[i], k)
                    n = (i + 1) * P
                    pe.matmul(ps_s[i][:, 0:n], qm[j][:, i * P:n], xT_all[:, bass.ds(sequence(u) * S, n)],
                              start=True, stop=False)
                    pe.matmul(ps_s[i][:, i * P:n], ident16[:, :], mask16[:, :], start=False, stop=True)\
                        .then_inc(scores_ps[i], 1)

                def turn(u, j, i):
                    k = 2 * u + j
                    pe.wait_ge(probs_ready[i], k + 1)
                    if i >= 2:
                        pe.wait_ge(pT_sb[i - 2], k + 1)
                    else:
                        when(pe, pT_sb[i + 2], k)
                    for n in range(i + 1):
                        mm = pe.transpose(ps_t[i % 2][:, n * P:(n + 1) * P], probs[i][:, n * P:(n + 1) * P],
                                          ident[:, :])
                    mm.then_inc(pT_ps[i], 1)

                def weighted_values(u, j, i):
                    k = 2 * u + j
                    pe.wait_ge(pT_sb[i], k + 1)
                    if i == 0:
                        when(pe, out_ready, k)
                    for n in range(i + 1):
                        mm = pe.matmul(out_ps[:, i, :], probsT[i][:, n * P:(n + 1) * P],
                                       v_all[:, bass.ds((k * B + n) * PV, PV)], start=(n == 0), stop=(n == i))
                    mm.then_inc(out_block[i], 1)

                def step(u, j, nxt, last, this):
                    b = before(u, j, 1)
                    if this:
                        scores(u, j, 0)
                    if last:
                        turn(*b, 0)
                        turn(*b, 1)
                    if this:
                        scores(u, j, 1)
                    if last:
                        weighted_values(*b, 0)
                        turn(*b, 2)
                    if this:
                        scores(u, j, 2)
                    if last:
                        weighted_values(*b, 1)
                        turn(*b, 3)
                    if nxt:
                        queries(*before(u, j, -1))
                    if last:
                        weighted_values(*b, 2)
                    if this:
                        scores(u, j, 3)
                    if last:
                        weighted_values(*b, 3)
                queries(0, 0)
                steps(step)(pe)

            @block.scalar
            def _(act):
                for g in range(H // 4):
                    act.wait_ge(m_ps, g + 1)
                    act.copy(m_all[:, g * 4 * P:(g + 1) * 4 * P], ps_s[g][:, :]).then_inc(m_sb, 1)
                act.wait_ge(mb_ps, 1)
                act.mul(mb_all[:, :], ps_qm[:, 0:H], SCALE).then_inc(mb_sb, 1)
                act.wait_ge(mb_sb, 1)

                def copy_queries(u, j):
                    k = 2 * u + j
                    act.wait_ge(qm_ps, k + 1)
                    when(act, scores_ps[B - 1], k - 1)
                    act.activation(qm[j][:, :], ps_qm[:, :], ACT.Identity,
                                   bias=mb_all[:, bass.ds(k % H, 1)], scale=SCALE).then_inc(qm_sb, 1)

                def exponentials(u, j, i):
                    k = 2 * u + j
                    act.wait_ge(max_ready[i], k + 1)
                    when(act, pT_ps[i], k)
                    act.activation(probs[i][:, :], ps_s[i][:, 0:(i + 1) * P], ACT.Exp,
                                   bias=neg_max[:, i:i + 1]).then_inc(probs_ready[i], 1)

                def copy_turned(u, j, i):
                    k = 2 * u + j
                    act.wait_ge(pT_ps[i], k + 1)
                    when(act, out_block[i], k)
                    act.copy(probsT[i][:, :], ps_t[i % 2][:, 0:(i + 1) * P]).then_inc(pT_sb[i], 1)

                def step(u, j, nxt, last, this):
                    b = before(u, j, 1)
                    if this:
                        exponentials(u, j, 0)
                        exponentials(u, j, 1)
                    if this:
                        exponentials(u, j, 2)
                    if last:
                        copy_turned(*b, 3)
                    if nxt:
                        copy_queries(*before(u, j, -1))
                    if this:
                        exponentials(u, j, 3)
                copy_queries(0, 0)
                steps(step)(act)

            @block.vector
            def _(dve):
                def row_max(u, j, i):
                    k = 2 * u + j
                    dve.wait_ge(scores_ps[i], k + 1)
                    dve.tensor_reduce(neg_max[:, i:i + 1], ps_s[i][:, 0:(i + 1) * P], AX_X, ALU.max,
                                      negate=True).then_inc(max_ready[i], 1)

                def copy_turned(u, j, i):
                    k = 2 * u + j
                    dve.wait_ge(pT_ps[i], k + 1)
                    when(dve, out_block[i], k)
                    dve.tensor_copy(probsT[i][:, :], ps_t[i % 2][:, 0:(i + 1) * P]).then_inc(pT_sb[i], 1)

                def normalise(u, j):
                    k = 2 * u + j
                    dve.wait_ge(out_block[B - 1], k + 1)
                    when(dve, out_ready, k)
                    dve.reciprocal(recip[:, :], out_ps[:, :, DH]).then_inc(recips_ready, 1)
                    dve.wait_ge(recips_ready, k + 1)
                    dve.tensor_tensor(sa_steps[:, bass.ds(k, 1), :, :].rearrange("p k i c -> p (k i) c"),
                                      out_ps[:, :, 0:DH], recip[:, :].unsqueeze(2).to_broadcast([P, B, DH]),
                                      ALU.mult).then_inc(out_ready, 1)

                def step(u, j, nxt, last, this):
                    b = before(u, j, 1)
                    if this:
                        row_max(u, j, 0)
                    if last:
                        copy_turned(*b, 0)
                        copy_turned(*b, 1)
                    if this:
                        row_max(u, j, 1)
                    if last:
                        copy_turned(*b, 2)
                    if this:
                        row_max(u, j, 2)
                        row_max(u, j, 3)
                    if last:
                        normalise(*b)
                steps(step)(dve)


def finish1(nc, sh, wp, bp, cT, wg, bg, w1, b1, w2, b2, keep, sa_all, out):
    x_all, ident, ones = keep
    B, S, C, CH = sh.blocks, sh.seq, sh.chunks, sh.chunk
    NG = sh.batches
    with ExitStack() as ctx:
        def sb(name, shape, dt=F32):
            return ctx.enter_context(nc.sbuf_tensor(name, shape, dt))

        def sem(name):
            return ctx.enter_context(nc.semaphore(name))

        wp_sb, bp_sb = sb("wp_sb", [P, P]), sb("bp_sb", [1, P])
        cT_sb, cT2, csq_in, csq = sb("cT_sb", [P, E]), sb("cT2", [P, E]), sb("csq_in", [P, E]), sb("csq", [1, E])
        ones_col = sb("ones_col", [P, 1])
        wg_sb, w1_sb = sb("wg_sb", [P, E * C * CH]), sb("w1_sb", [P, E * C * CH])
        bg_sb, b1_sb = sb("bg_sb", [CH, E * C]), sb("b1_sb", [CH, E * C])
        w2_sb, b2_sb = sb("w2_sb", [CH, E * C * P]), sb("b2_sb", [E, P])
        iota = sb("c_iota", [P, E])
        exponents = sb("exponents", [P, B * E])
        minus_half = sb("c_minus_half", [P, B])

        sa_tile = sb("sa_tile", [P, S])
        saT = sb("saT", [P, S])
        r3 = sb("r3", [P, S])
        stats3, mv3, var3, rstd3 = sb("stats3", [P, B * 6]), sb("mv3", [P, B * 2]), sb("var3", [P, B]), sb("rstd3", [P, B])
        x3 = [sb(f"x3_{j}", [P, S]) for j in range(2)]
        x3T = [sb(f"x3T_{j}", [P, S]) for j in range(2)]
        square, norm_sq = sb("square", [P, P]), sb("norm_sq", [P, B])
        dist2, dist = sb("dist2", [P, B * E]), sb("dist", [P, B * E])
        top, top_idx, top_idxf = sb("c_top", [P, B * 8]), sb("c_top_idx", [P, B * 8], U32), sb("c_top_idxf", [P, B * 8])
        wdiff, wexp, wden = sb("wdiff", [P, B]), sb("wexp", [P, B]), sb("wden", [P, B])
        pair = sb("pair", [P, 2 * B])
        first, second = sb("first", [P, B * E]), sb("second", [P, B * E])
        we = [sb(f"we{j}", [P, B * E]) for j in range(2)]
        weT = sb("weT", [E, S])
        acc = [sb(f"c_acc{j}", [P, S]) for j in range(2)]
        silu = [sb(f"silu{i}", [CH, S]) for i in range(2)]
        hid = [sb(f"hid{i}", [CH, S]) for i in range(2 * C)]
        stats4, mv4, var4, rstd4 = sb("stats4", [P, B * 6]), sb("mv4", [P, B * 2]), sb("var4", [P, B]), sb("rstd4", [P, B])
        x4 = sb("x4", [P, S])

        def pb(name):
            return ctx.enter_context(nc.psum_tensor(name, [P, S], F32))
        ps_turn, ps_front = pb("ps_turn"), pb("ps_front")
        ps_gate = [pb(f"ps_g{i}") for i in range(2)]
        ps_up = [pb(f"ps_u{i}") for i in range(2)]
        ps_y = [pb(f"ps_yy{i}") for i in range(2)]

        weights_in = sem("c_weights_in")
        consts_made, c_squared, csq_ps, c_ready = sem("c_consts"), sem("c_squared"), sem("csq_ps"), sem("c_ready")
        sa_copied, saT_ps, saT_sb, proj_ps = sem("sa_copied"), sem("saT_ps"), sem("saT_sb"), sem("c_proj_ps")
        norm3_step, rstd3_ready, x3_ready = sem("norm3_step"), sem("rstd3_ready"), sem("x3_ready")
        x3T_ps, x3T_sb, dist_ps = sem("x3T_ps"), sem("x3T_sb"), sem("dist_ps")
        square_step, dist2_ready, dist_ready = sem("square_step"), sem("dist2_ready"), sem("dist_ready")
        pick_step, wdiff_ready, wexp_ready, we_ready = sem("pick_step"), sem("wdiff_ready"), sem("wexp_ready"), sem("we_ready")
        weT_ps, weT_sb, bias_ps, acc_begun = sem("weT_ps"), sem("weT_sb"), sem("bias_ps"), sem("acc_begun")
        gate_ps, up_ps, silu_ready, hid_ready = sem("gate_ps"), sem("up_ps"), sem("silu_ready"), sem("hid_ready")
        y_ps, acc_step = sem("y_ps"), sem("c_acc_step")
        passed, sp_passed = sem("c_passed"), sem("c_sp_passed")
        norm4_step, rstd4_ready, x4_ready, stored = sem("norm4_step"), sem("rstd4_ready"), sem("x4_ready"), sem("stored")

        NWEIGHTS = 9
        NORM = B * 2 + 2
        NORM4 = B * 2 + 1
        EC = E * C

        def groups(eng, group):
            group(0, 0, True)
            with eng.Fori(0, NG // 2 - 1) as u:
                group(u, 1, True)
                group(u + 1, 0, True)
            group(NG // 2 - 1, 1, False)

        def after(u, j):
            return (u, 1) if j == 0 else (u + 1, 0)

        def blk(t, i, n=P):
            return t[:, i * n:(i + 1) * n]

        sa_groups = sa_all[:, :].rearrange("p (g h i c) -> p g h i c", h=H, i=B, c=DH)
        out_groups = out.rearrange("(g i p) d -> p g i d", i=B, p=P)

        with nc.Block() as block:

            @block.sync
            def _(sp):
                for dst, src in ((wp_sb, wp), (bp_sb, bp), (cT_sb, cT), (wg_sb, wg), (w1_sb, w1), (bg_sb, bg),
                                 (b1_sb, b1), (w2_sb, w2), (b2_sb, b2)):
                    sp.dma_start(dst[:, :], src).then_inc(weights_in, 16)

                def group(u, j, nxt):
                    g = 2 * u + j
                    wait_alone(sp, x4_ready, B * (g + 1), sp_passed)
                    sp.dma_start(out_groups[:, bass.ds(g, 1), :, :].rearrange("p g i d -> p (g i) d"),
                                 x4[:, :].rearrange("p (i d) -> p i d", d=P)).then_inc(stored, 16)
                    wait_alone(sp, stored, 16 * (g + 1), sp_passed)
                groups(sp, group)

            @block.gpsimd
            def _(pool):
                pool.iota(iota[:, :], pattern=[[1, E]], base=0, channel_multiplier=0,
                          allow_small_or_imprecise_dtypes=True).then_inc(consts_made, 1)
                pool.memset(exponents[:, :], 0.5).then_inc(consts_made, 1)
                pool.memset(minus_half[:, :], -0.5).then_inc(consts_made, 1)
                pool.memset(ones_col[:, :], 1.0).then_inc(consts_made, 1)
                pool.wait_ge(consts_made, 4)

                def copy_sa(u, j):
                    g = 2 * u + j
                    when(pool, saT_ps, g)
                    src = sa_groups[:, bass.ds(g, 1), :, :, :].rearrange("p g h i c -> p (g h) i c")
                    for i in range(B):
                        pool.tensor_copy(blk(sa_tile, i).rearrange("p (h c) -> p h c", c=DH), src[:, :, i, :])\
                            .then_inc(sa_copied, 1)

                def inverse3(u, j):
                    g = 2 * u + j
                    pool.wait_ge(norm3_step, NORM * (g + 1))
                    pool.tensor_tensor(rstd3[:, :], var3[:, :], minus_half[:, :], ALU.pow).then_inc(rstd3_ready, 1)

                def distances(u, j):
                    g = 2 * u + j
                    pool.wait_ge(dist2_ready, B * (g + 1))
                    pool.tensor_tensor(dist[:, :], dist2[:, :], exponents[:, :], ALU.pow).then_inc(dist_ready, 1)

                def inverse4(u, j):
                    g = 2 * u + j
                    pool.wait_ge(norm4_step, NORM4 * (g + 1))
                    pool.tensor_tensor(rstd4[:, :], var4[:, :], minus_half[:, :], ALU.pow).then_inc(rstd4_ready, 1)

                def front(u, j):
                    copy_sa(u, j)
                    inverse3(u, j)
                    distances(u, j)

                def group(u, j, nxt):
                    if nxt:
                        front(*after(u, j))
                    inverse4(u, j)
                front(0, 0)
                groups(pool, group)

            @block.tensor
            def _(pe):
                pe.wait_ge(weights_in, 16 * NWEIGHTS)
                pe.wait_ge(consts_made, 4)
                pe.wait_ge(c_squared, 2)
                pe.matmul(ps_front[0:1, 0:E], ones_col[:, :], csq_in[:, :], start=True, stop=True).then_inc(csq_ps, 1)
                pe.wait_ge(c_ready, 1)

                def turn_sa(u, j):
                    g = 2 * u + j
                    pe.wait_ge(sa_copied, B * (g + 1))
                    when(pe, weT_sb, g)
                    for i in range(B):
                        mm = pe.transpose(blk(ps_turn, i), blk(sa_tile, i), ident[:, :])
                    mm.then_inc(saT_ps, 1)

                def project(u, j):
                    g = 2 * u + j
                    pe.wait_ge(saT_sb, g + 1)
                    when(pe, acc_begun, g)
                    for i in range(B):
                        pe.matmul(blk(ps_front, i), blk(saT, i), wp_sb[:, :], start=True, stop=False)
                        mm = pe.matmul(blk(ps_front, i), ones[0:1, 0:P], bp_sb[:, :], start=False, stop=True)
                    mm.then_inc(proj_ps, 1)

                def turn_x3(u, j):
                    g = 2 * u + j
                    pe.wait_ge(x3_ready, B * (g + 1))
                    for i in range(B):
                        mm = pe.transpose(blk(ps_turn, i), blk(x3[j], i), ident[:, :])
                    mm.then_inc(x3T_ps, 1)

                def centroid_products(u, j):
                    g = 2 * u + j
                    pe.wait_ge(x3T_sb, g + 1)
                    for i in range(B):
                        pe.matmul(blk(ps_front, i, E), blk(x3T[j], i), cT2[:, :], start=True, stop=False)
                        mm = pe.matmul(blk(ps_front, i, E), ones[0:1, 0:P], csq[:, :], start=False, stop=True)
                    mm.then_inc(dist_ps, 1)

                def gated_biases(u, j):
                    g = 2 * u + j
                    pe.wait_ge(we_ready, g + 1)
                    for i in range(B):
                        mm = pe.transpose(ps_turn[0:E, i * P:(i + 1) * P], blk(we[j], i, E), ident[:, :])
                    mm.then_inc(weT_ps, 1)
                    pe.wait_ge(weT_sb, g + 1)
                    for i in range(B):
                        mm = pe.matmul(blk(ps_front, i), blk(weT, i), b2_sb[:, :], start=True, stop=True)
                    mm.then_inc(bias_ps, 1)

                def hidden(u, j, e, c):
                    n = EC * (2 * u + j) + e * C + c
                    when(pe, silu_ready, n - 1)
                    w = e * C + c
                    pe.matmul(ps_gate[w % 2][0:CH, :], blk(wg_sb, w, CH), x3T[j][:, :], start=True, stop=True)\
                        .then_inc(gate_ps, 1)
                    when(pe, hid_ready, n - 1)
                    pe.matmul(ps_up[w % 2][0:CH, :], blk(w1_sb, w, CH), x3T[j][:, :], start=True, stop=True)\
                        .then_inc(up_ps, 1)

                def down(u, j, e):
                    g = 2 * u + j
                    pe.wait_ge(hid_ready, EC * g + (e + 1) * C)
                    when(pe, acc_step, B * (E * g + e - 1))
                    for i in range(B):
                        for c in range(C):
                            mm = pe.matmul(blk(ps_y[e % 2], i), blk(hid[(e % 2) * C + c], i),
                                           blk(w2_sb, e * C + c), start=(c == 0), stop=(c == C - 1))
                    mm.then_inc(y_ps, 1)

                front = {0: turn_sa, 1: project, 4: turn_x3, 5: centroid_products, 7: gated_biases}

                def group(u, j, nxt):
                    for e in range(E):
                        hidden(u, j, e, 0)
                        if nxt and e in front:
                            front[e](*after(u, j))
                        hidden(u, j, e, 1)
                        if e:
                            down(u, j, e - 1)
                        hidden(u, j, e, 2)
                    down(u, j, E - 1)
                for e in sorted(front):
                    front[e](0, 0)
                groups(pe, group)

            @block.scalar
            def _(act):
                def copy(dst, src, ready, count, done, free=None, free_count=0):
                    act.wait_ge(ready, count)
                    if free is not None:
                        when(act, free, free_count)
                    act.copy(dst, src).then_inc(done, 1)

                def front_saT(u, j):
                    g = 2 * u + j
                    copy(saT[:, :], ps_turn[:, :], saT_ps, g + 1, saT_sb, proj_ps, g)

                def front_x3T(u, j):
                    g = 2 * u + j
                    copy(x3T[j][:, :], ps_turn[:, :], x3T_ps, g + 1, x3T_sb, up_ps, EC * (g - 1))

                def front_exp(u, j):
                    g = 2 * u + j
                    act.wait_ge(wdiff_ready, g + 1)
                    act.activation(wexp[:, :], wdiff[:, :], ACT.Exp).then_inc(wexp_ready, 1)

                def front_weT(u, j):
                    g = 2 * u + j
                    copy(weT[:, :], ps_turn[0:E, :], weT_ps, g + 1, weT_sb, bias_ps, g)

                def gate(u, j, e, c):
                    n = EC * (2 * u + j) + e * C + c
                    w = e * C + c
                    act.wait_ge(gate_ps, n + 1)
                    when(act, hid_ready, n - 1)
                    act.activation(silu[w % 2][:, :], ps_gate[w % 2][0:CH, :], ACT.Silu, bias=bg_sb[:, w:w + 1])\
                        .then_inc(silu_ready, 1)

                front = {0: [front_saT], 4: [front_x3T], 6: [front_exp], 7: [front_weT]}

                def group(u, j, nxt):
                    for e in range(E):
                        gate(u, j, e, 0)
                        if nxt:
                            for f in front.get(e, []):
                                f(*after(u, j))
                        gate(u, j, e, 1)
                        gate(u, j, e, 2)
                act.wait_ge(weights_in, 16 * NWEIGHTS)
                for e in sorted(front):
                    for f in front[e]:
                        f(0, 0)
                groups(act, group)

            @block.vector
            def _(dve):
                dve.wait_ge(weights_in, 16 * NWEIGHTS)
                dve.wait_ge(consts_made, 4)
                dve.tensor_scalar(cT2[:, :], cT_sb[:, :], -2.0, None, ALU.mult).then_inc(c_squared, 1)
                dve.tensor_tensor(csq_in[:, :], cT_sb[:, :], cT_sb[:, :], ALU.mult).then_inc(c_squared, 1)
                dve.wait_ge(csq_ps, 1)
                dve.tensor_copy(csq[:, :], ps_front[0:1, 0:E]).then_inc(c_ready, 1)

                def statistics(base, rows, stats, mv, var, count):
                    for i in range(B):
                        dve.bn_stats(blk(stats, i, 6), blk(rows, i)).then_inc(count, 1)
                    for i in range(B):
                        wait_alone(dve, count, base + i + 1, passed)
                        dve.bn_aggr(blk(mv, i, 2), blk(stats, i, 6)).then_inc(count, 1)
                    dve.wait_ge(count, base + 2 * B)
                    dve.tensor_scalar(var[:, :], mv[:, :].rearrange("p (i c) -> p i c", c=2)[:, :, 1], EPS, None,
                                      ALU.add).then_inc(count, 1)

                def residual(u, j):
                    g = 2 * u + j
                    dve.wait_ge(proj_ps, g + 1)
                    when(dve, x3_ready, B * g)
                    dve.tensor_tensor(r3[:, :], x_all[:, bass.ds(g * S, S)], ps_front[:, :], ALU.add)\
                        .then_inc(norm3_step, 1)
                    dve.wait_ge(norm3_step, NORM * g + 1)
                    statistics(NORM * g + 1, r3, stats3, mv3, var3, norm3_step)

                def norm3(u, j):
                    g = 2 * u + j
                    dve.wait_ge(rstd3_ready, g + 1)
                    when(dve, acc_begun, g - 1)
                    when(dve, x3T_ps, g - 1)
                    for i in range(B):
                        dve.tensor_scalar(blk(x3[j], i), blk(r3, i), mv3[:, 2 * i:2 * i + 1], rstd3[:, i:i + 1],
                                          ALU.subtract, ALU.mult).then_inc(x3_ready, 1)
                    for i in range(B):
                        dve.wait_ge(x3_ready, B * g + i + 1)
                        when(dve, square_step, B * g + i)
                        dve.scalar_tensor_tensor(out=square[:, :], in0=blk(x3[j], i), scalar=1.0,
                                                 in1=blk(x3[j], i), op0=ALU.mult, op1=ALU.mult,
                                                 accum_out=norm_sq[:, i:i + 1]).then_inc(square_step, 1)

                def square_distances(u, j):
                    g = 2 * u + j
                    dve.wait_ge(dist_ps, g + 1)
                    dve.wait_ge(square_step, B * (g + 1))
                    for i in range(B):
                        dve.tensor_scalar(blk(dist2, i, E), blk(ps_front, i, E), norm_sq[:, i:i + 1], 1e-12,
                                          ALU.add, ALU.max).then_inc(dist2_ready, 1)

                PICK = 4 * B + 5

                def pick(u, j):
                    g = 2 * u + j
                    base = PICK * g
                    wait_alone(dve, dist_ready, g + 1, passed)
                    tops = top[:, :].rearrange("p (i c) -> p i c", c=8)
                    for i in range(B):
                        dve.max(blk(top, i, 8), blk(dist, i, E)).then_inc(pick_step, 1)
                    dve.wait_ge(pick_step, base + B)
                    dve.tensor_tensor(wdiff[:, :], tops[:, :, 1], tops[:, :, 0], ALU.subtract)\
                        .then_inc(wdiff_ready, 1)
                    for i in range(B):
                        dve.max_index(blk(top_idx, i, 8), blk(top, i, 8), blk(dist, i, E)).then_inc(pick_step, 1)
                    dve.wait_ge(pick_step, base + 2 * B)
                    dve.tensor_copy(top_idxf[:, :], top_idx[:, :]).then_inc(pick_step, 1)
                    dve.wait_ge(wexp_ready, g + 1)
                    dve.tensor_scalar(wden[:, :], wexp[:, :], 1.0, None, ALU.add).then_inc(pick_step, 1)
                    dve.wait_ge(pick_step, base + 2 * B + 2)
                    dve.reciprocal(pair[:, 0:B], wden[:, :]).then_inc(pick_step, 1)
                    dve.wait_ge(pick_step, base + 2 * B + 3)
                    dve.tensor_tensor(pair[:, B:2 * B], wexp[:, :], pair[:, 0:B], ALU.mult).then_inc(pick_step, 1)
                    dve.wait_ge(pick_step, base + 2 * B + 4)
                    for rank, spread in ((0, first), (1, second)):
                        for i in range(B):
                            dve.tensor_scalar(blk(spread, i, E), iota[:, :],
                                              top_idxf[:, i * 8 + rank:i * 8 + rank + 1],
                                              pair[:, rank * B + i:rank * B + i + 1], ALU.is_equal, ALU.mult)\
                               .then_inc(pick_step, 1)
                    dve.wait_ge(pick_step, base + 4 * B + 4)
                    when(dve, acc_step, B * E * (g - 1))
                    when(dve, weT_ps, g - 1)
                    dve.tensor_tensor(we[j][:, :], first[:, :], second[:, :], ALU.add).then_inc(we_ready, 1)
                    dve.wait_ge(we_ready, g + 1)
                    dve.sem_inc(pick_step, 1)

                def begin_sum(u, j):
                    g = 2 * u + j
                    dve.wait_ge(bias_ps, g + 1)
                    when(dve, x4_ready, B * (g - 1))
                    dve.tensor_tensor(acc[j][:, :], x3[j][:, :], ps_front[:, :], ALU.add).then_inc(acc_begun, 1)

                def multiply(u, j, e, c):
                    n = EC * (2 * u + j) + e * C + c
                    w = e * C + c
                    dve.wait_ge(up_ps, n + 1)
                    dve.wait_ge(silu_ready, n + 1)
                    when(dve, y_ps, E * (2 * u + j) + e - 1)
                    dve.scalar_tensor_tensor(out=hid[(e % 2) * C + c][:, :], in0=ps_up[w % 2][0:CH, :],
                                             scalar=b1_sb[:, w:w + 1], in1=silu[w % 2][:, :], op0=ALU.add,
                                             op1=ALU.mult).then_inc(hid_ready, 1)

                def add_expert(u, j, e):
                    g = 2 * u + j
                    dve.wait_ge(y_ps, E * g + e + 1)
                    dve.wait_ge(acc_begun, g + 1)
                    for i in range(B):
                        when(dve, acc_step, B * (E * g + e - 1) + i + 1)
                        dve.scalar_tensor_tensor(out=blk(acc[j], i), in0=blk(ps_y[e % 2], i),
                                                 scalar=we[j][:, i * E + e:i * E + e + 1], in1=blk(acc[j], i),
                                                 op0=ALU.mult, op1=ALU.add).then_inc(acc_step, 1)

                def norm4(u, j):
                    g = 2 * u + j
                    dve.wait_ge(acc_step, B * E * (g + 1))
                    statistics(NORM4 * g, acc[j], stats4, mv4, var4, norm4_step)
                    dve.wait_ge(rstd4_ready, g + 1)
                    when(dve, stored, 16 * g)
                    for i in range(B):
                        dve.tensor_scalar(blk(x4, i), blk(acc[j], i), mv4[:, 2 * i:2 * i + 1], rstd4[:, i:i + 1],
                                          ALU.subtract, ALU.mult).then_inc(x4_ready, 1)

                front = {2: [residual], 3: [norm3], 5: [square_distances], 6: [pick], 7: [begin_sum]}

                def group(u, j, nxt):
                    for e in range(E):
                        multiply(u, j, e, 0)
                        if nxt:
                            for f in front.get(e, []):
                                f(*after(u, j))
                        multiply(u, j, e, 1)
                        if e:
                            add_expert(u, j, e - 1)
                        multiply(u, j, e, 2)
                    add_expert(u, j, E - 1)
                    norm4(u, j)
                for e in sorted(front):
                    for f in front[e]:
                        f(0, 0)
                groups(dve, group)


def two_layers(nc, sh, x, xT, wqkv, wproj, bproj, gate_w, gate_b, expert_w, expert_b, wqT, wkT, bq, wv1, bv1,
               wp, bp, cT, wg, bg, w1, b1, w2, b2, out):
    with ExitStack() as ctx:
        def sb(name, shape):
            return ctx.enter_context(nc.sbuf_tensor(name, shape, F32))
        x_all = sb("x_all", [P, sh.tokens])
        sa_all = sb("sa_all", [P, sh.tokens])
        ident = sb("ident", [P, P])
        ones = sb("ones", [1, P])
        with ExitStack() as two_stages:
            xT_all = two_stages.enter_context(nc.sbuf_tensor("xT_all", [P, sh.tokens], F32))
            v_all = two_stages.enter_context(nc.sbuf_tensor("v_all", [P, sh.tiles * H * (DH + 1)], F32))
            layer0(nc, sh, x, xT, wqkv, wproj, bproj, gate_w, gate_b, expert_w, expert_b, wv1, bv1,
                   (x_all, xT_all, v_all, ident, ones))
            attention1(nc, sh, wqT, wkT, bq, (xT_all, v_all, ident), sa_all)
        finish1(nc, sh, wp, bp, cT, wg, bg, w1, b1, w2, b2, (x_all, ident, ones), sa_all, out)


def laid_out(i):
    import numpy as np
    heads = i["L0_attn_Wqkv"].reshape(H, 3, DH, P)
    kqv = i["L1_attn_Wkqv"]
    hidden = i["L1_ffn_Wg"].shape[2]
    chunk = hidden // -(-hidden // P)
    x = i["L0_attn_x"].reshape(-1, P)
    made = {
        "x": x,
        "xT": x.T,
        "wqkv": np.concatenate([heads[:, 0].reshape(P, P), heads[:, 1].reshape(P, P),
                                heads[:, 2].transpose(1, 0, 2).reshape(P, P)], axis=0).T,
        "wproj": i["L0_attn_Wproj"].T,
        "bproj": i["L0_attn_bproj"].reshape(1, P),
        "gate_w": i["L0_ffn_gate_w"].T,
        "gate_b": i["L0_ffn_gate_b"].reshape(1, E),
        "expert_w": i["L0_ffn_expert_w"].transpose(1, 0, 2).reshape(P, E * P),
        "expert_b": i["L0_ffn_expert_b"],
        "wqT": kqv[:, :, P:2 * P].transpose(2, 0, 1).reshape(P, H * P),
        "wkT": kqv[:, :, 0:P].transpose(2, 0, 1).reshape(P, H * P),
        "bq": i["L1_attn_bkqv"][:, P:2 * P].T,
        "wv1": kqv[:, :, 2 * P:].transpose(1, 0, 2).reshape(P, P),
        "bv1": i["L1_attn_bkqv"][:, 2 * P:].reshape(1, P),
        "wp": i["L1_attn_Wp"],
        "bp": i["L1_attn_bp"].reshape(1, P),
        "cT": i["L1_ffn_centroid"].T,
        "wg": i["L1_ffn_Wg"].transpose(1, 0, 2).reshape(P, E * hidden),
        "bg": i["L1_ffn_bg"].reshape(-1, chunk).T,
        "w1": i["L1_ffn_W1"].transpose(1, 0, 2).reshape(P, E * hidden),
        "b1": i["L1_ffn_b1"].reshape(-1, chunk).T,
        "w2": i["L1_ffn_W2"].reshape(-1, chunk, P).transpose(1, 0, 2).reshape(chunk, -1),
        "b2": i["L1_ffn_b2"],
    }
    return {name: np.ascontiguousarray(a) for name, a in made.items()}


def kernel(**inputs):
    import numpy as np
    import concourse.bacc as bacc
    from concourse import mybir as _mybir
    from concourse.bass_utils import run_bass_kernel_spmd

    inputs = {name: np.asarray(a) for name, a in inputs.items()}
    nc = bacc.Bacc("TRN2", target_bir_lowering=False, num_devices=1)
    batch, seq, _ = inputs["L0_attn_x"].shape
    sh = Shapes(batch * seq, seq, inputs["L1_ffn_Wg"].shape[2])
    arrays, args = {}, []
    for name, a in laid_out(inputs).items():
        arrays[f"in_{name}"] = a
        args.append(nc.dram_tensor(f"in_{name}", a.shape, _mybir.dt.from_np(a.dtype), kind="ExternalInput").ap())
    out = nc.dram_tensor("out_x", (batch * seq, P), _mybir.dt.float32, kind="ExternalOutput").ap()
    two_layers(nc, sh, *args, out)
    r = run_bass_kernel_spmd(nc, [arrays], core_ids=[0])
    return r.results[0]["out_x"].reshape(batch, seq, P)
```

```python
from contextlib import ExitStack

import concourse.bass as bass
from concourse import mybir

ALU = mybir.AluOpType
ACT = mybir.ActivationFunctionType
F32 = mybir.dt.float32
BF16 = mybir.dt.bfloat16
U32 = mybir.dt.uint32
I32 = mybir.dt.int32
AX_X = mybir.AxisListType.X

P = 128
H = 16
DH = P // H
E = 8
EPS = 1e-5
MASKED = -1e30


def when(eng, semaphore, count):
    if not isinstance(count, int) or count > 0:
        eng.wait_ge(semaphore, count)


def wait_alone(eng, semaphore, count, passed):
    eng.wait_ge(semaphore, count)
    eng.sem_inc(passed, 1)


class Shapes:

    def __init__(self, tokens, seq, hidden):
        self.tokens, self.seq, self.hidden = tokens, seq, hidden
        self.tiles = tokens // P
        self.blocks = seq // P
        self.batches = tokens // seq
        self.chunks = -(-hidden // P)
        self.chunk = hidden // self.chunks
        self.list_rows = tokens + P
        self.listed_tiles = 2 * self.tiles + E
        assert self.chunk * self.chunks == hidden and self.blocks == 4


def layer0(nc, sh, x, xT_in, wqkv, wproj, bproj, gate_w, gate_b, expert_w, expert_b, wv1, bv1,
           keep):
    x_all, xT_all, v_all, ident, ones = keep
    NP = sh.tiles // 2
    HH = H * H
    sems = []
    with ExitStack() as ctx:
        def sb(name, shape, dt=F32):
            return ctx.enter_context(nc.sbuf_tensor(name, shape, dt))

        def pb(name):
            return ctx.enter_context(nc.psum_tensor(name, [P, 4 * P], F32))

        def sem(name):
            sems.append(nc.alloc_semaphore(name))
            return sems[-1]

        wqkv_sb = sb("wqkv_sb", [P, 3 * P])
        wproj_sb = sb("wproj_sb", [P, P])
        bproj_sb = sb("bproj_sb", [1, P])
        gatew_sb = sb("gatew_sb", [P, E])
        gateb_sb = sb("gateb_sb", [1, E])
        expw_sb = sb("expw_sb", [P, E * P])
        expb_sb = sb("expb_sb", [E, P])
        wv1_sb = sb("wv1_sb", [P, P])
        bv1_sb = sb("bv1_sb", [1, P])
        iota = sb("iota", [P, E])
        minus_half = sb("minus_half", [P, 2])

        xT = [sb(f"xT{j}", [P, 2 * P]) for j in range(2)]
        qkv = [sb(f"qkv{j}", [P, 2 * 3 * P]) for j in range(2)]
        qk_prod = sb("qk_prod", [P, 2 * HH * DH])
        pv_prod = sb("pv_prod", [P, 2 * HH * DH])
        scores = sb("scores", [P, 2 * HH])
        score_max = sb("score_max", [P, 2 * H])
        shifted = sb("shifted", [P, 2 * HH])
        probs = [sb(f"probs{j}", [P, 2 * HH]) for j in range(2)]
        prob_sum = sb("prob_sum", [P, 2 * H])
        prob_rec = [sb(f"prob_rec{j}", [P, 2 * H]) for j in range(2)]
        pv_sum = sb("pv_sum", [P, 2 * P])
        attn = sb("attn", [P, 2 * P])
        attnT = sb("attnT", [P, 2 * P])
        r1 = sb("r1", [P, 2 * P])
        stats1, mv1, var1, rstd1 = sb("stats1", [P, 12]), sb("mv1", [P, 4]), sb("var1", [P, 2]), sb("rstd1", [P, 2])
        x1 = [sb(f"x1_{j}", [P, 2 * P]) for j in range(2)]
        x1T = sb("x1T", [P, 2 * P])
        top, top_idx, top_idxf = sb("top", [P, 16]), sb("top_idx", [P, 16], U32), sb("top_idxf", [P, 16])
        gdiff, gexp, gden, gw = sb("gdiff", [P, 2]), sb("gexp", [P, 2]), sb("gden", [P, 2]), sb("gw", [P, 4])
        gate1, gate2, gates = sb("gate1", [P, 2 * E]), sb("gate2", [P, 2 * E]), sb("gates", [P, 2 * E])
        gatesT = sb("gatesT", [E, 2 * P])
        gated = [sb(f"gated{a}", [P, E * P]) for a in range(2)]
        sum4, sum2, sum1 = sb("sum4", [P, 4 * P]), sb("sum2", [P, 2 * P]), sb("sum1", [P, P])
        acc = sb("acc", [P, 2 * P])
        r2 = sb("r2", [P, 2 * P])
        stats2, mv2, var2, rstd2 = sb("stats2", [P, 12]), sb("mv2", [P, 4]), sb("var2", [P, 2]), sb("rstd2", [P, 2])
        x2 = [sb(f"x2_{j}", [P, 2 * P]) for j in range(2)]
        x2T = [sb(f"x2T{j}", [P, 2 * P]) for j in range(2)]

        ps_qkv = [pb(f"ps_qkv{a}") for a in range(2)]
        ps_turn = pb("ps_turn0")
        ps_keep = pb("ps_keep")
        ps_front = pb("ps_front0")
        ps_bias = pb("ps_bias")
        ps_y = [pb(f"ps_y{i}") for i in range(2)]
        ps_oT, ps_x1T, ps_gT = ps_turn[:, 0:2 * P], ps_turn[:, 2 * P:4 * P], ps_turn[0:E, 0:2 * P]
        ps_x2T, ps_v = ps_keep[:, 0:2 * P], ps_keep[:, 2 * P:4 * P]
        ps_proj, ps_logits = ps_front[:, 0:2 * P], ps_front[:, 2 * P:2 * P + 2 * E]
        ps_eb = ps_bias[:, 0:2 * P]

        consts_made, passed, sp_passed = sem("consts_made"), sem("passed"), sem("sp_passed")
        ident_zeroed = sem("ident_zeroed")
        weights_in = sem("weights_in")
        x_in = [sem(f"x_in{j}") for j in range(2)]
        xT_loaded = [sem(f"xT_loaded{j}") for j in range(2)]
        x2_kept = [sem(f"x2_kept{j}") for j in range(2)]
        x2T_kept = [sem(f"x2T_kept{j}") for j in range(2)]
        qkv_ps, qkv_sb, qk_multiplied = sem("qkv_ps"), sem("qkv_sb"), sem("qk_multiplied")
        pv_multiplied, pv_summed, experts_summed = sem("pv_multiplied"), sem("pv_summed"), sem("experts_summed")
        x1_ready, x2_ready, v_sb = sem("x1_ready"), sem("x2_ready"), sem("v_sb")
        experts_ps, gated_ready = sem("experts_ps"), sem("gated_ready")
        scores_summed, max_found, scores_shifted = sem("scores_summed"), sem("max_found"), sem("scores_shifted")
        probs_ready, probs_summed, recips_ready = sem("probs_ready"), sem("probs_summed"), sem("recips_ready")
        attn_ready, oT_ps, oT_sb, proj_ps = sem("attn_ready"), sem("oT_ps"), sem("oT_sb"), sem("proj_ps")
        rstd1_ready, x1T_ps, x1T_sb, logits_ps = sem("rstd1_ready"), sem("x1T_ps"), sem("x1T_sb"), sem("logits_ps")
        gate_diff_ready, gate_exp_ready, gates_ready = sem("gate_diff_ready"), sem("gate_exp_ready"), sem("gates_ready")
        gT_ps, gT_sb, expert_bias_ps, rstd2_ready = sem("gT_ps"), sem("gT_sb"), sem("expert_bias_ps"), sem("rstd2_ready")
        x2T_ps, x2T_sb, v_ps = sem("x2T_ps"), sem("x2T_sb"), sem("v_ps")
        norm1_step, norm2_step, gate_step, sum_step = (
            sem("norm1_step"), sem("norm2_step"), sem("gate_step"), sem("sum_step"))

        NWEIGHTS = 9
        NORM_STEPS = 6
        GATE_STEPS = 12
        SUM_STEPS = 3

        def steps(eng, step):
            def one(s):
                step(s // 2, s % 2, (s + 1 < NP, s < NP, 1 <= s <= NP, 2 <= s))
            for s in range(5):
                one(s)
            with eng.Fori(2, NP // 2 - 1) as u:
                step(u, 1, (True, True, True, True))
                step(u + 1, 0, (True, True, True, True))
            for s in range(NP - 1, NP + 2):
                one(s)

        def before(u, j, k):
            return u + (j - k) // 2, (j - k) % 2

        x_tiles = x.rearrange("(t p) d -> p t d", p=P)
        x_sb = x_all[:, :].rearrange("p (t d) -> p t d", d=P)
        v_heads = v_all[:, :].rearrange("p (b h k c) -> p b h k c", h=H, k=sh.blocks, c=DH + 1)

        def tile(t, a, n=P):
            return t[:, a * n:(a + 1) * n]

        with nc.Block() as block:

            @block.sync
            def _(sp):
                def load(u, j):
                    s = 2 * u + j
                    when(sp, x_in[j], 16 * u)
                    sp.sem_inc(sp_passed, 1)
                    sp.dma_start(x_sb[:, bass.ds(2 * s, 2), :], x_tiles[:, bass.ds(2 * s, 2), :])\
                        .then_inc(x_in[j], 16)
                    when(sp, qkv_ps, 2 * (s - 1))
                    sp.sem_inc(sp_passed, 1)
                    sp.dma_start(xT[j][:, :], xT_in[:, bass.ds(s * 2 * P, 2 * P)]).then_inc(xT_loaded[j], 16)

                def keep_x2(u, j):
                    s = 2 * u + j
                    wait_alone(sp, x2_ready, 2 * (s + 1), sp_passed)
                    sp.dma_start(x_sb[:, bass.ds(2 * s, 2), :], x2[j][:, :].rearrange("p (a d) -> p a d", d=P))\
                        .then_inc(x2_kept[j], 16)
                    wait_alone(sp, x2T_sb, s + 1, sp_passed)
                    sp.dma_start(xT_all[:, bass.ds(s * 2 * P, 2 * P)], x2T[j][:, :]).then_inc(x2T_kept[j], 16)

                def step(u, j, part):
                    if part[0]:
                        load(*before(u, j, -1))
                    if part[3]:
                        keep_x2(*before(u, j, 2))
                sp.dma_start(wqkv_sb[:, :], wqkv).then_inc(weights_in, 16)
                load(0, 0)
                for dst, src in ((wproj_sb, wproj), (bproj_sb, bproj), (gatew_sb, gate_w),
                                 (gateb_sb, gate_b), (expw_sb, expert_w), (expb_sb, expert_b),
                                 (wv1_sb, wv1), (bv1_sb, bv1)):
                    sp.dma_start(dst[:, :], src).then_inc(weights_in, 16)
                steps(sp, step)
                for j in range(2):
                    sp.wait_ge(x2_kept[j], 16 * NP // 2)
                    sp.wait_ge(x2T_kept[j], 16 * NP // 2)

            @block.gpsimd
            def _(pool):
                pool.memset(v_all[:, :], 1.0).then_inc(consts_made, 1)
                pool.memset(ones[:, :], 1.0).then_inc(consts_made, 1)
                pool.memset(minus_half[:, :], -0.5).then_inc(consts_made, 1)
                pool.iota(iota[:, :], pattern=[[1, E]], base=0, channel_multiplier=0,
                          allow_small_or_imprecise_dtypes=True).then_inc(consts_made, 1)
                pool.memset(ident[:, :], 0.0).then_inc(ident_zeroed, 1)
                pool.wait_ge(ident_zeroed, 1)
                pool.affine_select(out=ident[:, :], in_=ident[:, :], compare_op=ALU.not_equal, fill=1.0,
                                   base=0, pattern=[[-1, P]], channel_multiplier=1).then_inc(consts_made, 1)
                pool.wait_ge(consts_made, 5)

                def inverse_deviation(u, j, step_sem, var, rstd, done):
                    s = 2 * u + j
                    pool.wait_ge(step_sem, NORM_STEPS * (s + 1))
                    pool.tensor_tensor(rstd[:, :], var[:, :], minus_half[:, :], ALU.pow).then_inc(done, 1)

                def pv_products(u, j):
                    s = 2 * u + j
                    pool.wait_ge(probs_ready, s + 1)
                    for a in range(2):
                        when(pool, pv_summed, 2 * (s - 1) + a + 1)
                        pool.tensor_tensor(
                            tile(pv_prod, a, HH * DH).rearrange("p (h d g) -> p h d g", h=H, d=DH),
                            tile(probs[j], a, HH).rearrange("p (h g) -> p h g", h=H).unsqueeze(2)
                            .to_broadcast([P, H, DH, H]),
                            qkv[j][:, (3 * a + 2) * P:(3 * a + 3) * P].rearrange("p (d g) -> p d g", d=DH)
                            .unsqueeze(1).to_broadcast([P, H, DH, H]), ALU.mult).then_inc(pv_multiplied, 1)

                def sum_experts(u, j):
                    s = 2 * u + j
                    when(pool, norm2_step, NORM_STEPS * (s - 1) + 1)
                    for a in range(2):
                        n = 2 * s + a
                        base = SUM_STEPS * n
                        pool.wait_ge(gated_ready, 2 * n + 2)
                        when(pool, experts_summed, n)
                        pool.tensor_tensor(sum4[:, :], gated[a][:, 0:4 * P], gated[a][:, 4 * P:8 * P],
                                           ALU.add).then_inc(sum_step, 1)
                        pool.wait_ge(sum_step, base + 1)
                        pool.tensor_tensor(sum2[:, :], sum4[:, 0:2 * P], sum4[:, 2 * P:4 * P],
                                           ALU.add).then_inc(sum_step, 1)
                        pool.wait_ge(sum_step, base + 2)
                        pool.tensor_tensor(sum1[:, :], sum2[:, 0:P], sum2[:, P:2 * P],
                                           ALU.add).then_inc(sum_step, 1)
                        pool.wait_ge(sum_step, base + 3)
                        pool.tensor_tensor(tile(acc, a), sum1[:, :], tile(x1[j], a), ALU.add)\
                            .then_inc(experts_summed, 1)

                def step(u, j, part):
                    if part[2]:
                        inverse_deviation(*before(u, j, 1), norm1_step, var1, rstd1, rstd1_ready)
                    if part[3]:
                        inverse_deviation(*before(u, j, 2), norm2_step, var2, rstd2, rstd2_ready)
                    if part[1]:
                        pv_products(u, j)
                    if part[2]:
                        sum_experts(*before(u, j, 1))
                steps(pool, step)

            @block.tensor
            def _(pe):
                pe.wait_ge(consts_made, 5)
                pe.wait_ge(weights_in, 16 * NWEIGHTS)

                def qkv_products(u, j):
                    s = 2 * u + j
                    pe.wait_ge(xT_loaded[j], 16 * (u + 1))
                    for a in range(2):
                        when(pe, qkv_sb, 2 * (s - 1) + a + 1)
                        pe.matmul(ps_qkv[a][:, 0:3 * P], tile(xT[j], a), wqkv_sb[:, :], start=True,
                                  stop=True).then_inc(qkv_ps, 1)

                def attention_out(u, j):
                    s = 2 * u + j
                    pe.wait_ge(attn_ready, s + 1)
                    when(pe, gT_sb, s)
                    for a in range(2):
                        mm = pe.transpose(tile(ps_oT, a), tile(attn, a), ident[:, :])
                    mm.then_inc(oT_ps, 1)
                    pe.wait_ge(oT_sb, s + 1)
                    when(pe, gates_ready, s)
                    for a in range(2):
                        pe.matmul(tile(ps_proj, a), tile(attnT, a), wproj_sb[:, :], start=True, stop=False)
                        mm = pe.matmul(tile(ps_proj, a), ones[0:1, 0:P], bproj_sb[:, :], start=False, stop=True)
                    mm.then_inc(proj_ps, 1)

                def four_experts(s, a, half):
                    when(pe, gated_ready, 4 * s + 2 * a + half - 1)
                    pe.matmul(ps_y[half][:, :], tile(x1T, a), expw_sb[:, half * 4 * P:(half + 1) * 4 * P],
                              start=True, stop=True).then_inc(experts_ps, 1)

                def experts(u, j):
                    s = 2 * u + j
                    pe.wait_ge(x1_ready, 2 * (s + 1))
                    for a in range(2):
                        mm = pe.transpose(tile(ps_x1T, a), tile(x1[j], a), ident[:, :])
                    mm.then_inc(x1T_ps, 1)
                    pe.wait_ge(x1T_sb, s + 1)
                    for a in range(2):
                        pe.matmul(tile(ps_logits, a, E), tile(x1T, a), gatew_sb[:, :], start=True, stop=False)
                        mm = pe.matmul(tile(ps_logits, a, E), ones[0:1, 0:P], gateb_sb[:, :], start=False, stop=True)
                    mm.then_inc(logits_ps, 1)
                    four_experts(s, 0, 0)
                    four_experts(s, 0, 1)
                    pe.wait_ge(gates_ready, s + 1)
                    for a in range(2):
                        mm = pe.transpose(tile(ps_gT, a), tile(gates, a, E), ident[:, :])
                    mm.then_inc(gT_ps, 1)
                    four_experts(s, 1, 0)
                    four_experts(s, 1, 1)
                    pe.wait_ge(gT_sb, s + 1)
                    when(pe, norm2_step, NORM_STEPS * (s - 1) + 1)
                    for a in range(2):
                        mm = pe.matmul(tile(ps_eb, a), tile(gatesT, a), expb_sb[:, :], start=True, stop=True)
                    mm.then_inc(expert_bias_ps, 1)

                def values(u, j):
                    s = 2 * u + j
                    pe.wait_ge(x2_ready, 2 * (s + 1))
                    when(pe, v_sb, 2 * s)
                    for a in range(2):
                        mm = pe.transpose(tile(ps_x2T, a), tile(x2[j], a), ident[:, :])
                    mm.then_inc(x2T_ps, 1)
                    pe.wait_ge(x2T_sb, s + 1)
                    for a in range(2):
                        pe.matmul(tile(ps_v, a), tile(x2T[j], a), wv1_sb[:, :], start=True, stop=False)
                        mm = pe.matmul(tile(ps_v, a), ones[0:1, 0:P], bv1_sb[:, :], start=False, stop=True)
                    mm.then_inc(v_ps, 1)

                def step(u, j, part):
                    if part[0]:
                        qkv_products(*before(u, j, -1))
                    if part[2]:
                        attention_out(*before(u, j, 1))
                        experts(*before(u, j, 1))
                    if part[3]:
                        values(*before(u, j, 2))
                qkv_products(0, 0)
                steps(pe, step)

            @block.scalar
            def _(act):
                act.wait_ge(consts_made, 5)

                def copy_qkv(u, j):
                    s = 2 * u + j
                    when(act, qk_multiplied, 2 * (s - 1))
                    when(act, pv_multiplied, 2 * (s - 1))
                    for a in range(2):
                        act.wait_ge(qkv_ps, 2 * s + a + 1)
                        act.copy(tile(qkv[j], a, 3 * P), ps_qkv[a][:, 0:3 * P]).then_inc(qkv_sb, 1)

                def copy_oT(u, j):
                    s = 2 * u + j
                    act.wait_ge(oT_ps, s + 1)
                    when(act, proj_ps, s)
                    act.copy(attnT[:, :], ps_oT).then_inc(oT_sb, 1)

                def exponentials(u, j):
                    s = 2 * u + j
                    act.wait_ge(scores_shifted, s + 1)
                    when(act, pv_multiplied, 2 * (s - 1))
                    when(act, probs_summed, s - 1)
                    act.activation(probs[j][:, :], shifted[:, :], ACT.Exp, scale=0.125).then_inc(probs_ready, 1)

                def copy_x1T(u, j):
                    s = 2 * u + j
                    act.wait_ge(x1T_ps, s + 1)
                    when(act, experts_ps, 4 * s)
                    act.copy(x1T[:, :], ps_x1T).then_inc(x1T_sb, 1)

                def gate_exp(u, j):
                    s = 2 * u + j
                    act.wait_ge(gate_diff_ready, s + 1)
                    act.activation(gexp[:, :], gdiff[:, :], ACT.Exp).then_inc(gate_exp_ready, 1)

                def apply_gates(u, j, a):
                    s = 2 * u + j
                    act.wait_ge(gates_ready, s + 1)
                    when(act, sum_step, SUM_STEPS * (2 * (s - 1) + a) + 1)
                    for half in range(2):
                        act.wait_ge(experts_ps, 4 * s + 2 * a + half + 1)
                        for e in range(4 * half, 4 * half + 4):
                            last = act.activation(tile(gated[a], e), tile(ps_y[half], e % 4), ACT.Copy,
                                                  scale=gates[:, a * E + e:a * E + e + 1])
                        last.then_inc(gated_ready, 1)

                def copy_gT(u, j):
                    s = 2 * u + j
                    act.wait_ge(gT_ps, s + 1)
                    when(act, expert_bias_ps, s)
                    act.copy(gatesT[:, :], ps_gT).then_inc(gT_sb, 1)

                def copy_x2T(u, j):
                    s = 2 * u + j
                    act.wait_ge(x2T_ps, s + 1)
                    when(act, v_ps, s - 1)
                    when(act, x2T_kept[j], 16 * u)
                    act.copy(x2T[j][:, :], ps_x2T).then_inc(x2T_sb, 1)

                def copy_v(u, j):
                    s = 2 * u + j
                    act.wait_ge(v_ps, s + 1)
                    for a in range(2):
                        act.copy(v_heads[:, bass.ds(u, 1), :, 2 * j + a:2 * j + a + 1, 0:DH]
                                 .rearrange("p b h k c -> p (b h k) c"),
                                 tile(ps_v, a).rearrange("p (h c) -> p h c", h=H)).then_inc(v_sb, 1)

                def step(u, j, part):
                    if part[0]:
                        copy_qkv(*before(u, j, -1))
                    if part[2]:
                        copy_oT(*before(u, j, 1))
                    if part[1]:
                        exponentials(u, j)
                    if part[2]:
                        copy_x1T(*before(u, j, 1))
                        gate_exp(*before(u, j, 1))
                        apply_gates(*before(u, j, 1), 0)
                        copy_gT(*before(u, j, 1))
                        apply_gates(*before(u, j, 1), 1)
                    if part[3]:
                        copy_x2T(*before(u, j, 2))
                        copy_v(*before(u, j, 2))
                copy_qkv(0, 0)
                steps(act, step)

            @block.vector
            def _(dve):
                dve.wait_ge(consts_made, 5)

                def by_head(t, n=H):
                    return t[:, :].rearrange("p (h g) -> p h g", g=n)

                def qk_products(u, j):
                    s = 2 * u + j
                    when(dve, scores_summed, s)
                    for a in range(2):
                        dve.wait_ge(qkv_sb, 2 * s + a + 1)
                        dve.tensor_tensor(
                            tile(qk_prod, a, HH * DH).rearrange("p (h g d) -> p h g d", h=H, g=H),
                            qkv[j][:, 3 * a * P:(3 * a + 1) * P].rearrange("p (h d) -> p h d", h=H).unsqueeze(2)
                            .to_broadcast([P, H, H, DH]),
                            qkv[j][:, (3 * a + 1) * P:(3 * a + 2) * P].rearrange("p (g d) -> p g d", g=H)
                            .unsqueeze(1).to_broadcast([P, H, H, DH]), ALU.mult).then_inc(qk_multiplied, 1)

                def qk_sums(u, j):
                    s = 2 * u + j
                    dve.wait_ge(qk_multiplied, 2 * (s + 1))
                    when(dve, scores_shifted, s)
                    dve.tensor_reduce(scores[:, :], by_head(qk_prod, DH), AX_X, ALU.add).then_inc(scores_summed, 1)

                def find_max(u, j):
                    s = 2 * u + j
                    dve.wait_ge(scores_summed, s + 1)
                    dve.tensor_reduce(score_max[:, :], by_head(scores), AX_X, ALU.max).then_inc(max_found, 1)

                def shift_scores(u, j):
                    s = 2 * u + j
                    dve.wait_ge(max_found, s + 1)
                    when(dve, probs_ready, s)
                    dve.tensor_tensor(by_head(shifted), by_head(scores),
                                      score_max[:, :].unsqueeze(2).to_broadcast([P, 2 * H, H]),
                                      ALU.subtract).then_inc(scores_shifted, 1)

                def prob_sums(u, j):
                    s = 2 * u + j
                    dve.wait_ge(probs_ready, s + 1)
                    when(dve, recips_ready, s)
                    dve.tensor_reduce(prob_sum[:, :], by_head(probs[j]), AX_X, ALU.add).then_inc(probs_summed, 1)

                def prob_recips(u, j):
                    s = 2 * u + j
                    dve.wait_ge(probs_summed, s + 1)
                    when(dve, attn_ready, s - 1)
                    dve.reciprocal(prob_rec[j][:, :], prob_sum[:, :]).then_inc(recips_ready, 1)

                def pv_sums(u, j):
                    s = 2 * u + j
                    when(dve, attn_ready, s)
                    for a in range(2):
                        dve.wait_ge(pv_multiplied, 2 * s + a + 1)
                        dve.tensor_reduce(tile(pv_sum, a), tile(pv_prod, a, HH * DH)
                                          .rearrange("p (s g) -> p s g", g=H), AX_X, ALU.add)\
                           .then_inc(pv_summed, 1)

                def normalise(u, j):
                    s = 2 * u + j
                    dve.wait_ge(pv_summed, 2 * (s + 1))
                    dve.wait_ge(recips_ready, s + 1)
                    when(dve, oT_ps, s)
                    dve.tensor_tensor(by_head(attn, DH), by_head(pv_sum, DH),
                                      prob_rec[j][:, :].unsqueeze(2).to_broadcast([P, 2 * H, DH]),
                                      ALU.mult).then_inc(attn_ready, 1)

                def statistics(s, rows, stats, mv, var, count):
                    base = NORM_STEPS * s
                    dve.wait_ge(count, base + 1)
                    for a in range(2):
                        dve.bn_stats(tile(stats, a, 6), tile(rows, a)).then_inc(count, 1)
                    for a in range(2):
                        wait_alone(dve, count, base + 2 + a, passed)
                        dve.bn_aggr(tile(mv, a, 2), tile(stats, a, 6)).then_inc(count, 1)
                    dve.wait_ge(count, base + 5)
                    dve.tensor_scalar(var[:, :], mv[:, :].rearrange("p (a c) -> p a c", c=2)[:, :, 1], EPS, None,
                                      ALU.add).then_inc(count, 1)

                def residual1(u, j):
                    s = 2 * u + j
                    dve.wait_ge(x_in[j], 16 * (u + 1))
                    dve.wait_ge(proj_ps, s + 1)
                    when(dve, x1_ready, 2 * s)
                    dve.tensor_tensor(r1[:, :].rearrange("p (a d) -> p a d", d=P), x_sb[:, bass.ds(2 * s, 2), :],
                                      ps_proj.rearrange("p (a d) -> p a d", d=P), ALU.add).then_inc(norm1_step, 1)
                    statistics(s, r1, stats1, mv1, var1, norm1_step)

                def norm1(u, j):
                    s = 2 * u + j
                    dve.wait_ge(rstd1_ready, s + 1)
                    when(dve, x1T_ps, s - 1)
                    when(dve, experts_summed, 2 * (s - 1))
                    for a in range(2):
                        dve.tensor_scalar(tile(x1[j], a), tile(r1, a), mv1[:, 2 * a:2 * a + 1],
                                          rstd1[:, a:a + 1], ALU.subtract, ALU.mult).then_inc(x1_ready, 1)

                def gate(u, j):
                    s = 2 * u + j
                    base = GATE_STEPS * s
                    tops = top[:, :].rearrange("p (a c) -> p a c", c=8)
                    dve.wait_ge(logits_ps, s + 1)
                    when(dve, gates_ready, s)
                    dve.sem_inc(passed, 1)
                    for a in range(2):
                        dve.max(tile(top, a, 8), tile(ps_logits, a, E)).then_inc(gate_step, 1)
                    dve.wait_ge(gate_step, base + 2)
                    dve.tensor_tensor(gdiff[:, :], tops[:, :, 1], tops[:, :, 0], ALU.subtract)\
                        .then_inc(gate_diff_ready, 1)
                    for a in range(2):
                        dve.max_index(tile(top_idx, a, 8), tile(top, a, 8), tile(ps_logits, a, E))\
                           .then_inc(gate_step, 1)
                    dve.wait_ge(gate_step, base + 4)
                    dve.tensor_copy(top_idxf[:, :], top_idx[:, :]).then_inc(gate_step, 1)
                    dve.wait_ge(gate_exp_ready, s + 1)
                    dve.tensor_scalar(gden[:, :], gexp[:, :], 1.0, None, ALU.add).then_inc(gate_step, 1)
                    dve.wait_ge(gate_step, base + 6)
                    dve.reciprocal(gw[:, 0:2], gden[:, :]).then_inc(gate_step, 1)
                    dve.wait_ge(gate_step, base + 7)
                    dve.tensor_tensor(gw[:, 2:4], gexp[:, :], gw[:, 0:2], ALU.mult).then_inc(gate_step, 1)
                    for rank, spread in ((0, gate1), (1, gate2)):
                        if rank == 1:
                            dve.wait_ge(gate_step, base + 8)
                        for a in range(2):
                            dve.tensor_scalar(tile(spread, a, E), iota[:, :],
                                              top_idxf[:, 8 * a + rank:8 * a + rank + 1],
                                              gw[:, 2 * rank + a:2 * rank + a + 1], ALU.is_equal, ALU.mult)\
                               .then_inc(gate_step, 1)
                    dve.wait_ge(gate_step, base + 12)
                    when(dve, gT_ps, s)
                    when(dve, gated_ready, 4 * s)
                    dve.tensor_tensor(gates[:, :], gate1[:, :], gate2[:, :], ALU.add).then_inc(gates_ready, 1)

                def residual2(u, j):
                    s = 2 * u + j
                    dve.wait_ge(experts_summed, 2 * (s + 1))
                    dve.wait_ge(expert_bias_ps, s + 1)
                    when(dve, x2_ready, 2 * s)
                    dve.tensor_tensor(r2[:, :], acc[:, :], ps_eb, ALU.add).then_inc(norm2_step, 1)
                    statistics(s, r2, stats2, mv2, var2, norm2_step)

                def norm2(u, j):
                    s = 2 * u + j
                    dve.wait_ge(rstd2_ready, s + 1)
                    when(dve, x2T_ps, s - 1)
                    when(dve, x2_kept[j], 16 * u)
                    for a in range(2):
                        dve.tensor_scalar(tile(x2[j], a), tile(r2, a), mv2[:, 2 * a:2 * a + 1],
                                          rstd2[:, a:a + 1], ALU.subtract, ALU.mult).then_inc(x2_ready, 1)

                def step(u, j, part):
                    if part[1]:
                        qk_products(u, j)
                    if part[2]:
                        pv_sums(*before(u, j, 1))
                        normalise(*before(u, j, 1))
                    if part[1]:
                        qk_sums(u, j)
                    if part[2]:
                        residual1(*before(u, j, 1))
                    if part[1]:
                        find_max(u, j)
                    if part[3]:
                        residual2(*before(u, j, 2))
                    if part[1]:
                        shift_scores(u, j)
                    if part[2]:
                        norm1(*before(u, j, 1))
                    if part[1]:
                        prob_sums(u, j)
                    if part[3]:
                        norm2(*before(u, j, 2))
                    if part[1]:
                        prob_recips(u, j)
                    if part[2]:
                        gate(*before(u, j, 1))
                steps(dve, step)

    nc.clear_and_free_semaphores(sems)
    nc.all_engine_barrier()


def attention1(nc, sh, wqT, wkT, bq, keep, sa_all):
    xT_all, v_all, ident = keep
    S, B = sh.seq, sh.blocks
    NK = sh.batches * H
    PV = DH + 1
    SCALE = float(P) ** -0.5
    with ExitStack() as ctx:
        def sb(name, shape, dt=F32):
            return ctx.enter_context(nc.sbuf_tensor(name, shape, dt))

        def sem(name):
            return ctx.enter_context(nc.semaphore(name))

        wq = sb("wq_sb", [P, H * P])
        wk = sb("wk_sb", [P, H * P])
        bq_sb = sb("bq_sb", [P, H])
        m_all = sb("m_all", [P, H * P])
        mb_all = sb("mb_all", [P, H])
        m_head = [sb(f"m_head{j}", [P, P]) for j in range(2)]
        ident16 = sb("ident16", [P, P], BF16)
        mask16 = sb("mask16", [P, P], BF16)
        qm = [sb(f"qm{j}", [P, S]) for j in range(2)]
        neg_max = sb("neg_max", [P, B])
        probs = [sb(f"p{i}", [P, (i + 1) * P]) for i in range(B)]
        probsT = [sb(f"pT{i}", [P, (i + 1) * P]) for i in range(B)]
        recip = sb("recip", [P, B])

        ps_s = [ctx.enter_context(nc.psum_tensor(f"ps_s{i}", [P, S], F32)) for i in range(B)]
        ps_t = [ctx.enter_context(nc.psum_tensor(f"ps_t{i}", [P, S], F32)) for i in range(2)]
        ps_qm = ctx.enter_context(nc.psum_tensor("ps_qm", [P, S], F32))
        ps_o = ctx.enter_context(nc.psum_tensor("ps_o", [P, S], F32))
        out_ps = ps_o[:, 0:B * PV].rearrange("p (i c) -> p i c", c=PV)

        weights_in = sem("b_weights_in")
        consts_zeroed, consts_made = sem("b_consts_zeroed"), sem("b_consts_made")
        m_ps, m_sb = sem("m_ps"), sem("m_sb")
        mb_ps, mb_sb = sem("mb_ps"), sem("mb_sb")
        m_head_ready = sem("m_head_ready")
        qm_ps, qm_sb = sem("qm_ps"), sem("qm_sb")
        scores_ps = [sem(f"scores_ps{i}") for i in range(B)]
        max_ready = [sem(f"max_ready{i}") for i in range(B)]
        probs_ready = [sem(f"probs_ready{i}") for i in range(B)]
        pT_ps = [sem(f"pT_ps{i}") for i in range(B)]
        pT_sb = [sem(f"pT_sb{i}") for i in range(B)]
        out_block = [sem(f"out_block{i}") for i in range(B)]
        recips_ready, out_ready = sem("b_recips_ready"), sem("out_ready")

        def steps(step):
            def one(k):
                step(k // 2, k % 2, k + 1 < NK, k >= 1, k < NK)
            def run(eng):
                one(0)
                one(1)
                with eng.Fori(1, NK // 2 - 1) as u:
                    for j in range(2):
                        step(u, j, True, True, True)
                for k in range(NK - 2, NK + 1):
                    one(k)
            return run

        def before(u, j, k):
            return u + (j - k) // 2, (j - k) % 2

        sa_steps = sa_all[:, :].rearrange("p (k i c) -> p k i c", i=B, c=DH)

        def sequence(u):
            return u // (H // 2)

        with nc.Block() as block:

            @block.sync
            def _(sp):
                sp.dma_start(wq[:, :], wqT).then_inc(weights_in, 16)
                sp.dma_start(wk[:, :], wkT).then_inc(weights_in, 16)
                sp.dma_start(bq_sb[:, :], bq).then_inc(weights_in, 16)

            @block.gpsimd
            def _(pool):
                pool.memset(mask16[:, :], 0.0).then_inc(consts_zeroed, 1)
                pool.tensor_copy(ident16[:, :], ident[:, :]).then_inc(consts_made, 1)
                pool.wait_ge(consts_zeroed, 1)
                pool.affine_select(out=mask16[:, :], in_=mask16[:, :], compare_op=ALU.is_ge, fill=MASKED,
                                   base=0, pattern=[[-1, P]], channel_multiplier=1).then_inc(consts_made, 1)
                pool.wait_ge(m_sb, H // 4)

                def load_head(u, j):
                    k = 2 * u + j
                    when(pool, qm_ps, k - 1)
                    pool.tensor_copy(m_head[j][:, :], m_all[:, bass.ds((k % H) * P, P)])\
                        .then_inc(m_head_ready, 1)

                def step(u, j, nxt, last, this):
                    if nxt:
                        load_head(*before(u, j, -1))
                load_head(0, 0)
                steps(step)(pool)

            @block.tensor
            def _(pe):
                pe.wait_ge(weights_in, 48)
                for g in range(H // 4):
                    for h in range(4 * g, 4 * g + 4):
                        mm = pe.matmul(ps_s[g][:, (h % 4) * P:(h % 4 + 1) * P], wq[:, h * P:(h + 1) * P],
                                       wk[:, h * P:(h + 1) * P], start=True, stop=True)
                    mm.then_inc(m_ps, 1)
                for h in range(H):
                    mm = pe.matmul(ps_qm[:, h:h + 1], wk[:, h * P:(h + 1) * P], bq_sb[:, h:h + 1],
                                   start=True, stop=True)
                mm.then_inc(mb_ps, 1)
                pe.wait_ge(consts_made, 2)
                pe.wait_ge(m_sb, H // 4)
                pe.wait_ge(mb_sb, 1)

                def queries(u, j):
                    k = 2 * u + j
                    pe.wait_ge(m_head_ready, k + 1)
                    when(pe, qm_sb, k)
                    pe.matmul(ps_qm[:, :], m_head[j][:, :], xT_all[:, bass.ds(sequence(u) * S, S)],
                              start=True, stop=True).then_inc(qm_ps, 1)

                def scores(u, j, i):
                    k = 2 * u + j
                    pe.wait_ge(qm_sb, k + 1)
                    when(pe, probs_ready[i], k)
                    n = (i + 1) * P
                    pe.matmul(ps_s[i][:, 0:n], qm[j][:, i * P:n], xT_all[:, bass.ds(sequence(u) * S, n)],
                              start=True, stop=False)
                    pe.matmul(ps_s[i][:, i * P:n], ident16[:, :], mask16[:, :], start=False, stop=True)\
                        .then_inc(scores_ps[i], 1)

                def turn(u, j, i):
                    k = 2 * u + j
                    pe.wait_ge(probs_ready[i], k + 1)
                    if i >= 2:
                        pe.wait_ge(pT_sb[i - 2], k + 1)
                    else:
                        when(pe, pT_sb[i + 2], k)
                    for n in range(i + 1):
                        mm = pe.transpose(ps_t[i % 2][:, n * P:(n + 1) * P], probs[i][:, n * P:(n + 1) * P],
                                          ident[:, :])
                    mm.then_inc(pT_ps[i], 1)

                def weighted_values(u, j, i):
                    k = 2 * u + j
                    pe.wait_ge(pT_sb[i], k + 1)
                    if i == 0:
                        when(pe, out_ready, k)
                    for n in range(i + 1):
                        mm = pe.matmul(out_ps[:, i, :], probsT[i][:, n * P:(n + 1) * P],
                                       v_all[:, bass.ds((k * B + n) * PV, PV)], start=(n == 0), stop=(n == i))
                    mm.then_inc(out_block[i], 1)

                def step(u, j, nxt, last, this):
                    b = before(u, j, 1)
                    if this:
                        scores(u, j, 0)
                    if last:
                        turn(*b, 0)
                        turn(*b, 1)
                    if this:
                        scores(u, j, 1)
                    if last:
                        weighted_values(*b, 0)
                        turn(*b, 2)
                    if this:
                        scores(u, j, 2)
                    if last:
                        weighted_values(*b, 1)
                        turn(*b, 3)
                    if nxt:
                        queries(*before(u, j, -1))
                    if last:
                        weighted_values(*b, 2)
                    if this:
                        scores(u, j, 3)
                    if last:
                        weighted_values(*b, 3)
                queries(0, 0)
                steps(step)(pe)

            @block.scalar
            def _(act):
                for g in range(H // 4):
                    act.wait_ge(m_ps, g + 1)
                    act.copy(m_all[:, g * 4 * P:(g + 1) * 4 * P], ps_s[g][:, :]).then_inc(m_sb, 1)
                act.wait_ge(mb_ps, 1)
                act.mul(mb_all[:, :], ps_qm[:, 0:H], SCALE).then_inc(mb_sb, 1)
                act.wait_ge(mb_sb, 1)

                def copy_queries(u, j):
                    k = 2 * u + j
                    act.wait_ge(qm_ps, k + 1)
                    when(act, scores_ps[B - 1], k - 1)
                    act.activation(qm[j][:, :], ps_qm[:, :], ACT.Identity,
                                   bias=mb_all[:, bass.ds(k % H, 1)], scale=SCALE).then_inc(qm_sb, 1)

                def exponentials(u, j, i):
                    k = 2 * u + j
                    act.wait_ge(max_ready[i], k + 1)
                    when(act, pT_ps[i], k)
                    act.activation(probs[i][:, :], ps_s[i][:, 0:(i + 1) * P], ACT.Exp,
                                   bias=neg_max[:, i:i + 1]).then_inc(probs_ready[i], 1)

                def copy_turned(u, j, i):
                    k = 2 * u + j
                    act.wait_ge(pT_ps[i], k + 1)
                    when(act, out_block[i], k)
                    act.copy(probsT[i][:, :], ps_t[i % 2][:, 0:(i + 1) * P]).then_inc(pT_sb[i], 1)

                def step(u, j, nxt, last, this):
                    b = before(u, j, 1)
                    if this:
                        exponentials(u, j, 0)
                        exponentials(u, j, 1)
                    if this:
                        exponentials(u, j, 2)
                    if last:
                        copy_turned(*b, 3)
                    if nxt:
                        copy_queries(*before(u, j, -1))
                    if this:
                        exponentials(u, j, 3)
                copy_queries(0, 0)
                steps(step)(act)

            @block.vector
            def _(dve):
                def row_max(u, j, i):
                    k = 2 * u + j
                    dve.wait_ge(scores_ps[i], k + 1)
                    dve.tensor_reduce(neg_max[:, i:i + 1], ps_s[i][:, 0:(i + 1) * P], AX_X, ALU.max,
                                      negate=True).then_inc(max_ready[i], 1)

                def copy_turned(u, j, i):
                    k = 2 * u + j
                    dve.wait_ge(pT_ps[i], k + 1)
                    when(dve, out_block[i], k)
                    dve.tensor_copy(probsT[i][:, :], ps_t[i % 2][:, 0:(i + 1) * P]).then_inc(pT_sb[i], 1)

                def normalise(u, j):
                    k = 2 * u + j
                    dve.wait_ge(out_block[B - 1], k + 1)
                    when(dve, out_ready, k)
                    dve.reciprocal(recip[:, :], out_ps[:, :, DH]).then_inc(recips_ready, 1)
                    dve.wait_ge(recips_ready, k + 1)
                    dve.tensor_tensor(sa_steps[:, bass.ds(k, 1), :, :].rearrange("p k i c -> p (k i) c"),
                                      out_ps[:, :, 0:DH], recip[:, :].unsqueeze(2).to_broadcast([P, B, DH]),
                                      ALU.mult).then_inc(out_ready, 1)

                def step(u, j, nxt, last, this):
                    b = before(u, j, 1)
                    if this:
                        row_max(u, j, 0)
                    if last:
                        copy_turned(*b, 0)
                        copy_turned(*b, 1)
                    if this:
                        row_max(u, j, 1)
                    if last:
                        copy_turned(*b, 2)
                    if this:
                        row_max(u, j, 2)
                        row_max(u, j, 3)
                    if last:
                        normalise(*b)
                steps(step)(dve)


def skewed(eng, n, begin, ahead, depth, stride, step):
    def one(s):
        step(s // stride, s % stride, lambda p: 0 <= s - p < n)
    whole = (n - ahead - begin) // stride * stride
    for s in range(begin):
        one(s)
    first, j0 = begin // stride, begin % stride
    with eng.Fori(first, first + whole // stride) as u:
        for j in range(j0, j0 + stride):
            step(u + j // stride, j % stride, lambda p: True)
    for s in range(begin + whole, n + depth):
        one(s)


def earlier(u, j, p, stride=2):
    return u + (j - p) // stride, (j - p) % stride


ROW = P + 1
NOWHERE = 1 << 22


def route1(nc, sh, wp, bp, cT, keep, sa_all, routing):
    x_all, ident, ones = keep
    rows_dram, w_all, tile_expert, tile_row = routing
    B, S = sh.blocks, sh.seq
    NG, NT, LIST, TILES = sh.batches, sh.tiles, sh.list_rows, sh.listed_tiles
    with ExitStack() as ctx:
        def sb(name, shape, dt=F32):
            return ctx.enter_context(nc.sbuf_tensor(name, shape, dt))

        def sem(name):
            return ctx.enter_context(nc.semaphore(name))

        wp_sb, bp_sb = sb("wp_sb", [P, P]), sb("bp_sb", [1, P])
        cT_sb, cT2, csq_in, csq = sb("cT_sb", [P, E]), sb("cT2", [P, E]), sb("csq_in", [P, E]), sb("csq", [1, E])
        ones_col = sb("ones_col", [P, 1])
        iota = sb("r_iota", [P, B * E])
        list_base = sb("list_base", [P, E])
        place_in_tile = sb("place_in_tile", [P, 1])
        half = sb("half", [P, 2 * B])
        minus_half = sb("r_minus_half", [P, B])
        before16, ones16 = sb("before16", [P, P], BF16), sb("ones16", [P, P], BF16)
        ids = [sb(f"ids{r}", [P, NT], U32) for r in range(2)]
        filler = sb("filler", [P, ROW])

        sa_tile, saT, r3 = sb("sa_tile", [P, S]), sb("saT", [P, S]), sb("r3", [P, S])
        stats3, mv3, var3, rstd3 = sb("stats3", [P, B * 6]), sb("mv3", [P, B * 2]), sb("var3", [P, B]), sb("rstd3", [P, B])
        x3 = [sb(f"x3_{j}", [P, S]) for j in range(2)]
        x3T = sb("x3T", [P, S])
        square, norm_sq = sb("square", [P, P]), [sb(f"norm_sq{j}", [P, B]) for j in range(2)]
        dist2 = [sb(f"dist2_{j}", [P, B * E]) for j in range(2)]
        top, top_idx, top_idxf = sb("r_top", [P, B * 8]), sb("r_top_idx", [P, B * 8], U32), sb("r_top_idxf", [P, B * 8])
        two, dist = sb("two", [P, 2 * B]), sb("dist", [P, 2 * B])
        wdiff, wexp, wden = sb("wdiff", [P, B]), sb("wexp", [P, B]), sb("wden", [P, B])
        picked = [[sb(f"picked{r}_{j}", [P, B * E]) for j in range(2)] for r in range(2)]
        picked16 = sb("picked16", [P, B * E], BF16)
        base = sb("base", [P, E])
        place, masked = sb("place", [P, B * E]), sb("masked", [P, B * E])
        slot, slot_idx = sb("slot", [P, 2 * B]), [sb(f"slot_idx{j}", [P, 2 * B], U32) for j in range(2)]
        rows = [[sb(f"rows{r}_{j}", [P, B * ROW]) for j in range(2)] for r in range(2)]
        pad_place, pad_idx = sb("pad_place", [P, E]), sb("pad_idx", [P, E], U32)
        t_f, t_i = sb("t_f", [1, 5 * E]), sb("t_i", [1, 2 * E], I32)
        number = sb("number", [1, TILES])
        passed_end, end_terms = sb("passed_end", [1, E * TILES]), sb("end_terms", [1, E * TILES])
        sum_f = sb("sum_f", [1, 3 * TILES])

        def pb(name):
            return ctx.enter_context(nc.psum_tensor(name, [P, S], F32))
        ps_saT, ps_proj, ps_x3T, ps_dist, ps_place, ps_csq = (
            pb("r_saT"), pb("r_proj"), pb("r_x3T"), pb("r_dist"), pb("r_place"), pb("r_csq"))

        weights_in, filler_stored = sem("r_weights_in"), sem("filler_stored")
        consts_begun, consts_made = sem("r_consts_begun"), sem("r_consts")
        c_squared, csq_ps, c_ready = sem("c_squared"), sem("csq_ps"), sem("c_ready")
        sa_copied, saT_ps, saT_sb, proj_ps = sem("sa_copied"), sem("saT_ps"), sem("saT_sb"), sem("r_proj_ps")
        norm3_step, rstd3_ready, x3_ready = sem("norm3_step"), sem("rstd3_ready"), sem("x3_ready")
        x3_kept = [sem(f"x3_kept{j}") for j in range(2)]
        x3T_ps, x3T_sb, squared, dist_ps, dist2_ready = (
            sem("x3T_ps"), sem("x3T_sb"), sem("squared"), sem("dist_ps"), sem("dist2_ready"))
        pick_step, two_ready, dist_ready, wdiff_ready, wexp_ready = (
            sem("pick_step"), sem("two_ready"), sem("dist_ready"), sem("wdiff_ready"), sem("wexp_ready"))
        picked_ready, place_ps, place_step, slots_ready = (
            sem("picked_ready"), sem("place_ps"), sem("place_step"), sem("slots_ready"))
        rows_ready = sem("rows_ready")
        scattered = [sem(f"scattered{j}") for j in range(2)]
        pads_ready, pads_scattered, table_step = sem("pads_ready"), sem("pads_scattered"), sem("table_step")
        passed, sp_passed, pool_passed = sem("r_passed"), sem("r_sp_passed"), sem("r_pool_passed")
        weights_step, slot_step = sem("weights_step"), sem("slot_step")

        NORM = 2 * B + 2
        PICK = 2 * B + 3
        PLACE = 4

        def steps(eng, step):
            skewed(eng, NG, 5, 1, 3, 2, step)

        def blk(t, i, n=P):
            return t[:, i * n:(i + 1) * n]

        def by_tile(t, n):
            return t[:, :].rearrange("p (i c) -> p i c", c=n)

        sa_groups = sa_all[:, :].rearrange("p (g h i c) -> p g h i c", h=H, i=B, c=DH)

        with nc.Block() as block:

            @block.sync
            def _(sp):
                for dst, src in ((wp_sb, wp), (bp_sb, bp), (cT_sb, cT)):
                    sp.dma_start(dst[:, :], src).then_inc(weights_in, 16)
                sp.wait_ge(consts_made, 10)
                for n in range(E):
                    sp.dma_start(rows_dram[E * LIST + n * P:E * LIST + (n + 1) * P, :], filler[:, :])\
                      .then_inc(filler_stored, 16)

                def keep_x3(u, j):
                    g = 2 * u + j
                    wait_alone(sp, x3_ready, B * (g + 1), sp_passed)
                    sp.dma_start(x_all[:, bass.ds(g * S, S)], x3[j][:, :]).then_inc(x3_kept[j], 16)

                def step(u, j, alive):
                    if alive(1):
                        keep_x3(*earlier(u, j, 1))
                steps(sp, step)
                sp.wait_ge(filler_stored, 16 * E)
                for j in range(2):
                    sp.wait_ge(x3_kept[j], 16 * NG // 2)

            @block.gpsimd
            def _(pool):
                pool.iota(iota[:, :], pattern=[[0, B], [1, E]], base=0, channel_multiplier=0,
                          allow_small_or_imprecise_dtypes=True).then_inc(consts_made, 1)
                pool.iota(place_in_tile[:, :], pattern=[[0, 1]], base=0, channel_multiplier=1,
                          allow_small_or_imprecise_dtypes=True).then_inc(consts_made, 1)
                for r in range(2):
                    pool.iota(ids[r][:, :], pattern=[[P, NT]], base=r * sh.tokens, channel_multiplier=1)\
                        .then_inc(consts_made, 1)
                pool.iota(number[:, :], pattern=[[1, TILES]], base=0, channel_multiplier=0,
                          allow_small_or_imprecise_dtypes=True).then_inc(consts_made, 1)
                pool.memset(half[:, :], 0.5).then_inc(consts_made, 1)
                pool.memset(minus_half[:, :], -0.5).then_inc(consts_made, 1)
                pool.memset(ones_col[:, :], 1.0).then_inc(consts_made, 1)
                pool.memset(ones16[:, :], 1.0).then_inc(consts_begun, 1)
                pool.memset(filler[:, 0:P], 0.0).then_inc(consts_begun, 1)
                pool.memset(filler[:, P:ROW].bitcast(U32), NOWHERE).then_inc(consts_begun, 1)
                pool.wait_ge(consts_begun, 3)
                pool.affine_select(out=before16[:, :], in_=ones16[:, :], compare_op=ALU.is_ge, fill=0.0,
                                   base=-1, pattern=[[1, P]], channel_multiplier=-1).then_inc(consts_made, 1)
                pool.wait_ge(consts_made, 1)
                pool.tensor_scalar(list_base[:, :], iota[:, 0:E], float(LIST), 0.0, ALU.mult, ALU.add)\
                    .then_inc(consts_made, 1)
                pool.wait_ge(consts_made, 10)

                def inverse3(u, j):
                    g = 2 * u + j
                    pool.wait_ge(norm3_step, NORM * (g + 1))
                    pool.tensor_tensor(rstd3[:, :], var3[:, :], minus_half[:, :], ALU.pow).then_inc(rstd3_ready, 1)

                def distances(u, j):
                    g = 2 * u + j
                    pool.wait_ge(two_ready, g + 1)
                    pool.tensor_tensor(dist[:, :], two[:, :], half[:, :], ALU.pow).then_inc(dist_ready, 1)

                def scatter(u, j):
                    g = 2 * u + j
                    pool.wait_ge(slots_ready, g + 1)
                    wait_alone(pool, rows_ready, 4 * (g + 1), pool_passed)
                    for r in range(2):
                        for i in range(B):
                            pool.indirect_dma_start(
                                out=rows_dram[:, :], out_offset=bass.IndirectOffsetOnAxis(
                                    ap=slot_idx[j][:, r * B + i:r * B + i + 1], axis=0),
                                in_=blk(rows[r][j], i, ROW), in_offset=None).then_inc(scattered[j], 16)

                def step(u, j, alive):
                    if alive(2):
                        distances(*earlier(u, j, 2))
                    if alive(0):
                        inverse3(u, j)
                    if alive(3):
                        scatter(*earlier(u, j, 3))
                steps(pool, step)
                pool.wait_ge(pads_ready, 2)
                for e in range(E):
                    pool.indirect_dma_start(
                        out=rows_dram[:, :], out_offset=bass.IndirectOffsetOnAxis(ap=pad_idx[:, e:e + 1], axis=0),
                        in_=filler[:, :], in_offset=None).then_inc(pads_scattered, 16)
                for j in range(2):
                    pool.wait_ge(scattered[j], 16 * 2 * B * NG // 2)
                pool.wait_ge(pads_scattered, 16 * E)

            @block.tensor
            def _(pe):
                pe.wait_ge(weights_in, 48)
                pe.wait_ge(consts_made, 10)
                pe.wait_ge(c_squared, 2)
                pe.matmul(ps_csq[0:1, 0:E], ones_col[:, :], csq_in[:, :], start=True, stop=True).then_inc(csq_ps, 1)
                pe.wait_ge(c_ready, 1)

                def turn_sa(u, j):
                    g = 2 * u + j
                    pe.wait_ge(sa_copied, g + 1)
                    when(pe, saT_sb, g)
                    for i in range(B):
                        mm = pe.transpose(blk(ps_saT, i), blk(sa_tile, i), ident[:, :])
                    mm.then_inc(saT_ps, 1)

                def project(u, j):
                    g = 2 * u + j
                    pe.wait_ge(saT_sb, g + 1)
                    when(pe, norm3_step, NORM * (g - 1) + 1)
                    for i in range(B):
                        pe.matmul(blk(ps_proj, i), blk(saT, i), wp_sb[:, :], start=True, stop=False)
                        mm = pe.matmul(blk(ps_proj, i), ones[0:1, 0:P], bp_sb[:, :], start=False, stop=True)
                    mm.then_inc(proj_ps, 1)

                def turn_x3(u, j):
                    g = 2 * u + j
                    pe.wait_ge(x3_ready, B * (g + 1))
                    when(pe, x3T_sb, g)
                    for i in range(B):
                        mm = pe.transpose(blk(ps_x3T, i), blk(x3[j], i), ident[:, :])
                    mm.then_inc(x3T_ps, 1)

                def centroid_products(u, j):
                    g = 2 * u + j
                    pe.wait_ge(x3T_sb, g + 1)
                    when(pe, dist2_ready, B * g)
                    for i in range(B):
                        pe.matmul(blk(ps_dist, i, E), blk(x3T, i), cT2[:, :], start=True, stop=False)
                        mm = pe.matmul(blk(ps_dist, i, E), ones[0:1, 0:P], csq[:, :], start=False, stop=True)
                    mm.then_inc(dist_ps, 1)

                def count(u, j):
                    g = 2 * u + j
                    pe.wait_ge(picked_ready, g + 1)
                    when(pe, place_step, PLACE * (g - 1) + 2)
                    for i in range(B + 1):
                        for n in range(i):
                            mm = pe.matmul(blk(ps_place, i, E), ones16[:, :], blk(picked16, n, E),
                                           start=(n == 0), stop=(i == B and n == B - 1))
                        if i < B:
                            mm = pe.matmul(blk(ps_place, i, E), before16[:, :], blk(picked16, i, E),
                                           start=(i == 0), stop=True)
                    mm.then_inc(place_ps, 1)

                def step(u, j, alive):
                    if alive(0):
                        turn_sa(u, j)
                    if alive(1):
                        turn_x3(*earlier(u, j, 1))
                    if alive(0):
                        project(u, j)
                    if alive(1):
                        centroid_products(*earlier(u, j, 1))
                    if alive(2):
                        count(*earlier(u, j, 2))
                steps(pe, step)

            @block.scalar
            def _(act):
                act.wait_ge(consts_made, 10)

                def copy_sa(u, j):
                    g = 2 * u + j
                    when(act, saT_ps, g)
                    act.copy(sa_tile[:, :].rearrange("p (i h c) -> p h i c", h=H, c=DH),
                             sa_groups[:, bass.ds(g, 1), :, :, :].rearrange("p g h i c -> p (g h) i c"))\
                       .then_inc(sa_copied, 1)

                def copy_saT(u, j):
                    g = 2 * u + j
                    act.wait_ge(saT_ps, g + 1)
                    when(act, proj_ps, g)
                    act.copy(saT[:, :], ps_saT[:, :]).then_inc(saT_sb, 1)

                def copy_x3T(u, j):
                    g = 2 * u + j
                    act.wait_ge(x3T_ps, g + 1)
                    when(act, dist_ps, g)
                    act.copy(x3T[:, :], ps_x3T[:, :]).then_inc(x3T_sb, 1)

                def square_rows(u, j):
                    g = 2 * u + j
                    act.wait_ge(x3_ready, B * (g + 1))
                    when(act, dist2_ready, B * (g - 1))
                    for i in range(B):
                        when(act, squared, B * g + i)
                        act.activation(square[:, :], blk(x3[j], i), ACT.Square,
                                       accum_out=norm_sq[j][:, i:i + 1]).then_inc(squared, 1)

                def weight_exp(u, j):
                    g = 2 * u + j
                    act.wait_ge(wdiff_ready, g + 1)
                    act.activation(wexp[:, :], wdiff[:, :], ACT.Exp).then_inc(wexp_ready, 1)

                def make_rows(u, j):
                    g = 2 * u + j
                    act.wait_ge(x3_kept[j], 16 * (u + 1))
                    when(act, scattered[j], 16 * 2 * B * u)
                    for r in range(2):
                        out = by_tile(rows[r][j], ROW)
                        act.copy(out[:, :, 0:P], x_all[:, bass.ds(g * S, S)].rearrange("p (i d) -> p i d", d=P))\
                           .then_inc(rows_ready, 1)
                        act.copy(out[:, :, P].bitcast(U32), ids[r][:, bass.ds(g * B, B)]).then_inc(rows_ready, 1)

                def step(u, j, alive):
                    if alive(3):
                        make_rows(*earlier(u, j, 3))
                    if alive(0):
                        copy_saT(u, j)
                    if alive(-1):
                        copy_sa(*earlier(u, j, -1))
                    if alive(1):
                        square_rows(*earlier(u, j, 1))
                        copy_x3T(*earlier(u, j, 1))
                    if alive(2):
                        weight_exp(*earlier(u, j, 2))
                copy_sa(0, 0)
                steps(act, step)

            @block.vector
            def _(dve):
                dve.wait_ge(weights_in, 48)
                dve.wait_ge(consts_made, 10)
                dve.tensor_scalar(cT2[:, :], cT_sb[:, :], -2.0, None, ALU.mult).then_inc(c_squared, 1)
                dve.tensor_tensor(csq_in[:, :], cT_sb[:, :], cT_sb[:, :], ALU.mult).then_inc(c_squared, 1)
                dve.tensor_copy(base[:, :], list_base[:, :]).then_inc(c_ready, 1)
                dve.wait_ge(csq_ps, 1)
                dve.tensor_copy(csq[:, :], ps_csq[0:1, 0:E]).then_inc(c_ready, 1)
                dve.wait_ge(c_ready, 2)

                def residual(u, j):
                    g = 2 * u + j
                    dve.wait_ge(proj_ps, g + 1)
                    when(dve, x3_ready, B * g)
                    dve.tensor_tensor(r3[:, :], x_all[:, bass.ds(g * S, S)], ps_proj[:, :], ALU.add)\
                        .then_inc(norm3_step, 1)
                    dve.wait_ge(norm3_step, NORM * g + 1)
                    for i in range(B):
                        dve.bn_stats(blk(stats3, i, 6), blk(r3, i)).then_inc(norm3_step, 1)
                    wait_alone(dve, norm3_step, NORM * g + 1 + B, passed)
                    for i in range(B):
                        dve.bn_aggr(blk(mv3, i, 2), blk(stats3, i, 6)).then_inc(norm3_step, 1)
                    dve.wait_ge(norm3_step, NORM * g + 1 + 2 * B)
                    dve.tensor_scalar(var3[:, :], by_tile(mv3, 2)[:, :, 1], EPS, None, ALU.add)\
                       .then_inc(norm3_step, 1)

                def norm3(u, j):
                    g = 2 * u + j
                    dve.wait_ge(rstd3_ready, g + 1)
                    when(dve, x3T_ps, g - 1)
                    when(dve, squared, B * (g - 1))
                    when(dve, x3_kept[j], 16 * u)
                    for i in range(B):
                        dve.tensor_scalar(blk(x3[j], i), blk(r3, i), mv3[:, 2 * i:2 * i + 1], rstd3[:, i:i + 1],
                                          ALU.subtract, ALU.mult).then_inc(x3_ready, 1)

                def square_distances(u, j):
                    g = 2 * u + j
                    dve.wait_ge(dist_ps, g + 1)
                    dve.wait_ge(squared, B * (g + 1))
                    for i in range(B):
                        dve.tensor_scalar(blk(dist2[j], i, E), blk(ps_dist, i, E), norm_sq[j][:, i:i + 1], 1e-12,
                                          ALU.add, ALU.max).then_inc(dist2_ready, 1)

                tops, idxs = by_tile(top, 8), by_tile(top_idxf, 8)

                def pick(u, j):
                    g = 2 * u + j
                    base_count = PICK * g
                    dve.wait_ge(dist2_ready, B * (g + 1))
                    when(dve, picked_ready, g)
                    dve.sem_inc(passed, 1)
                    for i in range(B):
                        dve.max(blk(top, i, 8), blk(dist2[j], i, E)).then_inc(pick_step, 1)
                    dve.wait_ge(pick_step, base_count + B)
                    dve.tensor_copy(by_tile(two, 2), tops[:, :, 0:2]).then_inc(two_ready, 1)
                    for i in range(B):
                        dve.max_index(blk(top_idx, i, 8), blk(top, i, 8), blk(dist2[j], i, E)).then_inc(pick_step, 1)
                    dve.wait_ge(pick_step, base_count + 2 * B)
                    dve.tensor_copy(top_idxf[:, :], top_idx[:, :]).then_inc(pick_step, 1)
                    dve.wait_ge(pick_step, base_count + 2 * B + 1)
                    when(dve, place_step, PLACE * (g - 1))
                    for r in range(2):
                        dve.tensor_tensor(by_tile(picked[r][j], E), by_tile(iota, E),
                                          idxs[:, :, r:r + 1].to_broadcast([P, B, E]), ALU.is_equal)\
                           .then_inc(pick_step, 1)
                    dve.wait_ge(pick_step, base_count + 2 * B + 3)
                    when(dve, place_ps, g)
                    dve.tensor_tensor(picked16[:, :], picked[0][j][:, :], picked[1][j][:, :], ALU.add)\
                       .then_inc(picked_ready, 1)

                pairs = w_all[:, :].rearrange("p (g r i) -> p g r i", r=2, i=B)

                def weigh(u, j):
                    g = 2 * u + j
                    dists = by_tile(dist, 2)
                    mine = pairs[:, bass.ds(g, 1), :, :].rearrange("p g r i -> p (g r) i")
                    dve.wait_ge(dist_ready, g + 1)
                    when(dve, wexp_ready, g)
                    dve.tensor_tensor(wdiff[:, :], dists[:, :, 1], dists[:, :, 0], ALU.subtract)\
                        .then_inc(wdiff_ready, 1)
                    dve.wait_ge(wexp_ready, g + 1)
                    when(dve, weights_step, 3 * g)
                    dve.tensor_scalar(wden[:, :], wexp[:, :], 1.0, None, ALU.add).then_inc(weights_step, 1)
                    dve.wait_ge(weights_step, 3 * g + 1)
                    dve.reciprocal(mine[:, 0, :], wden[:, :]).then_inc(weights_step, 1)
                    dve.wait_ge(weights_step, 3 * g + 2)
                    dve.tensor_tensor(mine[:, 1, :], wexp[:, :], mine[:, 0, :], ALU.mult).then_inc(weights_step, 1)

                def find_places(u, j):
                    g = 2 * u + j
                    count = PLACE * g
                    dve.wait_ge(place_ps, g + 1)
                    when(dve, slots_ready, g)
                    dve.tensor_tensor(by_tile(place, E), ps_place[:, 0:B * E].rearrange("p (i c) -> p i c", c=E),
                                      base[:, :].unsqueeze(1).to_broadcast([P, B, E]), ALU.add)\
                       .then_inc(place_step, 1)
                    dve.wait_ge(place_step, count + 1)
                    dve.tensor_tensor(base[:, :], base[:, :], ps_place[:, B * E:(B + 1) * E], ALU.add)\
                       .then_inc(place_step, 1)
                    for r in range(2):
                        when(dve, slot_step, 4 * g + 2 * r)
                        dve.tensor_tensor(masked[:, :], place[:, :], picked[r][j][:, :], ALU.mult)\
                           .then_inc(slot_step, 1)
                        dve.wait_ge(slot_step, 4 * g + 2 * r + 1)
                        dve.tensor_reduce(blk(slot, r, B), by_tile(masked, E), AX_X, ALU.add).then_inc(slot_step, 1)
                    dve.wait_ge(slot_step, 4 * g + 4)
                    dve.wait_ge(place_step, count + 2)
                    dve.sem_inc(place_step, 2)
                    when(dve, scattered[j], 16 * 2 * B * u)
                    dve.tensor_copy(slot_idx[j][:, :], slot[:, :]).then_inc(slots_ready, 1)

                def step(u, j, alive):
                    if alive(1):
                        norm3(*earlier(u, j, 1))
                    if alive(2):
                        pick(*earlier(u, j, 2))
                    if alive(0):
                        residual(u, j)
                    if alive(3):
                        find_places(*earlier(u, j, 3))
                    if alive(2):
                        weigh(*earlier(u, j, 2))
                    if alive(1):
                        square_distances(*earlier(u, j, 1))
                steps(dve, step)

                dve.wait_ge(place_step, PLACE * NG)
                dve.tensor_scalar(pad_place[:, :], base[:, :], place_in_tile[:, :], None, ALU.add)\
                    .then_inc(pads_ready, 1)
                dve.wait_ge(pads_ready, 1)
                dve.tensor_copy(pad_idx[:, :], pad_place[:, :]).then_inc(pads_ready, 1)

                count, tiles, end, jump = (t_f[:, n * E:(n + 1) * E] for n in range(4))
                one = t_f[:, 4 * E:5 * E]
                dve.tensor_tensor(count, base[0:1, :], list_base[0:1, :], ALU.subtract).then_inc(table_step, 1)
                dve.memset(one, 1.0).then_inc(table_step, 1)
                dve.wait_ge(table_step, 2)
                dve.tensor_scalar(t_i[:, 0:E], count, float(P - 1), None, ALU.add).then_inc(table_step, 1)
                dve.wait_ge(table_step, 3)
                dve.tensor_scalar(t_i[:, E:2 * E], t_i[:, 0:E], P.bit_length() - 1, None,
                                  ALU.arith_shift_right).then_inc(table_step, 1)
                dve.wait_ge(table_step, 4)
                dve.tensor_copy(tiles, t_i[:, E:2 * E]).then_inc(table_step, 1)
                dve.wait_ge(table_step, 5)
                dve.tensor_tensor_scan(end, one, tiles, 0.0, ALU.mult, ALU.add).then_inc(table_step, 1)
                dve.tensor_scalar(jump, tiles, float(-P), float(LIST), ALU.mult, ALU.add).then_inc(table_step, 1)
                dve.wait_ge(table_step, 7)
                by_expert = passed_end[:, :].rearrange("p (e n) -> p e n", e=E)
                dve.tensor_tensor(by_expert, number[:, :].unsqueeze(1).to_broadcast([1, E, TILES]),
                                  end.unsqueeze(2).to_broadcast([1, E, TILES]), ALU.is_ge).then_inc(table_step, 1)
                dve.wait_ge(table_step, 8)
                dve.tensor_tensor(end_terms[:, :].rearrange("p (e n) -> p e n", e=E), by_expert,
                                  jump.unsqueeze(2).to_broadcast([1, E, TILES]), ALU.mult).then_inc(table_step, 1)
                expert_f, moved, row_f = (sum_f[:, n * TILES:(n + 1) * TILES] for n in range(3))
                dve.tensor_reduce(expert_f, passed_end[:, :].rearrange("p (e n) -> p n e", e=E), AX_X, ALU.add)\
                   .then_inc(table_step, 1)
                dve.wait_ge(table_step, 10)
                dve.tensor_reduce(moved, end_terms[:, :].rearrange("p (e n) -> p n e", e=E), AX_X, ALU.add)\
                   .then_inc(table_step, 1)
                dve.tensor_scalar(tile_expert[:, :], expert_f, float(E - 1), None, ALU.min).then_inc(table_step, 1)
                dve.wait_ge(table_step, 12)
                dve.scalar_tensor_tensor(out=row_f, in0=number[:, :], scalar=float(P), in1=moved, op0=ALU.mult,
                                         op1=ALU.add).then_inc(table_step, 1)
                dve.wait_ge(table_step, 13)
                dve.tensor_copy(tile_row[:, :], row_f).then_inc(table_step, 1)


def experts1(nc, sh, wg, bg, w1, b1, w2, b2, keep, routing, results):
    x_all, ident, ones = keep
    rows_dram, w_all, tile_expert, tile_row = routing
    C, CH, HID, TILES, LIST = sh.chunks, sh.chunk, sh.hidden, sh.listed_tiles, sh.list_rows
    with ExitStack() as ctx:
        def sb(name, shape, dt=F32):
            return ctx.enter_context(nc.sbuf_tensor(name, shape, dt))

        def sem(name):
            return ctx.enter_context(nc.semaphore(name))

        wg_sb, w1_sb = sb("wg_sb", [P, E * HID]), sb("w1_sb", [P, E * HID])
        bg_sb, b1_sb = sb("bg_sb", [P, E * HID]), sb("b1_sb", [P, E * HID])
        w2_sb, b2_sb = sb("w2_sb", [CH, E * C * P]), sb("b2_sb", [P, E * P])
        R = 8
        row_in = [sb(f"row_in{r}", [P, ROW]) for r in range(R)]
        row_out = [sb(f"row_out{r}", [P, P]) for r in range(R)]
        xT = [sb(f"e_xT{j}", [P, P]) for j in range(2)]
        gate = [sb(f"e_gate{j}", [P, HID]) for j in range(2)]
        silu = [sb(f"e_silu{j}", [P, HID]) for j in range(2)]
        up = [sb(f"e_up{j}", [P, HID]) for j in range(2)]
        hid = [sb(f"e_hid{j}", [P, HID]) for j in range(2)]
        hidT = [sb(f"e_hidT{j}", [CH, C * P]) for j in range(2)]

        def pb(name):
            return ctx.enter_context(nc.psum_tensor(name, [P, 4 * P], F32))
        ps_x, ps_h, ps_y = pb("e_ps_x"), pb("e_ps_h"), pb("e_ps_y")
        ps_g, ps_u = [pb(f"e_ps_g{j}") for j in range(2)], [pb(f"e_ps_u{j}") for j in range(2)]

        weights_in = sem("e_weights_in")
        row_loaded = [sem(f"row_loaded{r}") for r in range(R)]
        sent = [sem(f"sent{r}") for r in range(R)]
        xT_ps, xT_sb, gate_ps, up_ps = sem("e_xT_ps"), sem("e_xT_sb"), sem("e_gate_ps"), sem("e_up_ps")
        gate_sb, silu_ready, up_sb, hid_ready = sem("e_gate_sb"), sem("e_silu"), sem("e_up_sb"), sem("e_hid")
        hT_ps, hT_sb, y_ps, y_sb = sem("e_hT_ps"), sem("e_hT_sb"), sem("e_y_ps"), sem("e_y_sb")
        sp_passed, pool_passed = sem("e_sp_passed"), sem("e_pool_passed")

        def steps(eng, step):
            skewed(eng, TILES, R, 1, 3, R, step)

        def back(u, r, p):
            return earlier(u, r, p, R)

        def expert_of(eng, n):
            return eng.value_load(tile_expert[0:1, bass.ds(n, 1)], min_val=0, max_val=E - 1)

        with nc.Block() as block:

            @block.sync
            def _(sp):
                sp.dma_start(wg_sb[:, :], wg).then_inc(weights_in, 16)

                def load(u, r):
                    n = R * u + r
                    row = sp.value_load(tile_row[0:1, bass.ds(n, 1)], min_val=0, max_val=E * LIST + (E - 1) * P)
                    when(sp, sent[r], 16 * u)
                    sp.sem_inc(sp_passed, 1)
                    when(sp, xT_ps, n - R + 1)
                    sp.sem_inc(sp_passed, 1)
                    sp.dma_start(row_in[r][:, :], rows_dram[bass.ds(row, P), :]).then_inc(row_loaded[r], 16)

                def step(u, r, alive):
                    if alive(0):
                        load(u, r)
                for r in range(R):
                    load(0, r)
                for dst, src in ((w1_sb, w1), (w2_sb, w2)):
                    sp.dma_start(dst[:, :], src).then_inc(weights_in, 16)
                for dst, src in ((bg_sb, bg), (b1_sb, b1), (b2_sb, b2)):
                    sp.dma_start(dst[:, :], src.partition_broadcast(P)).then_inc(weights_in, 16)
                with sp.Fori(1, TILES // R) as u:
                    for r in range(R):
                        load(u, r)

            @block.gpsimd
            def _(pool):
                def send(u, r):
                    n = R * u + r
                    wait_alone(pool, y_sb, n + 1, pool_passed)
                    pool.indirect_dma_start(
                        out=results[:, :], out_offset=bass.IndirectOffsetOnAxis(
                            ap=row_in[r][:, P:ROW].bitcast(U32), axis=0),
                        in_=row_out[r][:, :], in_offset=None, bounds_check=2 * sh.tokens - 1,
                        oob_is_err=False).then_inc(sent[r], 16)

                def step(u, r, alive):
                    if alive(2):
                        send(*back(u, r, 2))
                steps(pool, step)
                for r in range(R):
                    pool.wait_ge(sent[r], 16 * TILES // R)

            @block.tensor
            def _(pe):
                pe.wait_ge(weights_in, 16 * 6)

                def turn_rows(u, r):
                    n = R * u + r
                    pe.wait_ge(row_loaded[r], 16 * (u + 1))
                    when(pe, xT_sb, n)
                    pe.transpose(ps_x[:, 0:P], row_in[r][:, 0:P], ident[:, :]).then_inc(xT_ps, 1)

                experts = {}

                def load_first(u, alive):
                    for p in (2, 1, 0):
                        if alive(p):
                            experts[-p % R] = expert_of(pe, R * u - p)

                def load_next(u, r):
                    if r + 1 < R:
                        experts[r + 1] = expert_of(pe, R * u + r + 1)

                def hidden(u, r):
                    n = R * u + r
                    j = r % 2
                    e = experts[r]
                    pe.wait_ge(xT_sb, n + 1)
                    when(pe, gate_sb, n - 1)
                    pe.matmul(ps_g[j][:, 0:HID], xT[j][:, :], wg_sb[:, bass.ds(e * HID, HID)], start=True,
                              stop=True).then_inc(gate_ps, 1)
                    when(pe, up_sb, n - 1)
                    pe.matmul(ps_u[j][:, 0:HID], xT[j][:, :], w1_sb[:, bass.ds(e * HID, HID)], start=True,
                              stop=True).then_inc(up_ps, 1)

                def turn_hidden(u, r):
                    n = R * u + r
                    pe.wait_ge(hid_ready, n + 1)
                    when(pe, hT_sb, n)
                    for c in range(C):
                        mm = pe.transpose(ps_h[0:CH, c * P:(c + 1) * P], hid[r % 2][:, c * CH:(c + 1) * CH],
                                          ident[:, :])
                    mm.then_inc(hT_ps, 1)

                def down(u, r):
                    n = R * u + r
                    e = experts[r]
                    pe.wait_ge(hT_sb, n + 1)
                    when(pe, y_sb, n)
                    for c in range(C):
                        mm = pe.matmul(ps_y[:, 0:P], hidT[r % 2][:, c * P:(c + 1) * P],
                                       w2_sb[:, bass.ds(e * C * P + c * P, P)], start=(c == 0), stop=(c == C - 1))
                    mm.then_inc(y_ps, 1)

                def step(u, r, alive):
                    if r == 0:
                        load_first(u, alive)
                    if alive(0):
                        hidden(u, r)
                    if alive(-1):
                        turn_rows(*back(u, r, -1))
                        load_next(u, r)
                    if alive(2):
                        down(*back(u, r, 2))
                    if alive(1):
                        turn_hidden(*back(u, r, 1))
                turn_rows(0, 0)
                steps(pe, step)

            @block.scalar
            def _(act):
                def copy_xT(u, r):
                    n = R * u + r
                    act.wait_ge(xT_ps, n + 1)
                    when(act, up_ps, n - 1)
                    act.copy(xT[r % 2][:, :], ps_x[:, 0:P]).then_inc(xT_sb, 1)

                def apply_silu(u, r):
                    n = R * u + r
                    act.wait_ge(gate_sb, n + 1)
                    when(act, hid_ready, n - 1)
                    act.activation(silu[r % 2][:, :], gate[r % 2][:, :], ACT.Silu).then_inc(silu_ready, 1)

                def copy_hT(u, r):
                    n = R * u + r
                    act.wait_ge(hT_ps, n + 1)
                    when(act, y_ps, n - 1)
                    act.copy(hidT[r % 2][:, :], ps_h[0:CH, 0:C * P]).then_inc(hT_sb, 1)

                def step(u, r, alive):
                    if alive(-1):
                        copy_xT(*back(u, r, -1))
                    if alive(0):
                        apply_silu(u, r)
                    if alive(1):
                        copy_hT(*back(u, r, 1))
                copy_xT(0, 0)
                steps(act, step)

            @block.vector
            def _(dve):
                dve.wait_ge(weights_in, 16 * 6)

                def add_biases(u, r):
                    n = R * u + r
                    j = r % 2
                    e = expert_of(dve, n)
                    dve.wait_ge(gate_ps, n + 1)
                    when(dve, silu_ready, n - 1)
                    dve.tensor_tensor(gate[j][:, :], ps_g[j][:, 0:HID], bg_sb[:, bass.ds(e * HID, HID)],
                                      ALU.add).then_inc(gate_sb, 1)
                    dve.wait_ge(up_ps, n + 1)
                    when(dve, hid_ready, n - 1)
                    dve.tensor_tensor(up[j][:, :], ps_u[j][:, 0:HID], b1_sb[:, bass.ds(e * HID, HID)],
                                      ALU.add).then_inc(up_sb, 1)

                def multiply(u, r):
                    n = R * u + r
                    j = r % 2
                    dve.wait_ge(up_sb, n + 1)
                    dve.wait_ge(silu_ready, n + 1)
                    when(dve, hT_ps, n - 1)
                    dve.tensor_tensor(hid[j][:, :], up[j][:, :], silu[j][:, :], ALU.mult).then_inc(hid_ready, 1)

                def finish(u, r):
                    n = R * u + r
                    e = expert_of(dve, n)
                    dve.wait_ge(y_ps, n + 1)
                    when(dve, sent[r], 16 * u)
                    dve.tensor_tensor(row_out[r][:, :], ps_y[:, 0:P], b2_sb[:, bass.ds(e * P, P)],
                                      ALU.add).then_inc(y_sb, 1)

                def step(u, r, alive):
                    if alive(0):
                        add_biases(u, r)
                    if alive(2):
                        finish(*back(u, r, 2))
                    if alive(0):
                        multiply(u, r)
                steps(dve, step)


def combine1(nc, sh, keep, w_all, results, out):
    x_all, ident, ones = keep
    B, S, NG = sh.blocks, sh.seq, sh.batches
    with ExitStack() as ctx:
        def sb(name, shape, dt=F32):
            return ctx.enter_context(nc.sbuf_tensor(name, shape, dt))

        def sem(name):
            return ctx.enter_context(nc.semaphore(name))

        minus_half = sb("f_minus_half", [P, B])
        y = [[sb(f"y{r}_{j}", [P, S]) for j in range(2)] for r in range(2)]
        weighted = [[sb(f"weighted{r}_{j}", [P, S]) for j in range(2)] for r in range(2)]
        part, r4 = sb("f_part", [P, S]), [sb(f"r4_{j}", [P, S]) for j in range(2)]
        stats, mv = sb("f_stats", [P, B * 6]), [sb(f"f_mv{j}", [P, B * 2]) for j in range(2)]
        var, rstd = [sb(f"f_var{j}", [P, B]) for j in range(2)], [sb(f"f_rstd{j}", [P, B]) for j in range(2)]
        x4 = [sb(f"x4_{j}", [P, S]) for j in range(2)]

        const_made = sem("f_const")
        loaded = [sem(f"y_loaded{j}") for j in range(2)]
        weighted_ready, norm_step, rstd_ready, x4_ready = (
            sem("weighted_ready"), sem("f_norm_step"), sem("f_rstd_ready"), sem("x4_ready"))
        stored = [sem(f"stored{j}") for j in range(2)]
        passed, sp_passed, act_passed = sem("f_passed"), sem("f_sp_passed"), sem("f_act_passed")
        NORM = 2 * B + 3

        def steps(eng, step):
            skewed(eng, NG, 3, 1, 1, 2, step)

        def blk(t, i, n=P):
            return t[:, i * n:(i + 1) * n]

        y_dram = results.rearrange("(r g i p) d -> p r g i d", r=2, i=B, p=P)
        out_dram = out.rearrange("(g i p) d -> p g i d", i=B, p=P)

        with nc.Block() as block:

            @block.sync
            def _(sp):
                def load(u, j):
                    g = 2 * u + j
                    when(sp, weighted_ready, 2 * B * (g - 1))
                    sp.sem_inc(sp_passed, 1)
                    for r in range(2):
                        sp.dma_start(y[r][j][:, :].rearrange("p (i d) -> p i d", d=P),
                                     y_dram[:, r, bass.ds(g, 1), :, :].rearrange("p g i d -> p (g i) d"))\
                          .then_inc(loaded[j], 16)

                def step(u, j, alive):
                    if alive(0):
                        load(u, j)
                steps(sp, step)

            @block.gpsimd
            def _(pool):
                pool.memset(minus_half[:, :], -0.5).then_inc(const_made, 1)
                pool.wait_ge(const_made, 1)

                def step(u, j, alive):
                    if alive(0):
                        g = 2 * u + j
                        pool.wait_ge(norm_step, NORM * (g + 1))
                        when(pool, x4_ready, B * (g - 1))
                        pool.tensor_tensor(rstd[j][:, :], var[j][:, :], minus_half[:, :], ALU.pow)\
                            .then_inc(rstd_ready, 1)
                steps(pool, step)

            @block.scalar
            def _(act):
                pairs = w_all[:, :].rearrange("p (g r i) -> p g r i", r=2, i=B)

                def weigh(u, j):
                    g = 2 * u + j
                    act.wait_ge(loaded[j], 32 * (u + 1))
                    when(act, norm_step, NORM * (g - 2) + 2)
                    for r in range(2):
                        for i in range(B):
                            act.activation(blk(weighted[r][j], i), blk(y[r][j], i), ACT.Copy,
                                           scale=pairs[:, bass.ds(g, 1), r, i:i + 1]
                                           .rearrange("p g i -> p (g i)")).then_inc(weighted_ready, 1)

                def store(u, j):
                    g = 2 * u + j
                    act.wait_ge(x4_ready, B * (g + 1))
                    act.sem_inc(act_passed, 1)
                    act.dma_start(out_dram[:, bass.ds(g, 1), :, :].rearrange("p g i d -> p (g i) d"),
                                  x4[j][:, :].rearrange("p (i d) -> p i d", d=P)).then_inc(stored[j], 16)

                def step(u, j, alive):
                    if alive(0):
                        weigh(u, j)
                    if alive(1):
                        store(*earlier(u, j, 1))
                steps(act, step)
                for j in range(2):
                    act.wait_ge(stored[j], 16 * NG // 2)

            @block.vector
            def _(dve):
                def add(u, j):
                    g = 2 * u + j
                    base = NORM * g
                    dve.wait_ge(weighted_ready, 2 * B * (g + 1))
                    when(dve, norm_step, base)
                    dve.tensor_tensor(part[:, :], weighted[0][j][:, :], x_all[:, bass.ds(g * S, S)], ALU.add)\
                        .then_inc(norm_step, 1)
                    dve.wait_ge(norm_step, base + 1)
                    when(dve, x4_ready, B * (g - 1))
                    dve.tensor_tensor(r4[j][:, :], part[:, :], weighted[1][j][:, :], ALU.add).then_inc(norm_step, 1)
                    dve.wait_ge(norm_step, base + 2)
                    for i in range(B):
                        dve.bn_stats(blk(stats, i, 6), blk(r4[j], i)).then_inc(norm_step, 1)
                    wait_alone(dve, norm_step, base + 2 + B, passed)
                    for i in range(B):
                        dve.bn_aggr(blk(mv[j], i, 2), blk(stats, i, 6)).then_inc(norm_step, 1)
                    dve.wait_ge(norm_step, base + 2 + 2 * B)
                    when(dve, rstd_ready, g - 1)
                    dve.tensor_scalar(var[j][:, :], mv[j][:, :].rearrange("p (i c) -> p i c", c=2)[:, :, 1], EPS,
                                      None, ALU.add).then_inc(norm_step, 1)

                def norm(u, j):
                    g = 2 * u + j
                    dve.wait_ge(rstd_ready, g + 1)
                    when(dve, stored[j], 16 * u)
                    for i in range(B):
                        dve.tensor_scalar(blk(x4[j], i), blk(r4[j], i), mv[j][:, 2 * i:2 * i + 1],
                                          rstd[j][:, i:i + 1], ALU.subtract, ALU.mult).then_inc(x4_ready, 1)

                def step(u, j, alive):
                    if alive(0):
                        add(u, j)
                    if alive(1):
                        norm(*earlier(u, j, 1))
                steps(dve, step)


def two_layers(nc, sh, x, xT, wqkv, wproj, bproj, gate_w, gate_b, expert_w, expert_b, wqT, wkT, bq, wv1, bv1,
               wp, bp, cT, wg, bg, w1, b1, w2, b2, out):
    with ExitStack() as ctx:
        def sb(name, shape):
            return ctx.enter_context(nc.sbuf_tensor(name, shape, F32))
        x_all = sb("x_all", [P, sh.tokens])
        ident = sb("ident", [P, P])
        ones = sb("ones", [1, P])
        w_all = sb("w_all", [P, 2 * sh.tiles])
        tile_expert = ctx.enter_context(nc.sbuf_tensor("tile_expert", [1, sh.listed_tiles], I32))
        tile_row = ctx.enter_context(nc.sbuf_tensor("tile_row", [1, sh.listed_tiles], I32))
        with ExitStack() as two_stages:
            xT_all = two_stages.enter_context(nc.sbuf_tensor("xT_all", [P, sh.tokens], F32))
            v_all = two_stages.enter_context(nc.sbuf_tensor("v_all", [P, sh.tiles * H * (DH + 1)], F32))
            layer0(nc, sh, x, xT, wqkv, wproj, bproj, gate_w, gate_b, expert_w, expert_b, wv1, bv1,
                   (x_all, xT_all, v_all, ident, ones))
            sa_all = ctx.enter_context(nc.sbuf_tensor("sa_all", [P, sh.tokens], F32, side="right"))
            attention1(nc, sh, wqT, wkT, bq, (xT_all, v_all, ident), sa_all)
        rows_dram = nc.dram_tensor("rows_dram", [E * sh.list_rows + E * P, ROW], F32).ap()
        results = nc.dram_tensor("results", [2 * sh.tokens, P], F32).ap()
        routing = (rows_dram, w_all, tile_expert, tile_row)
        route1(nc, sh, wp, bp, cT, (x_all, ident, ones), sa_all, routing)
        experts1(nc, sh, wg, bg, w1, b1, w2, b2, (x_all, ident, ones), routing, results)
        combine1(nc, sh, (x_all, ident, ones), w_all, results, out)


def laid_out(i):
    import numpy as np
    heads = i["L0_attn_Wqkv"].reshape(H, 3, DH, P)
    kqv = i["L1_attn_Wkqv"]
    hidden = i["L1_ffn_Wg"].shape[2]
    chunk = hidden // -(-hidden // P)
    x = i["L0_attn_x"].reshape(-1, P)
    made = {
        "x": x,
        "xT": x.T,
        "wqkv": np.concatenate([heads[:, 0].reshape(P, P), heads[:, 1].reshape(P, P),
                                heads[:, 2].transpose(1, 0, 2).reshape(P, P)], axis=0).T,
        "wproj": i["L0_attn_Wproj"].T,
        "bproj": i["L0_attn_bproj"].reshape(1, P),
        "gate_w": i["L0_ffn_gate_w"].T,
        "gate_b": i["L0_ffn_gate_b"].reshape(1, E),
        "expert_w": i["L0_ffn_expert_w"].transpose(1, 0, 2).reshape(P, E * P),
        "expert_b": i["L0_ffn_expert_b"],
        "wqT": kqv[:, :, P:2 * P].transpose(2, 0, 1).reshape(P, H * P),
        "wkT": kqv[:, :, 0:P].transpose(2, 0, 1).reshape(P, H * P),
        "bq": i["L1_attn_bkqv"][:, P:2 * P].T,
        "wv1": kqv[:, :, 2 * P:].transpose(1, 0, 2).reshape(P, P),
        "bv1": i["L1_attn_bkqv"][:, 2 * P:].reshape(1, P),
        "wp": i["L1_attn_Wp"],
        "bp": i["L1_attn_bp"].reshape(1, P),
        "cT": i["L1_ffn_centroid"].T,
        "wg": i["L1_ffn_Wg"].transpose(1, 0, 2).reshape(P, E * hidden),
        "bg": i["L1_ffn_bg"].reshape(1, -1),
        "w1": i["L1_ffn_W1"].transpose(1, 0, 2).reshape(P, E * hidden),
        "b1": i["L1_ffn_b1"].reshape(1, -1),
        "w2": i["L1_ffn_W2"].reshape(-1, chunk, P).transpose(1, 0, 2).reshape(chunk, -1),
        "b2": i["L1_ffn_b2"].reshape(1, -1),
    }
    return {name: np.ascontiguousarray(a) for name, a in made.items()}


def kernel(**inputs):
    import numpy as np
    import concourse.bacc as bacc
    from concourse import mybir as _mybir
    from concourse.bass_utils import run_bass_kernel_spmd

    inputs = {name: np.asarray(a) for name, a in inputs.items()}
    nc = bacc.Bacc("TRN2", target_bir_lowering=False, num_devices=1)
    batch, seq, _ = inputs["L0_attn_x"].shape
    sh = Shapes(batch * seq, seq, inputs["L1_ffn_Wg"].shape[2])
    arrays, args = {}, []
    for name, a in laid_out(inputs).items():
        arrays[f"in_{name}"] = a
        args.append(nc.dram_tensor(f"in_{name}", a.shape, _mybir.dt.from_np(a.dtype), kind="ExternalInput").ap())
    out = nc.dram_tensor("out_x", (batch * seq, P), _mybir.dt.float32, kind="ExternalOutput").ap()
    two_layers(nc, sh, *args, out)
    r = run_bass_kernel_spmd(nc, [arrays], core_ids=[0])
    return r.results[0]["out_x"].reshape(batch, seq, P)
```

```python
from contextlib import ExitStack

import concourse.bass as bass
from concourse import mybir

ALU = mybir.AluOpType
ACT = mybir.ActivationFunctionType
F32 = mybir.dt.float32
BF16 = mybir.dt.bfloat16
F16 = mybir.dt.float16
U32 = mybir.dt.uint32
I32 = mybir.dt.int32
AX_X = mybir.AxisListType.X

P = 128
H = 16
DH = P // H
E = 8
EPS = 1e-5
MASKED = -1e30


def when(eng, semaphore, count):
    if not isinstance(count, int) or count > 0:
        eng.wait_ge(semaphore, count)


def wait_alone(eng, semaphore, count, passed):
    eng.wait_ge(semaphore, count)
    eng.sem_inc(passed, 1)


class Shapes:

    def __init__(self, tokens, seq, hidden):
        self.tokens, self.seq, self.hidden = tokens, seq, hidden
        self.tiles = tokens // P
        self.blocks = seq // P
        self.batches = tokens // seq
        self.chunks = -(-hidden // P)
        self.chunk = hidden // self.chunks
        self.list_rows = tokens + P
        self.listed_tiles = 2 * self.tiles + E
        assert self.chunk * self.chunks == hidden and self.blocks == 4


def layer0(nc, sh, x, xT_in, wqkv, wproj, bproj, gate_w, gate_b, expert_w, expert_b, wv1, bv1,
           keep):
    x_all, xT_all, v_all, ident, ones = keep
    NP = sh.tiles // 2
    HH = H * H
    sems = []
    with ExitStack() as ctx:
        def sb(name, shape, dt=F32):
            return ctx.enter_context(nc.sbuf_tensor(name, shape, dt))

        def pb(name):
            return ctx.enter_context(nc.psum_tensor(name, [P, 4 * P], F32))

        def sem(name):
            sems.append(nc.alloc_semaphore(name))
            return sems[-1]

        wqkv_sb = sb("wqkv_sb", [P, 3 * P])
        wproj_sb = sb("wproj_sb", [P, P])
        bproj_sb = sb("bproj_sb", [1, P])
        gatew_sb = sb("gatew_sb", [P, E])
        gateb_sb = sb("gateb_sb", [1, E])
        expw_sb = sb("expw_sb", [P, E * P])
        expb_sb = sb("expb_sb", [E, P])
        wv1_sb = sb("wv1_sb", [P, P])
        bv1_sb = sb("bv1_sb", [1, P])
        iota = sb("iota", [P, E])
        minus_half = sb("minus_half", [P, 2])

        xT = [sb(f"xT{j}", [P, 2 * P]) for j in range(2)]
        qkv = [sb(f"qkv{j}", [P, 2 * 3 * P]) for j in range(2)]
        qk_prod = sb("qk_prod", [P, 2 * HH * DH])
        pv_prod = sb("pv_prod", [P, 2 * HH * DH])
        scores = sb("scores", [P, 2 * HH])
        score_max = sb("score_max", [P, 2 * H])
        shifted = sb("shifted", [P, 2 * HH])
        exps = sb("exps", [P, 2 * HH])
        exp_sum, exp_rec = sb("exp_sum", [P, 2 * H]), sb("exp_rec", [P, 2 * H])
        probs = sb("probs", [P, 2 * HH])
        attnT = sb("attnT", [P, 2 * P])
        r1 = sb("r1", [P, 2 * P])
        stats1, mv1, var1, rstd1 = sb("stats1", [P, 12]), sb("mv1", [P, 4]), sb("var1", [P, 2]), sb("rstd1", [P, 2])
        x1 = [sb(f"x1_{j}", [P, 2 * P]) for j in range(2)]
        x1T = sb("x1T", [P, 2 * P])
        top, top_idx, top_idxf = sb("top", [P, 16]), sb("top_idx", [P, 16], U32), sb("top_idxf", [P, 16])
        gdiff, gexp, gden, gw = sb("gdiff", [P, 2]), sb("gexp", [P, 2]), sb("gden", [P, 2]), sb("gw", [P, 4])
        gate1, gate2, gates = sb("gate1", [P, 2 * E]), sb("gate2", [P, 2 * E]), sb("gates", [P, 2 * E])
        gatesT = sb("gatesT", [E, 2 * P])
        gated = [sb(f"gated{a}", [P, E * P]) for a in range(2)]
        sum4, sum2, sum1 = sb("sum4", [P, 4 * P]), sb("sum2", [P, 2 * P]), sb("sum1", [P, P])
        acc = [sb(f"acc{j}", [P, 2 * P]) for j in range(2)]
        r2 = sb("r2", [P, 2 * P])
        stats2, mv2, var2, rstd2 = sb("stats2", [P, 12]), sb("mv2", [P, 4]), sb("var2", [P, 2]), sb("rstd2", [P, 2])
        x2 = [sb(f"x2_{j}", [P, 2 * P]) for j in range(2)]
        x2T = [sb(f"x2T{j}", [P, 2 * P]) for j in range(2)]

        ps_qkv = [pb(f"ps_qkv{a}") for a in range(2)]
        ps_turn = pb("ps_turn0")
        ps_keep = pb("ps_keep")
        ps_front = pb("ps_front0")
        ps_bias = pb("ps_bias")
        ps_y = [pb(f"ps_y{i}") for i in range(2)]
        ps_oT, ps_x1T, ps_gT = ps_turn[:, 0:2 * P], ps_turn[:, 2 * P:4 * P], ps_bias[0:E, 2 * P:4 * P]
        ps_x2T, ps_v = ps_keep[:, 0:2 * P], ps_keep[:, 2 * P:4 * P]
        ps_proj, ps_logits = ps_front[:, 0:2 * P], ps_front[:, 2 * P:2 * P + 2 * E]
        ps_eb = ps_bias[:, 0:2 * P]

        consts_made, passed, sp_passed = sem("consts_made"), sem("passed"), sem("sp_passed")
        ident_zeroed = sem("ident_zeroed")
        weights_in = sem("weights_in")
        x_in = [sem(f"x_in{j}") for j in range(2)]
        xT_loaded = [sem(f"xT_loaded{j}") for j in range(2)]
        x2_kept = [sem(f"x2_kept{j}") for j in range(2)]
        x2T_kept = [sem(f"x2T_kept{j}") for j in range(2)]
        qkv_ps, qkv_sb, qk_multiplied = sem("qkv_ps"), sem("qkv_sb"), sem("qk_multiplied")
        pv_multiplied, pv_summed, experts_summed = sem("pv_multiplied"), sem("pv_summed"), sem("experts_summed")
        x1_ready, x2_ready, v_sb = sem("x1_ready"), sem("x2_ready"), sem("v_sb")
        experts_ps, gated_ready = sem("experts_ps"), sem("gated_ready")
        scores_summed, max_found, scores_shifted = sem("scores_summed"), sem("max_found"), sem("scores_shifted")
        exps_ready, exps_summed, recips_ready = sem("exps_ready"), sem("exps_summed"), sem("recips_ready")
        probs_ready, oT_sb, proj_ps = sem("probs_ready"), sem("oT_sb"), sem("proj_ps")
        rstd1_ready, x1T_ps, x1T_sb, logits_ps = sem("rstd1_ready"), sem("x1T_ps"), sem("x1T_sb"), sem("logits_ps")
        gate_diff_ready, gate_exp_ready, gates_ready = sem("gate_diff_ready"), sem("gate_exp_ready"), sem("gates_ready")
        gT_ps, gT_sb, expert_bias_ps = sem("gT_ps"), sem("gT_sb"), sem("expert_bias_ps")
        rstd2_ready = sem("rstd2_ready")
        x2T_ps, x2T_sb, v_ps = sem("x2T_ps"), sem("x2T_sb"), sem("v_ps")
        norm1_step, norm2_step, gate_step, sum_step = (
            sem("norm1_step"), sem("norm2_step"), sem("gate_step"), sem("sum_step"))

        NWEIGHTS = 9
        NORM_STEPS = 6
        GATE_STEPS = 12
        SUM_STEPS = 3

        def steps(eng, step):
            def one(s):
                step(s // 2, s % 2, tuple(0 <= s + 1 - n < NP for n in range(5)))
            for s in range(5):
                one(s)
            with eng.Fori(2, NP // 2 - 1) as u:
                step(u, 1, (True,) * 5)
                step(u + 1, 0, (True,) * 5)
            for s in range(NP - 1, NP + 3):
                one(s)

        def before(u, j, k):
            return u + (j - k) // 2, (j - k) % 2

        x_tiles = x.rearrange("(t p) d -> p t d", p=P)
        x_sb = x_all[:, :].rearrange("p (t d) -> p t d", d=P)
        v_heads = v_all[:, :].rearrange("p (b h k c) -> p b h k c", h=H, k=sh.blocks, c=DH + 1)

        def tile(t, a, n=P):
            return t[:, a * n:(a + 1) * n]

        with nc.Block() as block:

            @block.sync
            def _(sp):
                def load(u, j):
                    s = 2 * u + j
                    when(sp, x_in[j], 16 * u)
                    sp.sem_inc(sp_passed, 1)
                    sp.dma_start(x_sb[:, bass.ds(2 * s, 2), :], x_tiles[:, bass.ds(2 * s, 2), :])\
                        .then_inc(x_in[j], 16)
                    when(sp, qkv_ps, 2 * (s - 1))
                    sp.sem_inc(sp_passed, 1)
                    sp.dma_start(xT[j][:, :], xT_in[:, bass.ds(s * 2 * P, 2 * P)]).then_inc(xT_loaded[j], 16)

                def keep_x2(u, j):
                    s = 2 * u + j
                    wait_alone(sp, x2_ready, 2 * (s + 1), sp_passed)
                    sp.dma_start(x_sb[:, bass.ds(2 * s, 2), :], x2[j][:, :].rearrange("p (a d) -> p a d", d=P))\
                        .then_inc(x2_kept[j], 16)
                    wait_alone(sp, x2T_sb, s + 1, sp_passed)
                    sp.dma_start(xT_all[:, bass.ds(s * 2 * P, 2 * P)], x2T[j][:, :]).then_inc(x2T_kept[j], 16)

                def step(u, j, part):
                    if part[0]:
                        load(*before(u, j, -1))
                    if part[4]:
                        keep_x2(*before(u, j, 3))
                sp.dma_start(wqkv_sb[:, :], wqkv).then_inc(weights_in, 16)
                load(0, 0)
                for dst, src in ((wproj_sb, wproj), (bproj_sb, bproj), (gatew_sb, gate_w),
                                 (gateb_sb, gate_b), (expw_sb, expert_w), (expb_sb, expert_b),
                                 (wv1_sb, wv1), (bv1_sb, bv1)):
                    sp.dma_start(dst[:, :], src).then_inc(weights_in, 16)
                steps(sp, step)
                for j in range(2):
                    sp.wait_ge(x2_kept[j], 16 * NP // 2)
                    sp.wait_ge(x2T_kept[j], 16 * NP // 2)

            @block.gpsimd
            def _(pool):
                pool.memset(v_all[:, :], 1.0).then_inc(consts_made, 1)
                pool.memset(ones[:, :], 1.0).then_inc(consts_made, 1)
                pool.memset(minus_half[:, :], -0.5).then_inc(consts_made, 1)
                pool.iota(iota[:, :], pattern=[[1, E]], base=0, channel_multiplier=0,
                          allow_small_or_imprecise_dtypes=True).then_inc(consts_made, 1)
                pool.memset(ident[:, :], 0.0).then_inc(ident_zeroed, 1)
                pool.wait_ge(ident_zeroed, 1)
                pool.affine_select(out=ident[:, :], in_=ident[:, :], compare_op=ALU.not_equal, fill=1.0,
                                   base=0, pattern=[[-1, P]], channel_multiplier=1).then_inc(consts_made, 1)
                pool.wait_ge(consts_made, 5)

                def inverse_deviation(u, j, step_sem, var, rstd, done):
                    s = 2 * u + j
                    pool.wait_ge(step_sem, NORM_STEPS * (s + 1))
                    pool.tensor_tensor(rstd[:, :], var[:, :], minus_half[:, :], ALU.pow).then_inc(done, 1)

                def pv_products(u, j):
                    s = 2 * u + j
                    pool.wait_ge(probs_ready, s + 1)
                    for a in range(2):
                        when(pool, pv_summed, 2 * (s - 1) + a + 1)
                        pool.tensor_tensor(
                            tile(pv_prod, a, HH * DH).rearrange("p (g h d) -> p g h d", g=H, d=DH),
                            tile(probs, a, HH).rearrange("p (h g) -> p g h", h=H).unsqueeze(3)
                            .to_broadcast([P, H, H, DH]),
                            qkv[j][:, (3 * a + 2) * P:(3 * a + 3) * P].rearrange("p (g d) -> p g d", d=DH)
                            .unsqueeze(2).to_broadcast([P, H, H, DH]), ALU.mult).then_inc(pv_multiplied, 1)

                def sum_experts(u, j, a):
                    s = 2 * u + j
                    when(pool, norm2_step, NORM_STEPS * (s - 2) + 1)
                    n = 2 * s + a
                    base = SUM_STEPS * n
                    pool.wait_ge(gated_ready, 2 * n + 2)
                    when(pool, experts_summed, n)
                    pool.tensor_tensor(sum4[:, :], gated[a][:, 0:4 * P], gated[a][:, 4 * P:8 * P],
                                       ALU.add).then_inc(sum_step, 1)
                    pool.wait_ge(sum_step, base + 1)
                    pool.tensor_tensor(sum2[:, :], sum4[:, 0:2 * P], sum4[:, 2 * P:4 * P],
                                       ALU.add).then_inc(sum_step, 1)
                    pool.wait_ge(sum_step, base + 2)
                    pool.tensor_tensor(sum1[:, :], sum2[:, 0:P], sum2[:, P:2 * P],
                                       ALU.add).then_inc(sum_step, 1)
                    pool.wait_ge(sum_step, base + 3)
                    pool.tensor_tensor(tile(acc[j], a), sum1[:, :], tile(x1[j], a), ALU.add)\
                        .then_inc(experts_summed, 1)

                def step(u, j, part):
                    if part[2]:
                        pv_products(*before(u, j, 1))
                    if part[4]:
                        inverse_deviation(*before(u, j, 3), norm2_step, var2, rstd2, rstd2_ready)
                    if part[3]:
                        sum_experts(*before(u, j, 2), 0)
                    if part[2]:
                        inverse_deviation(*before(u, j, 1), norm1_step, var1, rstd1, rstd1_ready)
                    if part[3]:
                        sum_experts(*before(u, j, 2), 1)
                steps(pool, step)

            @block.tensor
            def _(pe):
                pe.wait_ge(consts_made, 5)
                pe.wait_ge(weights_in, 16 * NWEIGHTS)

                def qkv_products(u, j):
                    s = 2 * u + j
                    pe.wait_ge(xT_loaded[j], 16 * (u + 1))
                    for a in range(2):
                        when(pe, qkv_sb, 2 * (s - 1) + a + 1)
                        pe.matmul(ps_qkv[a][:, 0:3 * P], tile(xT[j], a), wqkv_sb[:, :], start=True,
                                  stop=True).then_inc(qkv_ps, 1)

                def sum_heads(u, j, a):
                    s = 2 * u + j
                    pe.wait_ge(pv_multiplied, 2 * s + a + 1)
                    if a == 0:
                        when(pe, oT_sb, s)
                        when(pe, x1T_sb, s)
                    for g in range(H):
                        mm = pe.matmul(tile(ps_oT, a), tile(pv_prod, a * H + g), ident[:, :],
                                       start=(g == 0), stop=(g == H - 1))
                    mm.then_inc(pv_summed, 1)

                def project(u, j):
                    s = 2 * u + j
                    pe.wait_ge(oT_sb, s + 1)
                    when(pe, gates_ready, s)
                    for a in range(2):
                        pe.matmul(tile(ps_proj, a), tile(attnT, a), wproj_sb[:, :], start=True, stop=False)
                        mm = pe.matmul(tile(ps_proj, a), ones[0:1, 0:P], bproj_sb[:, :], start=False, stop=True)
                    mm.then_inc(proj_ps, 1)

                def four_experts(s, a, half):
                    when(pe, gated_ready, 4 * s + 2 * a + half - 1)
                    pe.matmul(ps_y[half][:, :], tile(x1T, a), expw_sb[:, half * 4 * P:(half + 1) * 4 * P],
                              start=True, stop=True).then_inc(experts_ps, 1)

                def logits_and_experts(u, j):
                    s = 2 * u + j
                    pe.wait_ge(x1_ready, 2 * (s + 1))
                    for a in range(2):
                        mm = pe.transpose(tile(ps_x1T, a), tile(x1[j], a), ident[:, :])
                    mm.then_inc(x1T_ps, 1)
                    pe.wait_ge(x1T_sb, s + 1)
                    for a in range(2):
                        pe.matmul(tile(ps_logits, a, E), tile(x1T, a), gatew_sb[:, :], start=True, stop=False)
                        mm = pe.matmul(tile(ps_logits, a, E), ones[0:1, 0:P], gateb_sb[:, :], start=False, stop=True)
                    mm.then_inc(logits_ps, 1)
                    four_experts(s, 0, 0)
                    four_experts(s, 0, 1)

                def turn_gates(u, j):
                    s = 2 * u + j
                    pe.wait_ge(gates_ready, s + 1)
                    when(pe, norm2_step, NORM_STEPS * (s - 1) + 1)
                    for a in range(2):
                        mm = pe.transpose(tile(ps_gT, a), tile(gates, a, E), ident[:, :])
                    mm.then_inc(gT_ps, 1)

                def experts_and_biases(u, j):
                    s = 2 * u + j
                    four_experts(s, 1, 0)
                    four_experts(s, 1, 1)
                    pe.wait_ge(gT_sb, s + 1)
                    for a in range(2):
                        mm = pe.matmul(tile(ps_eb, a), tile(gatesT, a), expb_sb[:, :], start=True, stop=True)
                    mm.then_inc(expert_bias_ps, 1)

                def values(u, j):
                    s = 2 * u + j
                    pe.wait_ge(x2_ready, 2 * (s + 1))
                    when(pe, v_sb, 2 * s)
                    for a in range(2):
                        mm = pe.transpose(tile(ps_x2T, a), tile(x2[j], a), ident[:, :])
                    mm.then_inc(x2T_ps, 1)
                    pe.wait_ge(x2T_sb, s + 1)
                    for a in range(2):
                        pe.matmul(tile(ps_v, a), tile(x2T[j], a), wv1_sb[:, :], start=True, stop=False)
                        mm = pe.matmul(tile(ps_v, a), ones[0:1, 0:P], bv1_sb[:, :], start=False, stop=True)
                    mm.then_inc(v_ps, 1)

                def step(u, j, part):
                    if part[3]:
                        logits_and_experts(*before(u, j, 2))
                    if part[2]:
                        sum_heads(*before(u, j, 1), 0)
                    if part[3]:
                        turn_gates(*before(u, j, 2))
                    if part[2]:
                        sum_heads(*before(u, j, 1), 1)
                        project(*before(u, j, 1))
                    if part[3]:
                        experts_and_biases(*before(u, j, 2))
                    if part[0]:
                        qkv_products(*before(u, j, -1))
                    if part[4]:
                        values(*before(u, j, 3))
                qkv_products(0, 0)
                steps(pe, step)

            @block.scalar
            def _(act):
                act.wait_ge(consts_made, 5)

                def copy_qkv(u, j):
                    s = 2 * u + j
                    when(act, qk_multiplied, 2 * (s - 1))
                    when(act, pv_multiplied, 2 * (s - 1))
                    for a in range(2):
                        act.wait_ge(qkv_ps, 2 * s + a + 1)
                        act.copy(tile(qkv[j], a, 3 * P), ps_qkv[a][:, 0:3 * P]).then_inc(qkv_sb, 1)

                def copy_oT(u, j):
                    s = 2 * u + j
                    act.wait_ge(pv_summed, 2 * (s + 1))
                    when(act, proj_ps, s)
                    act.copy(attnT[:, :], ps_oT).then_inc(oT_sb, 1)

                def exponentials(u, j):
                    s = 2 * u + j
                    act.wait_ge(scores_shifted, s + 1)
                    when(act, probs_ready, s)
                    act.activation(exps[:, :], shifted[:, :], ACT.Exp, scale=0.125).then_inc(exps_ready, 1)

                def copy_x1T(u, j):
                    s = 2 * u + j
                    act.wait_ge(x1T_ps, s + 1)
                    when(act, experts_ps, 4 * s)
                    act.copy(x1T[:, :], ps_x1T).then_inc(x1T_sb, 1)

                def gate_exp(u, j):
                    s = 2 * u + j
                    act.wait_ge(gate_diff_ready, s + 1)
                    act.activation(gexp[:, :], gdiff[:, :], ACT.Exp).then_inc(gate_exp_ready, 1)

                def apply_gates(u, j, a):
                    s = 2 * u + j
                    act.wait_ge(gates_ready, s + 1)
                    when(act, sum_step, SUM_STEPS * (2 * (s - 1) + a) + 1)
                    for half in range(2):
                        act.wait_ge(experts_ps, 4 * s + 2 * a + half + 1)
                        for e in range(4 * half, 4 * half + 4):
                            last = act.activation(tile(gated[a], e), tile(ps_y[half], e % 4), ACT.Copy,
                                                  scale=gates[:, a * E + e:a * E + e + 1])
                        last.then_inc(gated_ready, 1)

                def copy_gT(u, j):
                    s = 2 * u + j
                    act.wait_ge(gT_ps, s + 1)
                    when(act, expert_bias_ps, s)
                    act.copy(gatesT[:, :], ps_gT).then_inc(gT_sb, 1)

                def copy_x2T(u, j):
                    s = 2 * u + j
                    act.wait_ge(x2T_ps, s + 1)
                    when(act, v_ps, s - 1)
                    when(act, x2T_kept[j], 16 * u)
                    act.copy(x2T[j][:, :], ps_x2T).then_inc(x2T_sb, 1)

                def copy_v(u, j):
                    s = 2 * u + j
                    act.wait_ge(v_ps, s + 1)
                    for a in range(2):
                        act.copy(v_heads[:, bass.ds(u, 1), :, 2 * j + a:2 * j + a + 1, 0:DH]
                                 .rearrange("p b h k c -> p (b h k) c"),
                                 tile(ps_v, a).rearrange("p (h c) -> p h c", h=H)).then_inc(v_sb, 1)

                def step(u, j, part):
                    if part[3]:
                        copy_x1T(*before(u, j, 2))
                        gate_exp(*before(u, j, 2))
                        apply_gates(*before(u, j, 2), 0)
                        copy_gT(*before(u, j, 2))
                    if part[2]:
                        copy_oT(*before(u, j, 1))
                    if part[1]:
                        exponentials(u, j)
                    if part[3]:
                        apply_gates(*before(u, j, 2), 1)
                    if part[0]:
                        copy_qkv(*before(u, j, -1))
                    if part[4]:
                        copy_x2T(*before(u, j, 3))
                        copy_v(*before(u, j, 3))
                copy_qkv(0, 0)
                steps(act, step)

            @block.vector
            def _(dve):
                dve.wait_ge(consts_made, 5)

                def by_head(t, n=H):
                    return t[:, :].rearrange("p (h g) -> p h g", g=n)

                def qk_products(u, j, a):
                    s = 2 * u + j
                    when(dve, scores_summed, s)
                    dve.wait_ge(qkv_sb, 2 * s + a + 1)
                    dve.tensor_tensor(
                        tile(qk_prod, a, HH * DH).rearrange("p (h g d) -> p h g d", h=H, g=H),
                        qkv[j][:, 3 * a * P:(3 * a + 1) * P].rearrange("p (h d) -> p h d", h=H).unsqueeze(2)
                        .to_broadcast([P, H, H, DH]),
                        qkv[j][:, (3 * a + 1) * P:(3 * a + 2) * P].rearrange("p (g d) -> p g d", g=H)
                        .unsqueeze(1).to_broadcast([P, H, H, DH]), ALU.mult).then_inc(qk_multiplied, 1)

                def qk_sums(u, j):
                    s = 2 * u + j
                    dve.wait_ge(qk_multiplied, 2 * (s + 1))
                    when(dve, scores_shifted, s)
                    dve.tensor_reduce(scores[:, :], by_head(qk_prod, DH), AX_X, ALU.add).then_inc(scores_summed, 1)

                def find_max(u, j):
                    s = 2 * u + j
                    dve.wait_ge(scores_summed, s + 1)
                    dve.tensor_reduce(score_max[:, :], by_head(scores), AX_X, ALU.max).then_inc(max_found, 1)

                def shift_scores(u, j):
                    s = 2 * u + j
                    dve.wait_ge(max_found, s + 1)
                    when(dve, exps_ready, s)
                    dve.tensor_tensor(by_head(shifted), by_head(scores),
                                      score_max[:, :].unsqueeze(2).to_broadcast([P, 2 * H, H]),
                                      ALU.subtract).then_inc(scores_shifted, 1)

                def exp_sums(u, j):
                    s = 2 * u + j
                    dve.wait_ge(exps_ready, s + 1)
                    when(dve, recips_ready, s)
                    dve.tensor_reduce(exp_sum[:, :], by_head(exps), AX_X, ALU.add).then_inc(exps_summed, 1)

                def exp_recips(u, j):
                    s = 2 * u + j
                    dve.wait_ge(exps_summed, s + 1)
                    when(dve, probs_ready, s)
                    dve.reciprocal(exp_rec[:, :], exp_sum[:, :]).then_inc(recips_ready, 1)

                def normalise(u, j):
                    s = 2 * u + j
                    dve.wait_ge(recips_ready, s + 1)
                    when(dve, pv_multiplied, 2 * s)
                    dve.tensor_tensor(by_head(probs), by_head(exps),
                                      exp_rec[:, :].unsqueeze(2).to_broadcast([P, 2 * H, H]),
                                      ALU.mult).then_inc(probs_ready, 1)

                def statistics(s, rows, stats, mv, var, count):
                    base = NORM_STEPS * s
                    dve.wait_ge(count, base + 1)
                    for a in range(2):
                        dve.bn_stats(tile(stats, a, 6), tile(rows, a)).then_inc(count, 1)
                    for a in range(2):
                        wait_alone(dve, count, base + 2 + a, passed)
                        dve.bn_aggr(tile(mv, a, 2), tile(stats, a, 6)).then_inc(count, 1)
                    dve.wait_ge(count, base + 5)
                    dve.tensor_scalar(var[:, :], mv[:, :].rearrange("p (a c) -> p a c", c=2)[:, :, 1], EPS, None,
                                      ALU.add).then_inc(count, 1)

                def residual1(u, j):
                    s = 2 * u + j
                    dve.wait_ge(x_in[j], 16 * (u + 1))
                    dve.wait_ge(proj_ps, s + 1)
                    when(dve, x1_ready, 2 * s)
                    dve.tensor_tensor(r1[:, :].rearrange("p (a d) -> p a d", d=P), x_sb[:, bass.ds(2 * s, 2), :],
                                      ps_proj.rearrange("p (a d) -> p a d", d=P), ALU.add).then_inc(norm1_step, 1)
                    statistics(s, r1, stats1, mv1, var1, norm1_step)

                def norm1(u, j):
                    s = 2 * u + j
                    dve.wait_ge(rstd1_ready, s + 1)
                    when(dve, x1T_ps, s - 1)
                    when(dve, experts_summed, 2 * (s - 1))
                    for a in range(2):
                        dve.tensor_scalar(tile(x1[j], a), tile(r1, a), mv1[:, 2 * a:2 * a + 1],
                                          rstd1[:, a:a + 1], ALU.subtract, ALU.mult).then_inc(x1_ready, 1)

                def gate(u, j):
                    s = 2 * u + j
                    base = GATE_STEPS * s
                    tops = top[:, :].rearrange("p (a c) -> p a c", c=8)
                    dve.wait_ge(logits_ps, s + 1)
                    when(dve, gates_ready, s)
                    dve.sem_inc(passed, 1)
                    for a in range(2):
                        dve.max(tile(top, a, 8), tile(ps_logits, a, E)).then_inc(gate_step, 1)
                    dve.wait_ge(gate_step, base + 2)
                    dve.tensor_tensor(gdiff[:, :], tops[:, :, 1], tops[:, :, 0], ALU.subtract)\
                        .then_inc(gate_diff_ready, 1)
                    for a in range(2):
                        dve.max_index(tile(top_idx, a, 8), tile(top, a, 8), tile(ps_logits, a, E))\
                           .then_inc(gate_step, 1)
                    dve.wait_ge(gate_step, base + 4)
                    dve.tensor_copy(top_idxf[:, :], top_idx[:, :]).then_inc(gate_step, 1)
                    dve.wait_ge(gate_exp_ready, s + 1)
                    dve.tensor_scalar(gden[:, :], gexp[:, :], 1.0, None, ALU.add).then_inc(gate_step, 1)
                    dve.wait_ge(gate_step, base + 6)
                    dve.reciprocal(gw[:, 0:2], gden[:, :]).then_inc(gate_step, 1)
                    dve.wait_ge(gate_step, base + 7)
                    dve.tensor_tensor(gw[:, 2:4], gexp[:, :], gw[:, 0:2], ALU.mult).then_inc(gate_step, 1)
                    for rank, spread in ((0, gate1), (1, gate2)):
                        if rank == 1:
                            dve.wait_ge(gate_step, base + 8)
                        for a in range(2):
                            dve.tensor_scalar(tile(spread, a, E), iota[:, :],
                                              top_idxf[:, 8 * a + rank:8 * a + rank + 1],
                                              gw[:, 2 * rank + a:2 * rank + a + 1], ALU.is_equal, ALU.mult)\
                               .then_inc(gate_step, 1)
                    dve.wait_ge(gate_step, base + 12)
                    when(dve, gT_ps, s)
                    when(dve, gated_ready, 4 * s)
                    dve.tensor_tensor(gates[:, :], gate1[:, :], gate2[:, :], ALU.add).then_inc(gates_ready, 1)

                def residual2(u, j):
                    s = 2 * u + j
                    dve.wait_ge(experts_summed, 2 * (s + 1))
                    dve.wait_ge(expert_bias_ps, s + 1)
                    when(dve, x2_ready, 2 * s)
                    dve.tensor_tensor(r2[:, :], acc[j][:, :], ps_eb, ALU.add).then_inc(norm2_step, 1)
                    statistics(s, r2, stats2, mv2, var2, norm2_step)

                def norm2(u, j):
                    s = 2 * u + j
                    dve.wait_ge(rstd2_ready, s + 1)
                    when(dve, x2T_ps, s - 1)
                    when(dve, x2_kept[j], 16 * u)
                    for a in range(2):
                        dve.tensor_scalar(tile(x2[j], a), tile(r2, a), mv2[:, 2 * a:2 * a + 1],
                                          rstd2[:, a:a + 1], ALU.subtract, ALU.mult).then_inc(x2_ready, 1)

                def step(u, j, part):
                    if part[1]:
                        qk_products(u, j, 0)
                    if part[4]:
                        residual2(*before(u, j, 3))
                    if part[1]:
                        qk_products(u, j, 1)
                    if part[3]:
                        gate(*before(u, j, 2))
                    if part[1]:
                        qk_sums(u, j)
                    if part[4]:
                        norm2(*before(u, j, 3))
                    if part[1]:
                        find_max(u, j)
                        shift_scores(u, j)
                    if part[2]:
                        residual1(*before(u, j, 1))
                    if part[1]:
                        exp_sums(u, j)
                        exp_recips(u, j)
                    if part[2]:
                        norm1(*before(u, j, 1))
                    if part[1]:
                        normalise(u, j)
                steps(dve, step)

    nc.clear_and_free_semaphores(sems)
    nc.all_engine_barrier()


def attention1(nc, sh, wqT, wkT, bq, keep, sa_all):
    xT_all, v_all, ident = keep
    S, B = sh.seq, sh.blocks
    NK = sh.batches * H
    PV = DH + 1
    PARTS = 3
    RAISE = 2.0 ** 15
    SCALE = float(P) ** -0.5
    with ExitStack() as ctx:
        def sb(name, shape, dt=F32):
            return ctx.enter_context(nc.sbuf_tensor(name, shape, dt))

        def sem(name):
            return ctx.enter_context(nc.semaphore(name))

        wq = sb("wq_sb", [P, H * P])
        wk = sb("wk_sb", [P, H * P])
        bq_sb = sb("bq_sb", [P, H])
        m_all = sb("m_all", [P, H * P])
        mb_all = sb("mb_all", [P, H])
        m_head = [sb(f"m_head{j}", [P, P]) for j in range(2)]
        ident16 = sb("ident16", [P, P], BF16)
        mask16 = sb("mask16", [P, P], BF16)
        qm = [sb(f"qm{j}", [P, S]) for j in range(2)]
        neg_max = sb("neg_max", [P, B])
        probs = [sb(f"p{i}", [P, (i + 1) * P]) for i in range(B)]
        leadT = [sb(f"leadT{i}", [P, (i + 1) * P], F16) for i in range(B)]
        restT = [sb(f"restT{i}", [P, (i + 1) * P], F16) for i in range(B)]
        v_parts = [sb(f"v_parts{j}", [P, B * PARTS * PV], BF16) for j in range(2)]
        v_rest = sb("v_rest", [P, B * PV])
        out_sum, recip = sb("out_sum", [P, B * PV]), sb("recip", [P, B])

        ps_s = [ctx.enter_context(nc.psum_tensor(f"ps_s{i}", [P, S], F32)) for i in range(B)]
        ps_t = [ctx.enter_context(nc.psum_tensor(f"ps_t{i}", [P, S], F32)) for i in range(2)]
        ps_qm = ctx.enter_context(nc.psum_tensor("ps_qm", [P, S], F32))
        ps_o = ctx.enter_context(nc.psum_tensor("ps_o", [P, S], F32))
        out_ps = ps_o[:, 0:B * PARTS * PV].rearrange("p (i n) -> p i n", n=PARTS * PV)

        weights_in = sem("b_weights_in")
        consts_zeroed, consts_made = sem("b_consts_zeroed"), sem("b_consts_made")
        m_ps, m_sb = sem("m_ps"), sem("m_sb")
        mb_ps, mb_sb = sem("mb_ps"), sem("mb_sb")
        m_head_ready = sem("m_head_ready")
        qm_ps, qm_sb = sem("qm_ps"), sem("qm_sb")
        scores_ps = [sem(f"scores_ps{i}") for i in range(B)]
        max_ready = [sem(f"max_ready{i}") for i in range(B)]
        probs_ready = [sem(f"probs_ready{i}") for i in range(B)]
        pT_ps = [sem(f"pT_ps{i}") for i in range(B)]
        lead_ready = [sem(f"lead_ready{i}") for i in range(B)]
        rest_ready = [sem(f"rest_ready{i}") for i in range(B)]
        v_rest_step, v_parts_ready, out_summed = sem("v_rest_step"), sem("v_parts_ready"), sem("out_summed")
        passed = sem("b_passed")
        out_block = [sem(f"out_block{i}") for i in range(B)]
        recips_ready, out_ready = sem("b_recips_ready"), sem("out_ready")

        def steps(step):
            def one(k):
                step(k // 2, k % 2, k + 1 < NK, k >= 1, k < NK)
            def run(eng):
                for k in range(4):
                    one(k)
                with eng.Fori(1, NK // 4 - 1) as v:
                    for j in range(4):
                        step(2 * v + j // 2, j % 2, True, True, True)
                for k in range(NK - 4, NK + 1):
                    one(k)
            return run

        def before(u, j, k):
            return u + (j - k) // 2, (j - k) % 2

        sa_steps = sa_all[:, :].rearrange("p (k i c) -> p k i c", i=B, c=DH)

        def sequence(u):
            return u // (H // 2)

        with nc.Block() as block:

            @block.sync
            def _(sp):
                sp.dma_start(wq[:, :], wqT).then_inc(weights_in, 16)
                sp.dma_start(wk[:, :], wkT).then_inc(weights_in, 16)
                sp.dma_start(bq_sb[:, :], bq).then_inc(weights_in, 16)

            @block.gpsimd
            def _(pool):
                pool.memset(mask16[:, :], 0.0).then_inc(consts_zeroed, 1)
                pool.tensor_copy(ident16[:, :], ident[:, :]).then_inc(consts_made, 1)
                pool.wait_ge(consts_zeroed, 1)
                pool.affine_select(out=mask16[:, :], in_=mask16[:, :], compare_op=ALU.is_ge, fill=MASKED,
                                   base=0, pattern=[[-1, P]], channel_multiplier=1).then_inc(consts_made, 1)
                pool.wait_ge(m_sb, H // 4)

                def load_head(u, j):
                    k = 2 * u + j
                    when(pool, qm_ps, k - 1)
                    pool.tensor_copy(m_head[j][:, :], m_all[:, bass.ds((k % H) * P, P)])\
                        .then_inc(m_head_ready, 1)

                def split_values(u, j):
                    k = 2 * u + j
                    parts = v_parts[j][:, :].rearrange("p (i s c) -> p i s c", s=PARTS, c=PV)
                    rest = v_rest[:, :].rearrange("p (i c) -> p i c", c=PV)
                    values = v_all[:, bass.ds(k * B * PV, B * PV)].rearrange("p (i c) -> p i c", c=PV)
                    when(pool, out_block[0], k - 1)
                    pool.sem_inc(passed, 1)
                    pool.tensor_copy(parts[:, :, 0, :], values).then_inc(v_parts_ready, 1)
                    wait_alone(pool, v_parts_ready, 3 * k + 1, passed)
                    pool.tensor_tensor(rest, values, parts[:, :, 0, :], ALU.subtract).then_inc(v_rest_step, 1)
                    wait_alone(pool, v_rest_step, k + 1, passed)
                    pool.tensor_copy(parts[:, :, 1, :], rest).then_inc(v_parts_ready, 1)
                    pool.wait_ge(v_parts_ready, 3 * k + 2)
                    pool.tensor_tensor(parts[:, :, 2, :], rest, parts[:, :, 1, :], ALU.subtract)\
                        .then_inc(v_parts_ready, 1)

                def step(u, j, nxt, last, this):
                    if nxt:
                        load_head(*before(u, j, -1))
                        split_values(*before(u, j, -1))
                load_head(0, 0)
                split_values(0, 0)
                steps(step)(pool)

            @block.tensor
            def _(pe):
                pe.wait_ge(weights_in, 48)
                for g in range(H // 4):
                    for h in range(4 * g, 4 * g + 4):
                        mm = pe.matmul(ps_s[g][:, (h % 4) * P:(h % 4 + 1) * P], wq[:, h * P:(h + 1) * P],
                                       wk[:, h * P:(h + 1) * P], start=True, stop=True)
                    mm.then_inc(m_ps, 1)
                for h in range(H):
                    mm = pe.matmul(ps_qm[:, h:h + 1], wk[:, h * P:(h + 1) * P], bq_sb[:, h:h + 1],
                                   start=True, stop=True)
                mm.then_inc(mb_ps, 1)
                pe.wait_ge(consts_made, 2)
                pe.wait_ge(m_sb, H // 4)
                pe.wait_ge(mb_sb, 1)

                def queries(u, j):
                    k = 2 * u + j
                    pe.wait_ge(m_head_ready, k + 1)
                    when(pe, qm_sb, k)
                    pe.matmul(ps_qm[:, :], m_head[j][:, :], xT_all[:, bass.ds(sequence(u) * S, S)],
                              start=True, stop=True).then_inc(qm_ps, 1)

                def scores(u, j, i):
                    k = 2 * u + j
                    pe.wait_ge(qm_sb, k + 1)
                    when(pe, probs_ready[i], k)
                    n = (i + 1) * P
                    pe.matmul(ps_s[i][:, 0:n], qm[j][:, i * P:n], xT_all[:, bass.ds(sequence(u) * S, n)],
                              start=True, stop=False)
                    pe.matmul(ps_s[i][:, i * P:n], ident16[:, :], mask16[:, :], start=False, stop=True)\
                        .then_inc(scores_ps[i], 1)

                def turn(u, j, i):
                    k = 2 * u + j
                    pe.wait_ge(probs_ready[i], k + 1)
                    if i < 2:
                        pe.wait_ge(rest_ready[i + 2], k + 1)
                    else:
                        when(pe, rest_ready[i - 2], k)
                    for n in range(i + 1):
                        mm = pe.transpose(ps_t[i % 2][:, n * P:(n + 1) * P], probs[i][:, n * P:(n + 1) * P],
                                          ident[:, :])
                    mm.then_inc(pT_ps[i], 1)

                def weighted_values(u, j, i):
                    k = 2 * u + j
                    pe.wait_ge(rest_ready[i], k + 1)
                    if i == B - 1:
                        pe.wait_ge(v_parts_ready, 3 * (k + 1))
                        when(pe, out_summed, k)
                    for n in range(i + 1):
                        for part in (leadT[i], restT[i]):
                            mm = pe.matmul(out_ps[:, i, :], part[:, n * P:(n + 1) * P],
                                           v_parts[j][:, n * PARTS * PV:(n + 1) * PARTS * PV],
                                           start=(n == 0 and part is leadT[i]), stop=(n == i and part is restT[i]))
                    mm.then_inc(out_block[i], 1)

                def step(u, j, nxt, last, this):
                    b = before(u, j, 1)
                    if last:
                        turn(*b, 3)
                        turn(*b, 2)
                    if this:
                        scores(u, j, 3)
                        scores(u, j, 2)
                    if last:
                        turn(*b, 1)
                    if nxt:
                        queries(*before(u, j, -1))
                    if last:
                        turn(*b, 0)
                    if this:
                        scores(u, j, 1)
                        scores(u, j, 0)
                    if last:
                        for i in reversed(range(B)):
                            weighted_values(*b, i)
                queries(0, 0)
                steps(step)(pe)

            @block.scalar
            def _(act):
                for g in range(H // 4):
                    act.wait_ge(m_ps, g + 1)
                    act.copy(m_all[:, g * 4 * P:(g + 1) * 4 * P], ps_s[g][:, :]).then_inc(m_sb, 1)
                act.wait_ge(mb_ps, 1)
                act.mul(mb_all[:, :], ps_qm[:, 0:H], SCALE).then_inc(mb_sb, 1)
                act.wait_ge(mb_sb, 1)

                def copy_queries(u, j):
                    k = 2 * u + j
                    act.wait_ge(qm_ps, k + 1)
                    when(act, scores_ps[0], k - 1)
                    act.activation(qm[j][:, :], ps_qm[:, :], ACT.Identity,
                                   bias=mb_all[:, bass.ds(k % H, 1)], scale=SCALE).then_inc(qm_sb, 1)

                def exponentials(u, j, i):
                    k = 2 * u + j
                    act.wait_ge(max_ready[i], k + 1)
                    when(act, pT_ps[i], k)
                    act.activation(probs[i][:, :], ps_s[i][:, 0:(i + 1) * P], ACT.Exp,
                                   bias=neg_max[:, i:i + 1]).then_inc(probs_ready[i], 1)

                def copy_lead(u, j, i):
                    k = 2 * u + j
                    act.wait_ge(pT_ps[i], k + 1)
                    when(act, out_block[i], k)
                    act.activation(leadT[i][:, :], ps_t[i % 2][:, 0:(i + 1) * P], ACT.Copy, scale=RAISE)\
                       .then_inc(lead_ready[i], 1)

                def step(u, j, nxt, last, this):
                    b = before(u, j, 1)
                    if last:
                        copy_lead(*b, 3)
                        copy_lead(*b, 2)
                        copy_lead(*b, 1)
                    if this:
                        exponentials(u, j, 3)
                        exponentials(u, j, 2)
                    if last:
                        copy_lead(*b, 0)
                    if nxt:
                        copy_queries(*before(u, j, -1))
                    if this:
                        exponentials(u, j, 1)
                        exponentials(u, j, 0)
                copy_queries(0, 0)
                steps(step)(act)

            @block.vector
            def _(dve):
                def row_max(u, j, i):
                    k = 2 * u + j
                    dve.wait_ge(scores_ps[i], k + 1)
                    dve.tensor_reduce(neg_max[:, i:i + 1], ps_s[i][:, 0:(i + 1) * P], AX_X, ALU.max,
                                      negate=True).then_inc(max_ready[i], 1)

                def take_rest(u, j, i):
                    k = 2 * u + j
                    dve.wait_ge(lead_ready[i], k + 1)
                    when(dve, out_block[i], k)
                    dve.scalar_tensor_tensor(out=restT[i][:, :], in0=ps_t[i % 2][:, 0:(i + 1) * P], scalar=RAISE,
                                             in1=leadT[i][:, :], op0=ALU.mult, op1=ALU.subtract)\
                       .then_inc(rest_ready[i], 1)

                def normalise(u, j):
                    k = 2 * u + j
                    sums = out_sum[:, :].rearrange("p (i c) -> p i c", c=PV)
                    dve.wait_ge(out_block[0], k + 1)
                    when(dve, out_ready, k)
                    dve.tensor_reduce(sums, out_ps.rearrange("p i (s c) -> p i c s", s=PARTS), AX_X, ALU.add)\
                       .then_inc(out_summed, 1)
                    dve.wait_ge(out_summed, k + 1)
                    dve.reciprocal(recip[:, :], sums[:, :, DH]).then_inc(recips_ready, 1)
                    dve.wait_ge(recips_ready, k + 1)
                    dve.tensor_tensor(sa_steps[:, bass.ds(k, 1), :, :].rearrange("p k i c -> p (k i) c"),
                                      sums[:, :, 0:DH], recip[:, :].unsqueeze(2).to_broadcast([P, B, DH]),
                                      ALU.mult).then_inc(out_ready, 1)

                def step(u, j, nxt, last, this):
                    b = before(u, j, 1)
                    if last:
                        take_rest(*b, 3)
                    if this:
                        row_max(u, j, 3)
                    if last:
                        take_rest(*b, 2)
                    if this:
                        row_max(u, j, 2)
                    if last:
                        take_rest(*b, 1)
                        take_rest(*b, 0)
                    if this:
                        row_max(u, j, 1)
                        row_max(u, j, 0)
                    if last:
                        normalise(*b)
                steps(step)(dve)


def skewed(eng, n, begin, ahead, depth, stride, step):
    def one(s):
        step(s // stride, s % stride, lambda p: 0 <= s - p < n)
    whole = (n - ahead - begin) // stride * stride
    for s in range(begin):
        one(s)
    first, j0 = begin // stride, begin % stride
    with eng.Fori(first, first + whole // stride) as u:
        for j in range(j0, j0 + stride):
            step(u + j // stride, j % stride, lambda p: True)
    for s in range(begin + whole, n + depth):
        one(s)


def earlier(u, j, p, stride=2):
    return u + (j - p) // stride, (j - p) % stride


ROW = P + 1
NOWHERE = 1 << 22


def route1(nc, sh, wp, bp, cT, keep, sa_all, routing, expert_loads):
    x_all, ident, ones = keep
    rows_dram, squares_all, tile_expert, tile_row = routing
    B, S = sh.blocks, sh.seq
    NG, NT, LIST, TILES = sh.batches, sh.tiles, sh.list_rows, sh.listed_tiles
    with ExitStack() as ctx:
        def sb(name, shape, dt=F32):
            return ctx.enter_context(nc.sbuf_tensor(name, shape, dt))

        def sem(name):
            return ctx.enter_context(nc.semaphore(name))

        wp_sb, bp_sb = sb("wp_sb", [P, P]), sb("bp_sb", [1, P])
        cT_sb, cT2, csq_in, csq = sb("cT_sb", [P, E]), sb("cT2", [P, E]), sb("csq_in", [P, E]), sb("csq", [1, E])
        ones_col = sb("ones_col", [P, 1])
        iota = sb("r_iota", [P, B * E])
        list_base = sb("list_base", [P, E])
        place_in_tile = sb("place_in_tile", [P, 1])
        minus_half = sb("r_minus_half", [P, B])
        before16, ones16 = sb("before16", [P, P], BF16), sb("ones16", [P, P], BF16)
        ids = [sb(f"ids{r}", [P, NT], U32) for r in range(2)]
        filler = sb("filler", [P, ROW])

        sa_tile, saT, r3 = sb("sa_tile", [P, S]), sb("saT", [P, S]), sb("r3", [P, S])
        stats3, mv3 = sb("stats3", [P, B * 6]), sb("mv3", [P, B * 2])
        var3, rstd3 = sb("var3", [P, B]), sb("rstd3", [P, B])
        x3 = [sb(f"x3_{j}", [P, S]) for j in range(2)]
        x3T = sb("x3T", [P, S])
        square, norm_sq = sb("square", [P, P]), [sb(f"norm_sq{j}", [P, B]) for j in range(2)]
        dist2 = [sb(f"dist2_{j}", [P, B * E]) for j in range(2)]
        top, top_idx, top_idxf = sb("r_top", [P, B * 8]), sb("r_top_idx", [P, B * 8], U32), sb("r_top_idxf", [P, B * 8])
        picked = [[sb(f"picked{r}_{j}", [P, B * E]) for j in range(2)] for r in range(2)]
        picked16 = sb("picked16", [P, B * E], BF16)
        base = sb("base", [P, E])
        place, masked = sb("place", [P, B * E]), sb("masked", [P, B * E])
        slot, slot_idx = sb("slot", [P, 2 * B]), [sb(f"slot_idx{j}", [P, 2 * B], U32) for j in range(2)]
        rows = [[sb(f"rows{r}_{j}", [P, B * ROW]) for j in range(2)] for r in range(2)]
        pad_place, pad_idx = sb("pad_place", [P, E]), sb("pad_idx", [P, E], U32)
        t_f, t_i = sb("t_f", [1, 5 * E]), sb("t_i", [1, 2 * E], I32)
        number = sb("number", [1, TILES])
        passed_end, end_terms = sb("passed_end", [1, E * TILES]), sb("end_terms", [1, E * TILES])
        sum_f = sb("sum_f", [1, 3 * TILES])

        def pb(name):
            return ctx.enter_context(nc.psum_tensor(name, [P, S], F32))
        ps_saT, ps_proj, ps_x3T, ps_dist, ps_place, ps_csq = (
            pb("r_saT"), pb("r_proj"), pb("r_x3T"), pb("r_dist"), pb("r_place"), pb("r_csq"))

        weights_in, filler_stored, experts_in = sem("r_weights_in"), sem("filler_stored"), sem("experts_in")
        consts_begun, consts_made = sem("r_consts_begun"), sem("r_consts")
        c_squared, csq_ps, c_ready = sem("c_squared"), sem("csq_ps"), sem("c_ready")
        sa_copied, saT_ps, saT_sb, proj_ps = sem("sa_copied"), sem("saT_ps"), sem("saT_sb"), sem("r_proj_ps")
        norm3_step, rstd3_ready, x3_ready = sem("norm3_step"), sem("rstd3_ready"), sem("x3_ready")
        x3_kept = [sem(f"x3_kept{j}") for j in range(2)]
        x3T_ps, x3T_sb, squared, dist_ps, dist2_ready = (
            sem("x3T_ps"), sem("x3T_sb"), sem("squared"), sem("dist_ps"), sem("dist2_ready"))
        pick_step, picked_ready, place_ps, place_step, slots_ready = (
            sem("pick_step"), sem("picked_ready"), sem("place_ps"), sem("place_step"), sem("slots_ready"))
        rows_ready = sem("rows_ready")
        scattered = [sem(f"scattered{j}") for j in range(2)]
        pads_ready, pads_scattered, table_step = sem("pads_ready"), sem("pads_scattered"), sem("table_step")
        passed, sp_passed, pool_passed = sem("r_passed"), sem("r_sp_passed"), sem("r_pool_passed")
        slot_step = sem("slot_step")

        NORM = 2 * B + 2
        PICK = 2 * B + 4
        PLACE = 4

        def steps(eng, step):
            skewed(eng, NG, 5, 1, 3, 2, step)

        def blk(t, i, n=P):
            return t[:, i * n:(i + 1) * n]

        def by_tile(t, n):
            return t[:, :].rearrange("p (i c) -> p i c", c=n)

        sa_groups = sa_all[:, :].rearrange("p (g h i c) -> p g h i c", h=H, i=B, c=DH)

        with nc.Block() as block:

            @block.sync
            def _(sp):
                for dst, src in ((wp_sb, wp), (bp_sb, bp), (cT_sb, cT)):
                    sp.dma_start(dst[:, :], src).then_inc(weights_in, 16)
                sp.wait_ge(consts_made, 9)
                for n in range(E):
                    sp.dma_start(rows_dram[E * LIST + n * P:E * LIST + (n + 1) * P, :], filler[:, :])\
                      .then_inc(filler_stored, 16)

                for dst, src in expert_loads:
                    sp.dma_start(dst[:, :], src).then_inc(experts_in, 16)

                def keep_x3(u, j):
                    g = 2 * u + j
                    wait_alone(sp, x3_ready, B * (g + 1), sp_passed)
                    sp.dma_start(x_all[:, bass.ds(g * S, S)], x3[j][:, :]).then_inc(x3_kept[j], 16)

                def step(u, j, alive):
                    if alive(1):
                        keep_x3(*earlier(u, j, 1))
                steps(sp, step)
                sp.wait_ge(filler_stored, 16 * E)
                sp.wait_ge(experts_in, 16 * len(expert_loads))
                for j in range(2):
                    sp.wait_ge(x3_kept[j], 16 * NG // 2)

            @block.gpsimd
            def _(pool):
                pool.iota(iota[:, :], pattern=[[0, B], [1, E]], base=0, channel_multiplier=0,
                          allow_small_or_imprecise_dtypes=True).then_inc(consts_made, 1)
                pool.iota(place_in_tile[:, :], pattern=[[0, 1]], base=0, channel_multiplier=1,
                          allow_small_or_imprecise_dtypes=True).then_inc(consts_made, 1)
                for r in range(2):
                    pool.iota(ids[r][:, :], pattern=[[P, NT]], base=r * sh.tokens, channel_multiplier=1)\
                        .then_inc(consts_made, 1)
                pool.iota(number[:, :], pattern=[[1, TILES]], base=0, channel_multiplier=0,
                          allow_small_or_imprecise_dtypes=True).then_inc(consts_made, 1)
                pool.memset(minus_half[:, :], -0.5).then_inc(consts_made, 1)
                pool.memset(ones_col[:, :], 1.0).then_inc(consts_made, 1)
                pool.memset(ones16[:, :], 1.0).then_inc(consts_begun, 1)
                pool.memset(filler[:, 0:P], 0.0).then_inc(consts_begun, 1)
                pool.memset(filler[:, P:ROW].bitcast(U32), NOWHERE).then_inc(consts_begun, 1)
                pool.wait_ge(consts_begun, 3)
                pool.affine_select(out=before16[:, :], in_=ones16[:, :], compare_op=ALU.is_ge, fill=0.0,
                                   base=-1, pattern=[[1, P]], channel_multiplier=-1).then_inc(consts_made, 1)
                pool.wait_ge(consts_made, 1)
                pool.tensor_scalar(list_base[:, :], iota[:, 0:E], float(LIST), 0.0, ALU.mult, ALU.add)\
                    .then_inc(consts_made, 1)
                pool.wait_ge(consts_made, 9)

                def inverse3(u, j):
                    g = 2 * u + j
                    pool.wait_ge(norm3_step, NORM * (g + 1))
                    pool.tensor_tensor(rstd3[:, :], var3[:, :], minus_half[:, :], ALU.pow).then_inc(rstd3_ready, 1)

                def scatter(u, j):
                    g = 2 * u + j
                    pool.wait_ge(slots_ready, g + 1)
                    wait_alone(pool, rows_ready, 4 * (g + 1), pool_passed)
                    for r in range(2):
                        for i in range(B):
                            pool.indirect_dma_start(
                                out=rows_dram[:, :], out_offset=bass.IndirectOffsetOnAxis(
                                    ap=slot_idx[j][:, r * B + i:r * B + i + 1], axis=0),
                                in_=blk(rows[r][j], i, ROW), in_offset=None).then_inc(scattered[j], 16)

                def step(u, j, alive):
                    if alive(0):
                        inverse3(u, j)
                    if alive(3):
                        scatter(*earlier(u, j, 3))
                steps(pool, step)
                pool.wait_ge(pads_ready, 2)
                for e in range(E):
                    pool.indirect_dma_start(
                        out=rows_dram[:, :], out_offset=bass.IndirectOffsetOnAxis(ap=pad_idx[:, e:e + 1], axis=0),
                        in_=filler[:, :], in_offset=None).then_inc(pads_scattered, 16)
                for j in range(2):
                    pool.wait_ge(scattered[j], 16 * 2 * B * NG // 2)
                pool.wait_ge(pads_scattered, 16 * E)

            @block.tensor
            def _(pe):
                pe.wait_ge(weights_in, 48)
                pe.wait_ge(consts_made, 9)
                pe.wait_ge(c_squared, 2)
                pe.matmul(ps_csq[0:1, 0:E], ones_col[:, :], csq_in[:, :], start=True, stop=True).then_inc(csq_ps, 1)
                pe.wait_ge(c_ready, 1)

                def turn_sa(u, j):
                    g = 2 * u + j
                    pe.wait_ge(sa_copied, g + 1)
                    when(pe, saT_sb, g)
                    for i in range(B):
                        mm = pe.transpose(blk(ps_saT, i), blk(sa_tile, i), ident[:, :])
                    mm.then_inc(saT_ps, 1)

                def project(u, j):
                    g = 2 * u + j
                    pe.wait_ge(saT_sb, g + 1)
                    when(pe, norm3_step, NORM * (g - 1) + 1)
                    for i in range(B):
                        pe.matmul(blk(ps_proj, i), blk(saT, i), wp_sb[:, :], start=True, stop=False)
                        mm = pe.matmul(blk(ps_proj, i), ones[0:1, 0:P], bp_sb[:, :], start=False, stop=True)
                    mm.then_inc(proj_ps, 1)

                def turn_x3(u, j):
                    g = 2 * u + j
                    pe.wait_ge(x3_ready, B * (g + 1))
                    when(pe, x3T_sb, g)
                    for i in range(B):
                        mm = pe.transpose(blk(ps_x3T, i), blk(x3[j], i), ident[:, :])
                    mm.then_inc(x3T_ps, 1)

                def centroid_products(u, j):
                    g = 2 * u + j
                    pe.wait_ge(x3T_sb, g + 1)
                    when(pe, dist2_ready, B * g)
                    for i in range(B):
                        pe.matmul(blk(ps_dist, i, E), blk(x3T, i), cT2[:, :], start=True, stop=False)
                        mm = pe.matmul(blk(ps_dist, i, E), ones[0:1, 0:P], csq[:, :], start=False, stop=True)
                    mm.then_inc(dist_ps, 1)

                def count(u, j):
                    g = 2 * u + j
                    pe.wait_ge(picked_ready, g + 1)
                    when(pe, place_step, PLACE * (g - 1) + 2)
                    for i in range(B + 1):
                        for n in range(i):
                            mm = pe.matmul(blk(ps_place, i, E), ones16[:, :], blk(picked16, n, E),
                                           start=(n == 0), stop=(i == B and n == B - 1))
                        if i < B:
                            mm = pe.matmul(blk(ps_place, i, E), before16[:, :], blk(picked16, i, E),
                                           start=(i == 0), stop=True)
                    mm.then_inc(place_ps, 1)

                def step(u, j, alive):
                    if alive(0):
                        turn_sa(u, j)
                    if alive(1):
                        turn_x3(*earlier(u, j, 1))
                    if alive(0):
                        project(u, j)
                    if alive(1):
                        centroid_products(*earlier(u, j, 1))
                    if alive(2):
                        count(*earlier(u, j, 2))
                steps(pe, step)

            @block.scalar
            def _(act):
                act.wait_ge(consts_made, 9)

                def copy_sa(u, j):
                    g = 2 * u + j
                    when(act, saT_ps, g)
                    act.copy(sa_tile[:, :].rearrange("p (i h c) -> p h i c", h=H, c=DH),
                             sa_groups[:, bass.ds(g, 1), :, :, :].rearrange("p g h i c -> p (g h) i c"))\
                       .then_inc(sa_copied, 1)

                def copy_saT(u, j):
                    g = 2 * u + j
                    act.wait_ge(saT_ps, g + 1)
                    when(act, proj_ps, g)
                    act.copy(saT[:, :], ps_saT[:, :]).then_inc(saT_sb, 1)

                def copy_x3T(u, j):
                    g = 2 * u + j
                    act.wait_ge(x3T_ps, g + 1)
                    when(act, dist_ps, g)
                    act.copy(x3T[:, :], ps_x3T[:, :]).then_inc(x3T_sb, 1)

                def square_rows(u, j):
                    g = 2 * u + j
                    act.wait_ge(x3_ready, B * (g + 1))
                    when(act, dist2_ready, B * (g - 1))
                    for i in range(B):
                        when(act, squared, B * g + i)
                        act.activation(square[:, :], blk(x3[j], i), ACT.Square,
                                       accum_out=norm_sq[j][:, i:i + 1]).then_inc(squared, 1)

                def make_rows(u, j):
                    g = 2 * u + j
                    act.wait_ge(x3_kept[j], 16 * (u + 1))
                    when(act, scattered[j], 16 * 2 * B * u)
                    for r in range(2):
                        out = by_tile(rows[r][j], ROW)
                        act.copy(out[:, :, 0:P], x_all[:, bass.ds(g * S, S)].rearrange("p (i d) -> p i d", d=P))\
                           .then_inc(rows_ready, 1)
                        act.copy(out[:, :, P].bitcast(U32), ids[r][:, bass.ds(g * B, B)]).then_inc(rows_ready, 1)

                def step(u, j, alive):
                    if alive(3):
                        make_rows(*earlier(u, j, 3))
                    if alive(0):
                        copy_saT(u, j)
                    if alive(-1):
                        copy_sa(*earlier(u, j, -1))
                    if alive(1):
                        square_rows(*earlier(u, j, 1))
                        copy_x3T(*earlier(u, j, 1))
                copy_sa(0, 0)
                steps(act, step)

            @block.vector
            def _(dve):
                dve.wait_ge(weights_in, 48)
                dve.wait_ge(consts_made, 9)
                dve.tensor_scalar(cT2[:, :], cT_sb[:, :], -2.0, None, ALU.mult).then_inc(c_squared, 1)
                dve.tensor_tensor(csq_in[:, :], cT_sb[:, :], cT_sb[:, :], ALU.mult).then_inc(c_squared, 1)
                dve.tensor_copy(base[:, :], list_base[:, :]).then_inc(c_ready, 1)
                dve.wait_ge(csq_ps, 1)
                dve.tensor_copy(csq[:, :], ps_csq[0:1, 0:E]).then_inc(c_ready, 1)
                dve.wait_ge(c_ready, 2)

                def residual(u, j):
                    g = 2 * u + j
                    dve.wait_ge(proj_ps, g + 1)
                    when(dve, x3_ready, B * g)
                    dve.tensor_tensor(r3[:, :], x_all[:, bass.ds(g * S, S)], ps_proj[:, :], ALU.add)\
                        .then_inc(norm3_step, 1)
                    dve.wait_ge(norm3_step, NORM * g + 1)
                    for i in range(B):
                        dve.bn_stats(blk(stats3, i, 6), blk(r3, i)).then_inc(norm3_step, 1)
                    wait_alone(dve, norm3_step, NORM * g + 1 + B, passed)
                    for i in range(B):
                        dve.bn_aggr(blk(mv3, i, 2), blk(stats3, i, 6)).then_inc(norm3_step, 1)
                    dve.wait_ge(norm3_step, NORM * g + 1 + 2 * B)
                    dve.tensor_scalar(var3[:, :], by_tile(mv3, 2)[:, :, 1], EPS, None, ALU.add)\
                       .then_inc(norm3_step, 1)

                def norm3(u, j):
                    g = 2 * u + j
                    dve.wait_ge(rstd3_ready, g + 1)
                    when(dve, x3T_ps, g - 1)
                    when(dve, squared, B * (g - 1))
                    when(dve, x3_kept[j], 16 * u)
                    for i in range(B):
                        dve.tensor_scalar(blk(x3[j], i), blk(r3, i), mv3[:, 2 * i:2 * i + 1], rstd3[:, i:i + 1],
                                          ALU.subtract, ALU.mult).then_inc(x3_ready, 1)

                def square_distances(u, j):
                    g = 2 * u + j
                    dve.wait_ge(dist_ps, g + 1)
                    dve.wait_ge(squared, B * (g + 1))
                    for i in range(B):
                        dve.tensor_scalar(blk(dist2[j], i, E), blk(ps_dist, i, E), norm_sq[j][:, i:i + 1], 1e-12,
                                          ALU.add, ALU.max).then_inc(dist2_ready, 1)

                tops, idxs = by_tile(top, 8), by_tile(top_idxf, 8)

                def pick(u, j):
                    g = 2 * u + j
                    base_count = PICK * g
                    dve.wait_ge(dist2_ready, B * (g + 1))
                    when(dve, picked_ready, g)
                    dve.sem_inc(passed, 1)
                    for i in range(B):
                        dve.max(blk(top, i, 8), blk(dist2[j], i, E)).then_inc(pick_step, 1)
                    dve.wait_ge(pick_step, base_count + B)
                    dve.tensor_copy(squares_all[:, bass.ds(g * 2 * B, 2 * B)].rearrange("p (i r) -> p i r", r=2),
                                    tops[:, :, 0:2]).then_inc(pick_step, 1)
                    for i in range(B):
                        dve.max_index(blk(top_idx, i, 8), blk(top, i, 8), blk(dist2[j], i, E)).then_inc(pick_step, 1)
                    dve.wait_ge(pick_step, base_count + 2 * B + 1)
                    dve.tensor_copy(top_idxf[:, :], top_idx[:, :]).then_inc(pick_step, 1)
                    dve.wait_ge(pick_step, base_count + 2 * B + 2)
                    when(dve, place_step, PLACE * (g - 1))
                    for r in range(2):
                        dve.tensor_tensor(by_tile(picked[r][j], E), by_tile(iota, E),
                                          idxs[:, :, r:r + 1].to_broadcast([P, B, E]), ALU.is_equal)\
                           .then_inc(pick_step, 1)
                    dve.wait_ge(pick_step, base_count + 2 * B + 4)
                    when(dve, place_ps, g)
                    dve.tensor_tensor(picked16[:, :], picked[0][j][:, :], picked[1][j][:, :], ALU.add)\
                       .then_inc(picked_ready, 1)

                def find_places(u, j):
                    g = 2 * u + j
                    count = PLACE * g
                    dve.wait_ge(place_ps, g + 1)
                    when(dve, slots_ready, g)
                    dve.tensor_tensor(by_tile(place, E), ps_place[:, 0:B * E].rearrange("p (i c) -> p i c", c=E),
                                      base[:, :].unsqueeze(1).to_broadcast([P, B, E]), ALU.add)\
                       .then_inc(place_step, 1)
                    dve.wait_ge(place_step, count + 1)
                    dve.tensor_tensor(base[:, :], base[:, :], ps_place[:, B * E:(B + 1) * E], ALU.add)\
                       .then_inc(place_step, 1)
                    for r in range(2):
                        when(dve, slot_step, 4 * g + 2 * r)
                        dve.tensor_tensor(masked[:, :], place[:, :], picked[r][j][:, :], ALU.mult)\
                           .then_inc(slot_step, 1)
                        dve.wait_ge(slot_step, 4 * g + 2 * r + 1)
                        dve.tensor_reduce(blk(slot, r, B), by_tile(masked, E), AX_X, ALU.add).then_inc(slot_step, 1)
                    dve.wait_ge(slot_step, 4 * g + 4)
                    dve.wait_ge(place_step, count + 2)
                    dve.sem_inc(place_step, 2)
                    when(dve, scattered[j], 16 * 2 * B * u)
                    dve.tensor_copy(slot_idx[j][:, :], slot[:, :]).then_inc(slots_ready, 1)

                def step(u, j, alive):
                    if alive(1):
                        norm3(*earlier(u, j, 1))
                    if alive(2):
                        pick(*earlier(u, j, 2))
                    if alive(0):
                        residual(u, j)
                    if alive(3):
                        find_places(*earlier(u, j, 3))
                    if alive(1):
                        square_distances(*earlier(u, j, 1))
                steps(dve, step)

                dve.wait_ge(place_step, PLACE * NG)
                dve.tensor_scalar(pad_place[:, :], base[:, :], place_in_tile[:, :], None, ALU.add)\
                    .then_inc(pads_ready, 1)
                dve.wait_ge(pads_ready, 1)
                dve.tensor_copy(pad_idx[:, :], pad_place[:, :]).then_inc(pads_ready, 1)

                count, tiles, end, jump = (t_f[:, n * E:(n + 1) * E] for n in range(4))
                one = t_f[:, 4 * E:5 * E]
                dve.tensor_tensor(count, base[0:1, :], list_base[0:1, :], ALU.subtract).then_inc(table_step, 1)
                dve.memset(one, 1.0).then_inc(table_step, 1)
                dve.wait_ge(table_step, 2)
                dve.tensor_scalar(t_i[:, 0:E], count, float(P - 1), None, ALU.add).then_inc(table_step, 1)
                dve.wait_ge(table_step, 3)
                dve.tensor_scalar(t_i[:, E:2 * E], t_i[:, 0:E], P.bit_length() - 1, None,
                                  ALU.arith_shift_right).then_inc(table_step, 1)
                dve.wait_ge(table_step, 4)
                dve.tensor_copy(tiles, t_i[:, E:2 * E]).then_inc(table_step, 1)
                dve.wait_ge(table_step, 5)
                dve.tensor_tensor_scan(end, one, tiles, 0.0, ALU.mult, ALU.add).then_inc(table_step, 1)
                dve.tensor_scalar(jump, tiles, float(-P), float(LIST), ALU.mult, ALU.add).then_inc(table_step, 1)
                dve.wait_ge(table_step, 7)
                by_expert = passed_end[:, :].rearrange("p (e n) -> p e n", e=E)
                dve.tensor_tensor(by_expert, number[:, :].unsqueeze(1).to_broadcast([1, E, TILES]),
                                  end.unsqueeze(2).to_broadcast([1, E, TILES]), ALU.is_ge).then_inc(table_step, 1)
                dve.wait_ge(table_step, 8)
                dve.tensor_tensor(end_terms[:, :].rearrange("p (e n) -> p e n", e=E), by_expert,
                                  jump.unsqueeze(2).to_broadcast([1, E, TILES]), ALU.mult).then_inc(table_step, 1)
                expert_f, moved, row_f = (sum_f[:, n * TILES:(n + 1) * TILES] for n in range(3))
                dve.tensor_reduce(expert_f, passed_end[:, :].rearrange("p (e n) -> p n e", e=E), AX_X, ALU.add)\
                   .then_inc(table_step, 1)
                dve.wait_ge(table_step, 10)
                dve.tensor_reduce(moved, end_terms[:, :].rearrange("p (e n) -> p n e", e=E), AX_X, ALU.add)\
                   .then_inc(table_step, 1)
                dve.tensor_scalar(tile_expert[:, :], expert_f, float(E - 1), None, ALU.min).then_inc(table_step, 1)
                dve.wait_ge(table_step, 12)
                dve.scalar_tensor_tensor(out=row_f, in0=number[:, :], scalar=float(P), in1=moved, op0=ALU.mult,
                                         op1=ALU.add).then_inc(table_step, 1)
                dve.wait_ge(table_step, 13)
                dve.tensor_copy(tile_row[:, :], row_f).then_inc(table_step, 1)


def experts1(nc, sh, weights, ident, routing, dist_all, results):
    wg_sb, w1_sb, w2_sb, bg_sb, b1_sb, b2_sb = weights
    rows_dram, squares_all, tile_expert, tile_row = routing
    C, CH, HID, TILES, LIST = sh.chunks, sh.chunk, sh.hidden, sh.listed_tiles, sh.list_rows
    with ExitStack() as ctx:
        def sb(name, shape, dt=F32):
            return ctx.enter_context(nc.sbuf_tensor(name, shape, dt))

        def sem(name):
            return ctx.enter_context(nc.semaphore(name))

        D2 = 2 * sh.blocks
        half = sb("half", [P, D2])
        assert TILES // 8 >= sh.batches
        R = 8
        row_in = [sb(f"row_in{r}", [P, ROW]) for r in range(R)]
        row_out = [sb(f"row_out{r}", [P, P]) for r in range(R)]
        xT = [sb(f"e_xT{j}", [P, P]) for j in range(2)]
        gate = [sb(f"e_gate{j}", [P, HID]) for j in range(2)]
        silu = [sb(f"e_silu{j}", [P, HID]) for j in range(2)]
        up = [sb(f"e_up{j}", [P, HID]) for j in range(2)]
        hid = [sb(f"e_hid{j}", [P, HID]) for j in range(2)]
        hidT = [sb(f"e_hidT{j}", [CH, C * P]) for j in range(2)]

        def pb(name):
            return ctx.enter_context(nc.psum_tensor(name, [P, 4 * P], F32))
        ps_x, ps_h, ps_y = pb("e_ps_x"), pb("e_ps_h"), pb("e_ps_y")
        ps_g, ps_u = [pb(f"e_ps_g{j}") for j in range(2)], [pb(f"e_ps_u{j}") for j in range(2)]

        row_loaded = [sem(f"row_loaded{r}") for r in range(R)]
        sent = [sem(f"sent{r}") for r in range(R)]
        xT_ps, xT_sb, gate_ps, up_ps = sem("e_xT_ps"), sem("e_xT_sb"), sem("e_gate_ps"), sem("e_up_ps")
        gate_sb, silu_ready, up_sb, hid_ready = sem("e_gate_sb"), sem("e_silu"), sem("e_up_sb"), sem("e_hid")
        hT_ps, hT_sb, y_ps, y_sb = sem("e_hT_ps"), sem("e_hT_sb"), sem("e_y_ps"), sem("e_y_sb")
        half_made, dist_ready = sem("half_made"), sem("dist_ready")
        sp_passed, pool_passed = sem("e_sp_passed"), sem("e_pool_passed")

        def steps(eng, step):
            skewed(eng, TILES, R, 1, 3, R, step)

        def back(u, r, p):
            return earlier(u, r, p, R)

        def expert_of(eng, n):
            return eng.value_load(tile_expert[0:1, bass.ds(n, 1)], min_val=0, max_val=E - 1)

        with nc.Block() as block:

            @block.sync
            def _(sp):
                def load(u, r):
                    n = R * u + r
                    row = sp.value_load(tile_row[0:1, bass.ds(n, 1)], min_val=0, max_val=E * LIST + (E - 1) * P)
                    when(sp, sent[r], 16 * u)
                    sp.sem_inc(sp_passed, 1)
                    when(sp, xT_ps, n - R + 1)
                    sp.sem_inc(sp_passed, 1)
                    sp.dma_start(row_in[r][:, :], rows_dram[bass.ds(row, P), :]).then_inc(row_loaded[r], 16)

                def step(u, r, alive):
                    if alive(0):
                        load(u, r)
                for r in range(R):
                    load(0, r)
                with sp.Fori(1, TILES // R) as u:
                    for r in range(R):
                        load(u, r)

            @block.gpsimd
            def _(pool):
                def send(u, r):
                    n = R * u + r
                    wait_alone(pool, y_sb, n + 1, pool_passed)
                    pool.indirect_dma_start(
                        out=results[:, :], out_offset=bass.IndirectOffsetOnAxis(
                            ap=row_in[r][:, P:ROW].bitcast(U32), axis=0),
                        in_=row_out[r][:, :], in_offset=None, bounds_check=2 * sh.tokens - 1,
                        oob_is_err=False).then_inc(sent[r], 16)

                def distances(g):
                    pool.tensor_tensor(dist_all[:, bass.ds(g * D2, D2)], squares_all[:, bass.ds(g * D2, D2)],
                                       half[:, :], ALU.pow).then_inc(dist_ready, 1)

                def step(u, r, alive):
                    if alive(2):
                        send(*back(u, r, 2))
                    if r == 4 and alive(r) and not (isinstance(u, int) and u >= sh.batches):
                        distances(u)
                pool.memset(half[:, :], 0.5).then_inc(half_made, 1)
                pool.wait_ge(half_made, 1)
                steps(pool, step)
                pool.wait_ge(dist_ready, sh.batches)
                for r in range(R):
                    pool.wait_ge(sent[r], 16 * TILES // R)

            @block.tensor
            def _(pe):
                def turn_rows(u, r):
                    n = R * u + r
                    pe.wait_ge(row_loaded[r], 16 * (u + 1))
                    when(pe, xT_sb, n)
                    pe.transpose(ps_x[:, 0:P], row_in[r][:, 0:P], ident[:, :]).then_inc(xT_ps, 1)

                experts = {}

                def load_expert(u, p):
                    experts[-p % R] = expert_of(pe, R * u - p)

                def load_next(u, r):
                    if r + 1 < R:
                        experts[r + 1] = expert_of(pe, R * u + r + 1)

                def hidden(u, r):
                    n = R * u + r
                    j = r % 2
                    e = experts[r]
                    pe.wait_ge(xT_sb, n + 1)
                    when(pe, gate_sb, n - 1)
                    pe.matmul(ps_g[j][:, 0:HID], xT[j][:, :], wg_sb[:, bass.ds(e * HID, HID)], start=True,
                              stop=True).then_inc(gate_ps, 1)
                    when(pe, up_sb, n - 1)
                    pe.matmul(ps_u[j][:, 0:HID], xT[j][:, :], w1_sb[:, bass.ds(e * HID, HID)], start=True,
                              stop=True).then_inc(up_ps, 1)

                def turn_hidden(u, r):
                    n = R * u + r
                    pe.wait_ge(hid_ready, n + 1)
                    when(pe, hT_sb, n)
                    for c in range(C):
                        mm = pe.transpose(ps_h[0:CH, c * P:(c + 1) * P], hid[r % 2][:, c * CH:(c + 1) * CH],
                                          ident[:, :])
                    mm.then_inc(hT_ps, 1)

                def down(u, r):
                    n = R * u + r
                    e = experts[r]
                    pe.wait_ge(hT_sb, n + 1)
                    when(pe, y_sb, n)
                    for c in range(C):
                        mm = pe.matmul(ps_y[:, 0:P], hidT[r % 2][:, c * P:(c + 1) * P],
                                       w2_sb[:, bass.ds(e * C * P + c * P, P)], start=(c == 0), stop=(c == C - 1))
                    mm.then_inc(y_ps, 1)

                def step(u, r, alive):
                    if r == 0 and alive(0):
                        load_expert(u, 0)
                    if alive(0):
                        hidden(u, r)
                    if alive(-1):
                        turn_rows(*back(u, r, -1))
                    if r < 2 and alive(2):
                        load_expert(u, 2 - r)
                    if alive(2):
                        down(*back(u, r, 2))
                    if alive(-1):
                        load_next(u, r)
                    if alive(1):
                        turn_hidden(*back(u, r, 1))
                turn_rows(0, 0)
                steps(pe, step)

            @block.scalar
            def _(act):
                def copy_xT(u, r):
                    n = R * u + r
                    act.wait_ge(xT_ps, n + 1)
                    when(act, up_ps, n - 1)
                    act.copy(xT[r % 2][:, :], ps_x[:, 0:P]).then_inc(xT_sb, 1)

                def apply_silu(u, r):
                    n = R * u + r
                    act.wait_ge(gate_sb, n + 1)
                    when(act, hid_ready, n - 1)
                    act.activation(silu[r % 2][:, :], gate[r % 2][:, :], ACT.Silu).then_inc(silu_ready, 1)

                def copy_hT(u, r):
                    n = R * u + r
                    act.wait_ge(hT_ps, n + 1)
                    when(act, y_ps, n - 1)
                    act.copy(hidT[r % 2][:, :], ps_h[0:CH, 0:C * P]).then_inc(hT_sb, 1)

                def step(u, r, alive):
                    if alive(-1):
                        copy_xT(*back(u, r, -1))
                    if alive(0):
                        apply_silu(u, r)
                    if alive(1):
                        copy_hT(*back(u, r, 1))
                copy_xT(0, 0)
                steps(act, step)

            @block.vector
            def _(dve):
                def add_biases(u, r):
                    n = R * u + r
                    j = r % 2
                    e = expert_of(dve, n)
                    dve.wait_ge(gate_ps, n + 1)
                    when(dve, silu_ready, n - 1)
                    dve.tensor_tensor(gate[j][:, :], ps_g[j][:, 0:HID], bg_sb[:, bass.ds(e * HID, HID)],
                                      ALU.add).then_inc(gate_sb, 1)
                    dve.wait_ge(up_ps, n + 1)
                    when(dve, hid_ready, n - 1)
                    dve.tensor_tensor(up[j][:, :], ps_u[j][:, 0:HID], b1_sb[:, bass.ds(e * HID, HID)],
                                      ALU.add).then_inc(up_sb, 1)

                def multiply(u, r):
                    n = R * u + r
                    j = r % 2
                    dve.wait_ge(up_sb, n + 1)
                    dve.wait_ge(silu_ready, n + 1)
                    when(dve, hT_ps, n - 1)
                    dve.tensor_tensor(hid[j][:, :], up[j][:, :], silu[j][:, :], ALU.mult).then_inc(hid_ready, 1)

                def finish(u, r):
                    n = R * u + r
                    e = expert_of(dve, n)
                    dve.wait_ge(y_ps, n + 1)
                    when(dve, sent[r], 16 * u)
                    dve.tensor_tensor(row_out[r][:, :], ps_y[:, 0:P], b2_sb[:, bass.ds(e * P, P)],
                                      ALU.add).then_inc(y_sb, 1)

                def step(u, r, alive):
                    if alive(0):
                        add_biases(u, r)
                    if alive(2):
                        finish(*back(u, r, 2))
                    if alive(0):
                        multiply(u, r)
                steps(dve, step)


def combine1(nc, sh, x_all, dist_all, results, out):
    B, S, NG = sh.blocks, sh.seq, sh.batches
    with ExitStack() as ctx:
        def sb(name, shape, dt=F32):
            return ctx.enter_context(nc.sbuf_tensor(name, shape, dt))

        def sem(name):
            return ctx.enter_context(nc.semaphore(name))

        minus_half = sb("f_minus_half", [P, B])
        w_all = sb("w_all", [P, 2 * sh.tiles])
        wdiff, wexp, wden = (sb(n, [P, sh.tiles]) for n in ("wdiff", "wexp", "wden"))
        y = [[sb(f"y{r}_{j}", [P, S]) for j in range(4)] for r in range(2)]
        weighted = [[sb(f"weighted{r}_{j}", [P, S]) for j in range(2)] for r in range(2)]
        part, r4 = sb("f_part", [P, S]), [sb(f"r4_{j}", [P, S]) for j in range(2)]
        stats, mv = sb("f_stats", [P, B * 6]), [sb(f"f_mv{j}", [P, B * 2]) for j in range(2)]
        var, rstd = [sb(f"f_var{j}", [P, B]) for j in range(2)], [sb(f"f_rstd{j}", [P, B]) for j in range(2)]
        x4 = [sb(f"x4_{j}", [P, S]) for j in range(2)]

        const_made, wdiff_ready, wexp_ready, weights_step = (
            sem("f_const"), sem("wdiff_ready"), sem("wexp_ready"), sem("weights_step"))
        loaded = [sem(f"y_loaded{j}") for j in range(4)]
        weighted_ready, norm_step, rstd_ready, x4_ready = (
            sem("weighted_ready"), sem("f_norm_step"), sem("f_rstd_ready"), sem("x4_ready"))
        stored = [sem(f"stored{j}") for j in range(4)]
        passed, sp_passed = sem("f_passed"), sem("f_sp_passed")
        NORM = 2 * B + 3

        def steps(eng, step):
            skewed(eng, NG, 4, 2, 1, 4, step)

        def blk(t, i, n=P):
            return t[:, i * n:(i + 1) * n]

        y_dram = results.rearrange("(r g i p) d -> p r g i d", r=2, i=B, p=P)
        out_dram = out.rearrange("(g i p) d -> p g i d", i=B, p=P)

        with nc.Block() as block:

            @block.sync
            def _(sp):
                def load(u, j):
                    g = 4 * u + j
                    when(sp, weighted_ready, 2 * B * (g - 3))
                    sp.sem_inc(sp_passed, 1)
                    for r in range(2):
                        sp.dma_start(y[r][j][:, :].rearrange("p (i d) -> p i d", d=P),
                                     y_dram[:, r, bass.ds(g, 1), :, :].rearrange("p g i d -> p (g i) d"))\
                          .then_inc(loaded[j], 16)

                def store(u, j):
                    g = 4 * u + j
                    sp.wait_ge(x4_ready, B * (g + 1))
                    sp.sem_inc(sp_passed, 1)
                    sp.dma_start(out_dram[:, bass.ds(g, 1), :, :].rearrange("p g i d -> p (g i) d"),
                                  x4[j % 2][:, :].rearrange("p (i d) -> p i d", d=P)).then_inc(stored[j], 16)

                def step(u, j, alive):
                    if alive(-2):
                        load(*earlier(u, j, -2, 4))
                    if alive(1):
                        store(*earlier(u, j, 1, 4))
                load(0, 0)
                load(0, 1)
                steps(sp, step)
                for j in range(4):
                    sp.wait_ge(stored[j], 16 * NG // 4)

            @block.gpsimd
            def _(pool):
                pool.memset(minus_half[:, :], -0.5).then_inc(const_made, 1)
                pool.wait_ge(const_made, 1)

                def step(u, j, alive):
                    if alive(0):
                        g = 4 * u + j
                        pool.wait_ge(norm_step, NORM * (g + 1))
                        when(pool, x4_ready, B * (g - 1))
                        pool.tensor_tensor(rstd[j % 2][:, :], var[j % 2][:, :], minus_half[:, :], ALU.pow)\
                            .then_inc(rstd_ready, 1)
                steps(pool, step)

            @block.scalar
            def _(act):
                act.wait_ge(wdiff_ready, 1)
                act.activation(wexp[:, :], wdiff[:, :], ACT.Exp).then_inc(wexp_ready, 1)
                act.wait_ge(weights_step, 3)

                def weigh(u, j):
                    g = 4 * u + j
                    act.wait_ge(loaded[j], 32 * (u + 1))
                    when(act, norm_step, NORM * (g - 2) + 2)
                    for r in range(2):
                        for i in range(B):
                            act.activation(blk(weighted[r][j % 2], i), blk(y[r][j], i), ACT.Copy,
                                           scale=w_all[:, bass.ds((g * B + i) * 2 + r, 1)])\
                               .then_inc(weighted_ready, 1)

                def step(u, j, alive):
                    if alive(0):
                        weigh(u, j)
                steps(act, step)

            @block.vector
            def _(dve):
                dists, weights = (t[:, :].rearrange("p (t r) -> p t r", r=2) for t in (dist_all, w_all))
                dve.tensor_tensor(wdiff[:, :], dists[:, :, 1], dists[:, :, 0], ALU.subtract).then_inc(wdiff_ready, 1)
                dve.wait_ge(wexp_ready, 1)
                dve.tensor_scalar(wden[:, :], wexp[:, :], 1.0, None, ALU.add).then_inc(weights_step, 1)
                dve.wait_ge(weights_step, 1)
                dve.reciprocal(weights[:, :, 0], wden[:, :]).then_inc(weights_step, 1)
                dve.wait_ge(weights_step, 2)
                dve.tensor_tensor(weights[:, :, 1], wexp[:, :], weights[:, :, 0], ALU.mult).then_inc(weights_step, 1)

                def add(u, j):
                    g = 4 * u + j
                    base = NORM * g
                    dve.wait_ge(weighted_ready, 2 * B * (g + 1))
                    when(dve, norm_step, base)
                    dve.tensor_tensor(part[:, :], weighted[0][j % 2][:, :], x_all[:, bass.ds(g * S, S)], ALU.add)\
                        .then_inc(norm_step, 1)
                    dve.wait_ge(norm_step, base + 1)
                    when(dve, x4_ready, B * (g - 1))
                    dve.tensor_tensor(r4[j % 2][:, :], part[:, :], weighted[1][j % 2][:, :], ALU.add)\
                       .then_inc(norm_step, 1)
                    dve.wait_ge(norm_step, base + 2)
                    for i in range(B):
                        dve.bn_stats(blk(stats, i, 6), blk(r4[j % 2], i)).then_inc(norm_step, 1)
                    wait_alone(dve, norm_step, base + 2 + B, passed)
                    for i in range(B):
                        dve.bn_aggr(blk(mv[j % 2], i, 2), blk(stats, i, 6)).then_inc(norm_step, 1)
                    dve.wait_ge(norm_step, base + 2 + 2 * B)
                    when(dve, rstd_ready, g - 1)
                    dve.tensor_scalar(var[j % 2][:, :],
                                      mv[j % 2][:, :].rearrange("p (i c) -> p i c", c=2)[:, :, 1], EPS, None,
                                      ALU.add).then_inc(norm_step, 1)

                def norm(u, j):
                    g = 4 * u + j
                    dve.wait_ge(rstd_ready, g + 1)
                    when(dve, stored[(j + 2) % 4], 16 * (u + j // 2))
                    for i in range(B):
                        dve.tensor_scalar(blk(x4[j % 2], i), blk(r4[j % 2], i), mv[j % 2][:, 2 * i:2 * i + 1],
                                          rstd[j % 2][:, i:i + 1], ALU.subtract, ALU.mult).then_inc(x4_ready, 1)

                def step(u, j, alive):
                    if alive(0):
                        add(u, j)
                    if alive(1):
                        norm(*earlier(u, j, 1, 4))
                steps(dve, step)


def two_layers(nc, sh, x, xT, wqkv, wproj, bproj, gate_w, gate_b, expert_w, expert_b, wqT, wkT, bq, wv1, bv1,
               wp, bp, cT, wg, bg, w1, b1, w2, b2, out):
    with ExitStack() as ctx:
        def sb(name, shape):
            return ctx.enter_context(nc.sbuf_tensor(name, shape, F32))
        x_all = sb("x_all", [P, sh.tokens])
        ident = sb("ident", [P, P])
        ones = sb("ones", [1, P])
        squares_all, dist_all = sb("squares_all", [P, 2 * sh.tiles]), sb("dist_all", [P, 2 * sh.tiles])
        tile_expert = ctx.enter_context(nc.sbuf_tensor("tile_expert", [1, sh.listed_tiles], I32))
        tile_row = ctx.enter_context(nc.sbuf_tensor("tile_row", [1, sh.listed_tiles], I32))
        with ExitStack() as two_stages:
            xT_all = two_stages.enter_context(nc.sbuf_tensor("xT_all", [P, sh.tokens], F32))
            v_all = two_stages.enter_context(nc.sbuf_tensor("v_all", [P, sh.tiles * H * (DH + 1)], F32))
            layer0(nc, sh, x, xT, wqkv, wproj, bproj, gate_w, gate_b, expert_w, expert_b, wv1, bv1,
                   (x_all, xT_all, v_all, ident, ones))
            sa_all = ctx.enter_context(nc.sbuf_tensor("sa_all", [P, sh.tokens], F32, side="right"))
            attention1(nc, sh, wqT, wkT, bq, (xT_all, v_all, ident), sa_all)
        rows_dram = nc.dram_tensor("rows_dram", [E * sh.list_rows + E * P, ROW], F32).ap()
        results = nc.dram_tensor("results", [2 * sh.tokens, P], F32).ap()
        routing = (rows_dram, squares_all, tile_expert, tile_row)
        with ExitStack() as expert_stages:
            def sb2(name, shape):
                return expert_stages.enter_context(nc.sbuf_tensor(name, shape, F32))
            wg_sb, w1_sb = sb2("wg_sb", [P, E * sh.hidden]), sb2("w1_sb", [P, E * sh.hidden])
            w2_sb = sb2("w2_sb", [sh.chunk, E * sh.chunks * P])
            bg_sb, b1_sb = sb2("bg_sb", [P, E * sh.hidden]), sb2("b1_sb", [P, E * sh.hidden])
            b2_sb = sb2("b2_sb", [P, E * P])
            expert_loads = ((wg_sb, wg), (w1_sb, w1), (w2_sb, w2), (bg_sb, bg.partition_broadcast(P)),
                            (b1_sb, b1.partition_broadcast(P)), (b2_sb, b2.partition_broadcast(P)))
            route1(nc, sh, wp, bp, cT, (x_all, ident, ones), sa_all, routing, expert_loads)
            experts1(nc, sh, (wg_sb, w1_sb, w2_sb, bg_sb, b1_sb, b2_sb), ident, routing, dist_all, results)
        combine1(nc, sh, x_all, dist_all, results, out)


def laid_out(i):
    import numpy as np
    heads = i["L0_attn_Wqkv"].reshape(H, 3, DH, P)
    kqv = i["L1_attn_Wkqv"]
    hidden = i["L1_ffn_Wg"].shape[2]
    chunk = hidden // -(-hidden // P)
    x = i["L0_attn_x"].reshape(-1, P)
    made = {
        "x": x,
        "xT": x.T,
        "wqkv": np.concatenate([heads[:, 0].reshape(P, P), heads[:, 1].reshape(P, P),
                                heads[:, 2].reshape(P, P)], axis=0).T,
        "wproj": i["L0_attn_Wproj"].T,
        "bproj": i["L0_attn_bproj"].reshape(1, P),
        "gate_w": i["L0_ffn_gate_w"].T,
        "gate_b": i["L0_ffn_gate_b"].reshape(1, E),
        "expert_w": i["L0_ffn_expert_w"].transpose(1, 0, 2).reshape(P, E * P),
        "expert_b": i["L0_ffn_expert_b"],
        "wqT": kqv[:, :, P:2 * P].transpose(2, 0, 1).reshape(P, H * P),
        "wkT": kqv[:, :, 0:P].transpose(2, 0, 1).reshape(P, H * P),
        "bq": i["L1_attn_bkqv"][:, P:2 * P].T,
        "wv1": kqv[:, :, 2 * P:].transpose(1, 0, 2).reshape(P, P),
        "bv1": i["L1_attn_bkqv"][:, 2 * P:].reshape(1, P),
        "wp": i["L1_attn_Wp"],
        "bp": i["L1_attn_bp"].reshape(1, P),
        "cT": i["L1_ffn_centroid"].T,
        "wg": i["L1_ffn_Wg"].transpose(1, 0, 2).reshape(P, E * hidden),
        "bg": i["L1_ffn_bg"].reshape(1, -1),
        "w1": i["L1_ffn_W1"].transpose(1, 0, 2).reshape(P, E * hidden),
        "b1": i["L1_ffn_b1"].reshape(1, -1),
        "w2": i["L1_ffn_W2"].reshape(-1, chunk, P).transpose(1, 0, 2).reshape(chunk, -1),
        "b2": i["L1_ffn_b2"].reshape(1, -1),
    }
    return {name: np.ascontiguousarray(a) for name, a in made.items()}


def kernel(**inputs):
    import numpy as np
    import concourse.bacc as bacc
    from concourse import mybir as _mybir
    from concourse.bass_utils import run_bass_kernel_spmd

    inputs = {name: np.asarray(a) for name, a in inputs.items()}
    nc = bacc.Bacc("TRN2", target_bir_lowering=False, num_devices=1)
    batch, seq, _ = inputs["L0_attn_x"].shape
    sh = Shapes(batch * seq, seq, inputs["L1_ffn_Wg"].shape[2])
    arrays, args = {}, []
    for name, a in laid_out(inputs).items():
        arrays[f"in_{name}"] = a
        args.append(nc.dram_tensor(f"in_{name}", a.shape, _mybir.dt.from_np(a.dtype), kind="ExternalInput").ap())
    out = nc.dram_tensor("out_x", (batch * seq, P), _mybir.dt.float32, kind="ExternalOutput").ap()
    two_layers(nc, sh, *args, out)
    r = run_bass_kernel_spmd(nc, [arrays], core_ids=[0])
    return r.results[0]["out_x"].reshape(batch, seq, P)
```
